# Optimizing a Trainium2 kernel written in Bass

```python
import numpy as np
import jax
import jax.numpy as jnp

def _softmax(x, axis=-1):
    return jax.nn.softmax(x, axis=axis)

def _gelu(x):
    return jax.nn.gelu(x, approximate=True)

def _silu(x):
    return jax.nn.silu(x)

def _sigmoid(x):
    return jax.nn.sigmoid(x)

def _layernorm(x, axis=-1, eps=1e-05):
    m = jnp.mean(x, axis=axis, keepdims=True)
    v = jnp.var(x, axis=axis, keepdims=True)
    return (x - m) / jnp.sqrt(v + eps)

def _scatter_add(tgt, idx, src, axis=0):
    return tgt.at[idx].add(src)

def _segment_sum(src, seg, n):
    return jax.ops.segment_sum(src, seg, n)
kernel_name = 'mk_flamingo_gated_d2_seqx_r4_b286a4'

def setup_inputs(seed: int=0):
    np.random.seed(seed)
    _w = jnp.asarray

    def _rec_inputs():
        import jax
        import jax.numpy as jnp
        _rk = jax.random.key(seed)
        x = -0.0005207 + 1.001 * jax.random.normal(jax.random.fold_in(_rk, 1), (4, 1024, 256), jnp.float32)
        _lenS = 1024 - jax.random.randint(jax.random.fold_in(_rk, 7), (4,), 0, max(1, 1024 // 4) + 1, jnp.int32)
        _lenS2 = 77 - jax.random.randint(jax.random.fold_in(_rk, 8), (4,), 0, max(1, 77 // 4) + 1, jnp.int32)
        _ctx_1024P = jax.random.normal(jax.random.fold_in(_rk, 12), (4, 16, 256), jnp.float32)
        _ctx_1024c = jax.random.dirichlet(jax.random.fold_in(_rk, 512), 0.3 * jnp.ones((16,), jnp.float32), (4, 77))
        _ctx_1024t = jnp.einsum('bsk,bkd->bsd', _ctx_1024c, _ctx_1024P)
        _ctx_1024t = _ctx_1024t * jax.lax.rsqrt(jnp.mean(jnp.square(_ctx_1024t)) + 1e-12) * 0.953939
        ctx_1024 = 0.00191187 + 0.999416 * (_ctx_1024t + 0.3 * jax.random.normal(jax.random.fold_in(_rk, 612), (4, 77, 256), jnp.float32))
        _validS = jnp.arange(1024)[None, :] < _lenS[:, None]
        _validS2 = jnp.arange(77)[None, :] < _lenS2[:, None]
        _causal = jnp.tril(jnp.ones((1024, 1024), dtype=bool))
        mask_BxS_ff1 = jnp.where(jnp.ones((4, 1024), dtype=bool), 1.0, 0.0).astype(jnp.float32)
        mask_BxS2_ik0 = jnp.where(jnp.broadcast_to(_validS2[:, :], (4, 77)), 0, 1).astype(jnp.int32)
        _g = jax.random.normal(jax.random.fold_in(_rk, 9001), (2, 2), jnp.float32)
        _g = jnp.sign(_g) * jnp.maximum(jnp.abs(_g), 1.0) + (_g == 0) * 1.0
        g_xattn = _g[0]
        g_ffn = _g[1]
        return (x, ctx_1024, mask_BxS_ff1, mask_BxS2_ik0, g_xattn, g_ffn)
    x, ctx_1024, mask_BxS_ff1, mask_BxS2_ik0, g_xattn, g_ffn = _rec_inputs()

    def _L0_xattn_setup():
        import jax, jax.numpy as jnp
        import numpy as np
        B, F, T, D = (8, 64, 32, 256)
        NEG = -1e+30
        key = jax.random.key(seed)
        ks = jax.random.split(key, 10)
        s = 1.0 / np.sqrt(D)
        return {'features': jax.random.normal(ks[0], (B, F, D), jnp.float32), 'masks': jnp.ones((B, F), jnp.float32), 'textual_features': jax.random.normal(ks[1], (B, T, D), jnp.float32), 'q_masks': jax.random.randint(ks[2], (B, T), 0, 2, jnp.int32), 'Ws': jax.random.normal(ks[3], (D, D), jnp.float32) * s, 'W': jax.random.normal(ks[4], (D, D), jnp.float32) * s, 'w': jax.random.normal(ks[5], (D, 1), jnp.float32) * s, 'b': jax.random.normal(ks[6], (1, D), jnp.float32) * s, 'Wcw': jax.random.normal(ks[7], (1, D), jnp.float32) * s, 'bcw': jnp.zeros((1,), jnp.float32), 'Wcb': jax.random.normal(ks[8], (1, D), jnp.float32) * s, 'bcb': jnp.zeros((1,), jnp.float32)}
    _L0_xattn_all = _L0_xattn_setup()
    _L0_xattn_in = {k: v for k, v in _L0_xattn_all.items() if k in ('Ws', 'W', 'w', 'b', 'Wcw', 'bcw', 'Wcb', 'bcb')}
    del _L0_xattn_all

    def _L0_ffn_setup():
        import jax, jax.numpy as jnp
        import numpy as np
        ALPHA = 1.0
        key = jax.random.key(seed)
        ks = jax.random.split(key, 7)
        B, S, IN, OUT = (8, 2048, 256, 256)
        RANK, DDIM, UDIM = (4, 100, 50)
        return {'hidden_states': jax.random.normal(ks[0], (B, S, IN), dtype=jnp.float32), 'W': jax.random.normal(ks[1], (OUT, IN), dtype=jnp.float32) * 0.02, 'b': jax.random.normal(ks[2], (OUT,), dtype=jnp.float32) * 0.02, 'lora_down': jax.random.normal(ks[3], (RANK, DDIM), dtype=jnp.float32) * 0.1, 'lora_up': jax.random.normal(ks[4], (UDIM, RANK), dtype=jnp.float32) * 0.1, 'down_aux': jax.random.normal(ks[5], (DDIM, IN), dtype=jnp.float32) * 0.03, 'up_aux': jax.random.normal(ks[6], (OUT, UDIM), dtype=jnp.float32) * 0.03}
    _L0_ffn_all = _L0_ffn_setup()
    _L0_ffn_in = {k: v for k, v in _L0_ffn_all.items() if k in ('W', 'b', 'lora_down', 'lora_up', 'down_aux', 'up_aux')}
    del _L0_ffn_all

    def _L1_xattn_setup():
        import jax, jax.numpy as jnp
        import numpy as np
        D_MODEL = 256
        N_HEADS = 16
        D_HEAD = D_MODEL // N_HEADS

        def _split_heads(x):
            B, S, _ = x.shape
            return x.reshape(B, S, N_HEADS, D_HEAD).transpose(0, 2, 1, 3)
        key = jax.random.key(seed)
        ks = jax.random.split(key, 11)
        B, S = (2, 512)
        scale = 1.0 / np.sqrt(D_MODEL)
        inp = {'query': jax.random.normal(ks[0], (B, S, D_MODEL), jnp.float32), 'key': jax.random.normal(ks[1], (B, S, D_MODEL), jnp.float32), 'value': jax.random.normal(ks[2], (B, S, D_MODEL), jnp.float32), 'Wq': jax.random.normal(ks[3], (D_MODEL, D_MODEL), jnp.float32) * scale, 'bq': jnp.zeros((D_MODEL,), jnp.float32), 'Wk': jax.random.normal(ks[4], (D_MODEL, D_MODEL), jnp.float32) * scale, 'bk': jnp.zeros((D_MODEL,), jnp.float32), 'Wv': jax.random.normal(ks[5], (D_MODEL, D_MODEL), jnp.float32) * scale, 'bv': jnp.zeros((D_MODEL,), jnp.float32), 'Wo': jax.random.normal(ks[6], (D_MODEL, D_MODEL), jnp.float32) * scale, 'bo': jnp.zeros((D_MODEL,), jnp.float32)}
        return inp
    _L1_xattn_all = _L1_xattn_setup()
    _L1_xattn_in = {k: v for k, v in _L1_xattn_all.items() if k in ('Wq', 'bq', 'Wk', 'bk', 'Wv', 'bv', 'Wo', 'bo')}
    del _L1_xattn_all

    def _L1_ffn_setup():
        import jax, jax.numpy as jnp
        import numpy as np
        B, S, D = (1, 512, 256)
        E, F = (16, 256)
        NG, TKG, K = (4, 2, 4)
        NSH = 2
        SCALE = 2.5
        STD = 0.02
        EPG = E // NG

        def _route(x_flat, router_w, bias):
            logits = x_flat.astype(jnp.float32) @ router_w.T
            scores = jax.nn.sigmoid(logits)
            s = scores + bias[None, :]
            sg = s.reshape(-1, NG, EPG)
            group_score = jax.lax.top_k(sg, 2)[0].sum(-1)
            gidx = jax.lax.top_k(group_score, TKG)[1]
            gmask = jnp.sum(jax.nn.one_hot(gidx, NG, dtype=jnp.float32), axis=1) > 0
            emask = jnp.repeat(gmask, EPG, axis=1)
            masked = jnp.where(emask, s, -1.0)
            topk_idx = jax.lax.top_k(masked, K)[1]
            tw = jnp.take_along_axis(scores, topk_idx, axis=1)
            tw = tw / (tw.sum(-1, keepdims=True) + 1e-20)
            tw = tw * SCALE
            return (topk_idx, tw)
        key = jax.random.key(seed)
        ks = jax.random.split(key, 8)
        return {'hidden_states': jax.random.normal(ks[0], (B, S, D), jnp.float32), 'router_w': jax.random.normal(ks[1], (E, D), jnp.float32) * STD, 'bias': jnp.zeros((E,), jnp.float32), 'gate_w': jax.random.normal(ks[2], (E, D, F), jnp.float32) * STD, 'up_w': jax.random.normal(ks[3], (E, D, F), jnp.float32) * STD, 'down_w': jax.random.normal(ks[4], (E, F, D), jnp.float32) * STD, 'sh_gate_w': jax.random.normal(ks[5], (D, NSH * F), jnp.float32) * STD, 'sh_up_w': jax.random.normal(ks[6], (D, NSH * F), jnp.float32) * STD, 'sh_down_w': jax.random.normal(ks[7], (NSH * F, D), jnp.float32) * STD}
    _L1_ffn_all = _L1_ffn_setup()
    _L1_ffn_in = {k: v for k, v in _L1_ffn_all.items() if k in ('router_w', 'bias', 'gate_w', 'up_w', 'down_w', 'sh_gate_w', 'sh_up_w', 'sh_down_w')}
    del _L1_ffn_all
    return {'x': x, 'ctx_1024': ctx_1024, 'mask_BxS_ff1': mask_BxS_ff1, 'mask_BxS2_ik0': mask_BxS2_ik0, 'g_xattn': g_xattn, 'g_ffn': g_ffn, 'L0_xattn_Ws': _L0_xattn_in['Ws'], 'L0_xattn_W': _L0_xattn_in['W'], 'L0_xattn_w': _L0_xattn_in['w'], 'L0_xattn_b': _L0_xattn_in['b'], 'L0_xattn_Wcw': _L0_xattn_in['Wcw'], 'L0_xattn_bcw': _L0_xattn_in['bcw'], 'L0_xattn_Wcb': _L0_xattn_in['Wcb'], 'L0_xattn_bcb': _L0_xattn_in['bcb'], 'L0_ffn_W': _L0_ffn_in['W'], 'L0_ffn_b': _L0_ffn_in['b'], 'L0_ffn_lora_down': _L0_ffn_in['lora_down'], 'L0_ffn_lora_up': _L0_ffn_in['lora_up'], 'L0_ffn_down_aux': _L0_ffn_in['down_aux'], 'L0_ffn_up_aux': _L0_ffn_in['up_aux'], 'L1_xattn_Wq': _L1_xattn_in['Wq'], 'L1_xattn_bq': _L1_xattn_in['bq'], 'L1_xattn_Wk': _L1_xattn_in['Wk'], 'L1_xattn_bk': _L1_xattn_in['bk'], 'L1_xattn_Wv': _L1_xattn_in['Wv'], 'L1_xattn_bv': _L1_xattn_in['bv'], 'L1_xattn_Wo': _L1_xattn_in['Wo'], 'L1_xattn_bo': _L1_xattn_in['bo'], 'L1_ffn_router_w': _L1_ffn_in['router_w'], 'L1_ffn_bias': _L1_ffn_in['bias'], 'L1_ffn_gate_w': _L1_ffn_in['gate_w'], 'L1_ffn_up_w': _L1_ffn_in['up_w'], 'L1_ffn_down_w': _L1_ffn_in['down_w'], 'L1_ffn_sh_gate_w': _L1_ffn_in['sh_gate_w'], 'L1_ffn_sh_up_w': _L1_ffn_in['sh_up_w'], 'L1_ffn_sh_down_w': _L1_ffn_in['sh_down_w']}

def reference(x, ctx_1024, mask_BxS_ff1, mask_BxS2_ik0, g_xattn, g_ffn, L0_xattn_Ws, L0_xattn_W, L0_xattn_w, L0_xattn_b, L0_xattn_Wcw, L0_xattn_bcw, L0_xattn_Wcb, L0_xattn_bcb, L0_ffn_W, L0_ffn_b, L0_ffn_lora_down, L0_ffn_lora_up, L0_ffn_down_aux, L0_ffn_up_aux, L1_xattn_Wq, L1_xattn_bq, L1_xattn_Wk, L1_xattn_bk, L1_xattn_Wv, L1_xattn_bv, L1_xattn_Wo, L1_xattn_bo, L1_ffn_router_w, L1_ffn_bias, L1_ffn_gate_w, L1_ffn_up_w, L1_ffn_down_w, L1_ffn_sh_gate_w, L1_ffn_sh_up_w, L1_ffn_sh_down_w):
    import jax
    import jax.numpy as jnp

    def _L0_xattn_ref(features, masks, textual_features, q_masks, Ws, W, w, b, Wcw, bcw, Wcb, bcb):
        import jax, jax.numpy as jnp
        import numpy as np
        B, F, T, D = (8, 64, 32, 256)
        NEG = -1e+30
        txt_proj = jnp.einsum('btd,de->bte', textual_features, Ws)
        feat_proj = jnp.einsum('bfd,de->bfe', features, W)
        h = jnp.tanh(txt_proj[:, None, :, :] + feat_proj[:, :, None, :] + b[None, None, :, :][..., 0, :])
        rho = jnp.einsum('bftd,d->bft', h, w[:, 0])
        qm = q_masks.astype(jnp.float32)
        rho = rho + (1.0 - qm)[:, None, :] * NEG
        att = jax.nn.softmax(rho, axis=-1)
        txt_h = jnp.einsum('bft,btd->bfd', att, textual_features)
        w_s = jnp.tanh(jnp.einsum('bfd,od->bfo', txt_h, Wcw) + bcw)
        b_s = jnp.tanh(jnp.einsum('bfd,od->bfo', txt_h, Wcb) + bcb)
        return w_s * features + b_s

    def _L0_ffn_ref(hidden_states, W, b, lora_down, lora_up, down_aux, up_aux):
        import jax, jax.numpy as jnp
        import numpy as np
        ALPHA = 1.0
        lilora_weight = up_aux @ (lora_up @ (lora_down @ down_aux))
        base = jnp.einsum('bsi,oi->bso', hidden_states, W) + b
        delta = jnp.einsum('bsi,oi->bso', hidden_states, lilora_weight)
        return base + ALPHA * delta

    def _L1_xattn_ref(query, key, value, Wq, bq, Wk, bk, Wv, bv, Wo, bo):
        import jax, jax.numpy as jnp
        import numpy as np
        D_MODEL = 256
        N_HEADS = 16
        D_HEAD = D_MODEL // N_HEADS

        def _split_heads(x):
            B, S, _ = x.shape
            return x.reshape(B, S, N_HEADS, D_HEAD).transpose(0, 2, 1, 3)
        q = _split_heads(query @ Wq + bq)
        k = _split_heads(key @ Wk + bk)
        v = _split_heads(value @ Wv + bv)
        scores = jnp.einsum('bhqd,bhkd->bhqk', q, k) / np.sqrt(D_HEAD)
        attn = jax.nn.softmax(scores, axis=-1)
        out = jnp.einsum('bhqk,bhkd->bhqd', attn, v)
        B, H, S, Dh = out.shape
        out = out.transpose(0, 2, 1, 3).reshape(B, S, H * Dh)
        return out @ Wo + bo

    def _L1_ffn_ref(hidden_states, router_w, bias, gate_w, up_w, down_w, sh_gate_w, sh_up_w, sh_down_w):
        import jax, jax.numpy as jnp
        import numpy as np
        B, S, D = (1, 512, 256)
        E, F = (16, 256)
        NG, TKG, K = (4, 2, 4)
        NSH = 2
        SCALE = 2.5
        STD = 0.02
        EPG = E // NG

        def _route(x_flat, router_w, bias):
            logits = x_flat.astype(jnp.float32) @ router_w.T
            scores = jax.nn.sigmoid(logits)
            s = scores + bias[None, :]
            sg = s.reshape(-1, NG, EPG)
            group_score = jax.lax.top_k(sg, 2)[0].sum(-1)
            gidx = jax.lax.top_k(group_score, TKG)[1]
            gmask = jnp.sum(jax.nn.one_hot(gidx, NG, dtype=jnp.float32), axis=1) > 0
            emask = jnp.repeat(gmask, EPG, axis=1)
            masked = jnp.where(emask, s, -1.0)
            topk_idx = jax.lax.top_k(masked, K)[1]
            tw = jnp.take_along_axis(scores, topk_idx, axis=1)
            tw = tw / (tw.sum(-1, keepdims=True) + 1e-20)
            tw = tw * SCALE
            return (topk_idx, tw)
        x = hidden_states.reshape(-1, D)
        topk_idx, tw = _route(x, router_w, bias)
        combine = (jax.nn.one_hot(topk_idx, E, dtype=tw.dtype) * tw[..., None]).sum(1)
        h = jnp.einsum('td,edf->etf', x, gate_w)
        u = jnp.einsum('td,edf->etf', x, up_w)
        y = jnp.einsum('etf,efd->etd', jax.nn.silu(h) * u, down_w)
        routed = jnp.einsum('etd,te->td', y, combine)
        sh = jax.nn.silu(x @ sh_gate_w) * (x @ sh_up_w) @ sh_down_w
        return (routed + sh).reshape(hidden_states.shape)
    x = x + jnp.tanh(g_xattn[0]) * _L0_xattn_ref(_layernorm(x, axis=-1), mask_BxS_ff1, ctx_1024, mask_BxS2_ik0, L0_xattn_Ws, L0_xattn_W, L0_xattn_w, L0_xattn_b, L0_xattn_Wcw, L0_xattn_bcw, L0_xattn_Wcb, L0_xattn_bcb)
    x = x + jnp.tanh(g_ffn[0]) * _L0_ffn_ref(_layernorm(x, axis=-1), L0_ffn_W, L0_ffn_b, L0_ffn_lora_down, L0_ffn_lora_up, L0_ffn_down_aux, L0_ffn_up_aux)
    x = x + jnp.tanh(g_xattn[1]) * _L1_xattn_ref(_layernorm(x, axis=-1), ctx_1024, ctx_1024, L1_xattn_Wq, L1_xattn_bq, L1_xattn_Wk, L1_xattn_bk, L1_xattn_Wv, L1_xattn_bv, L1_xattn_Wo, L1_xattn_bo)
    x = x + jnp.tanh(g_ffn[1]) * _L1_ffn_ref(_layernorm(x, axis=-1), L1_ffn_router_w, L1_ffn_bias, L1_ffn_gate_w, L1_ffn_up_w, L1_ffn_down_w, L1_ffn_sh_gate_w, L1_ffn_sh_up_w, L1_ffn_sh_down_w)
    return x

_drawn_inputs = setup_inputs


def setup_inputs(seed=0):
    import zlib

    import numpy as np

    out = dict(_drawn_inputs(seed))
    spreads = {'g_ffn': (-1.0, 0.6),
     'L1_xattn_bq': (0.0, 1.808),
     'L1_xattn_bk': (0.0, 2.0),
     'L1_xattn_bv': (0.0, 0.409),
     'L1_xattn_bo': (0.0, 0.506),
     'L1_ffn_bias': (0.0, 0.641)}
    factors = {'L0_xattn_b': 59.013,
     'L0_ffn_b': 18.106,
     'L0_ffn_lora_down': 4.824,
     'L0_ffn_lora_up': 5.383,
     'L0_ffn_down_aux': 4.985,
     'L0_ffn_up_aux': 4.974,
     'L1_ffn_router_w': 5.743,
     'L1_ffn_gate_w': 4.358,
     'L1_ffn_up_w': 4.312,
     'L1_ffn_down_w': 4.302,
     'L1_ffn_sh_gate_w': 3.865,
     'L1_ffn_sh_up_w': 3.771,
     'L1_ffn_sh_down_w': 3.797,
     'L0_xattn_Ws': 4.322,
     'L0_xattn_W': 5.348,
     'L0_xattn_w': 4.884}
    for name, (base, spread) in spreads.items():
        noise = np.random.default_rng([zlib.crc32(name.encode()), seed]).standard_normal(out[name].shape)
        drawn = base * np.exp(spread * noise) if base else spread * noise
        out[name] = jnp.asarray(drawn.astype(out[name].dtype))
    for name, factor in factors.items():
        out[name] = (out[name] * factor).astype(out[name].dtype)
    return out
```

```python
from contextlib import ExitStack

import numpy as np
import concourse.bass as bass
from concourse import mybir

F32 = mybir.dt.float32
F16 = mybir.dt.float16
I32 = mybir.dt.int32
ALU = mybir.AluOpType
ACT = mybir.ActivationFunctionType
AX = mybir.AxisListType.X

P = 128
D = 256
KC = D // P
B, S, TXT = 4, 1024, 77
TOK = 512
NT = TOK // P
STEPS = B * S // TOK
HALVES = S // TOK
HEADS, DH = 16, 16
HC = P // DH
PAIRS = HC * TXT
PH = PAIRS // 2
PCH = -(-PAIRS // P)
ROWS = [min(P, PAIRS - P * k) for k in range(PCH)]
GRP = -(-TXT // 4)
SL = 4 * GRP
E, NG, EPG, TOPG, TOPK = 16, 4, 4, 2, 4
EX = E + 2
NEG = -1e30
SCALE = 2.5
EPS = 1e-5
HRING = 12

SLOTS = 3 * EX
KV, LN1, FEAT, TANH0, TAIL = 0, 3, 5, 6, 30
SOFT, LN2, LIN, LN3T, QPROJ, PEAK, PEAKT, SCORES, PV, WO, LN4T, ROUTE = (
    TAIL + n for n in (1, 4, 5, 7, 8, 9, 11, 12, 16, 19, 21, 22))


def tanh_slot(g):
    return TANH0 + g * (TAIL - TANH0 - 2) // (GRP - 1)


class Step:

    def __init__(self, const, r=None):
        self.const, self.r, self.half = const, r, const % HALVES

    def at(self, per, k):
        return self.const * per + k if self.r is None else self.r * (2 * per) + (self.const * per + k)

    def batch_at(self, per, k):
        return self.batch() * per + k if self.r is None else self.r * per + (self.const // 2 * per + k)

    def batch(self):
        return self.const // 2 if self.r is None else self.r + self.const // 2

    def index(self):
        return self.const if self.r is None else self.r * 2 + self.const


class Chain:

    def __init__(self, eng, sem):
        self.eng, self.sem, self.n, self.per, self.at = eng, sem, 0, None, None

    def begin(self, at):
        self.at, self.n = at, 0

    def end(self):
        assert self.per in (None, self.n)
        self.per = self.n

    def link(self, ins):
        ins.then_inc(self.sem, 1)
        self.n += 1
        self.eng.wait_ge(self.sem, self.at(self.per or 0, self.n))


def build(nc, a, out):
    ctx = ExitStack()
    with ctx:
        ctx.enter_context(nc.allow_non_contiguous_dma(reason="small vectors and matrices, once"))

        def sb(name, shape, dt=F32):
            return ctx.enter_context(nc.sbuf_tensor(name, shape, dt))

        def sem(name):
            return ctx.enter_context(nc.semaphore(name))

        gate_hi, gate_lo, up_hi, up_lo = (sb(n, [P, EX, KC, D], F16) for n in
                                          ("gate_hi", "gate_lo", "up_hi", "up_lo"))
        down_dram = nc.dram_tensor("down_split", [EX, P, 2 * KC * D], F16, kind="Internal").ap()
        down = sb("down", [P, 3, 2, KC, D], F16)
        W0h, W0l, W1h, W1l, Wqh, Wql, Wkh, Wkl, Wvh, Wvl, Woh, Wol = (
            sb(n, [P, KC, D], F16) for n in ("W0h", "W0l", "W1h", "W1l", "Wqh", "Wql",
                                             "Wkh", "Wkl", "Wvh", "Wvl", "Woh", "Wol"))
        RWh, RWl = sb("RWh", [P, KC, E], F16), sb("RWl", [P, KC, E], F16)
        ident = sb("ident", [P, P])
        head_mask = sb("head_mask", [P, HC, TXT], F16)
        pair_mask = sb("pair_mask", [P, PCH, HC, DH], F16)
        head_sel = sb("head_sel", [P, KC, HC, TXT], F16)
        lower = sb("lower", [P, E, E], F16)
        text_bias = sb("text_bias", [P, KC, B * TXT])
        text_now = sb("text_now", [P, KC, TXT])
        wcol = sb("wcol", [P, KC])
        wslide = sb("wslide", [P, KC, 63])
        coef_w, coef_b = sb("coef_w", [P, B, SL]), sb("coef_b", [P, B, SL])
        text_mask = sb("text_mask", [P, B, SL])
        ctxT_hi, ctxT_lo = sb("ctxT_hi", [P, KC, B * TXT], F16), sb("ctxT_lo", [P, KC, B * TXT], F16)
        gains = sb("gains", [P, 4])
        bcol = sb("bcol", [P, KC])
        bq, bk = sb("bq", [P, KC]), sb("bk", [P, KC])
        wc_cols = sb("wc_cols", [P, 2, KC])
        bc_row = sb("bc_row", [P, 2])
        b1_row, bo_row, bv_row = sb("b1_row", [P, D]), sb("bo_row", [P, D]), sb("bv_row", [P, D])
        rbias = sb("rbias", [P, E])
        x = sb("x", [P, 2, NT, D])
        xn = sb("xn", [P, NT, D])
        xT_hi, xT_lo = sb("xT_hi", [P, KC, TOK], F16), sb("xT_lo", [P, KC, TOK], F16)
        eT_hi, eT_lo = sb("eT_hi", [P, 2, KC, TOK], F16), sb("eT_lo", [P, 2, KC, TOK], F16)
        stats, mv = sb("stats", [P, NT, 6]), sb("mv", [P, 2, NT])
        veps, rstd, nwt = sb("veps", [P, NT]), sb("rstd", [P, NT]), sb("nwt", [P, NT])
        K_hi, K_lo = sb("K_hi", [P, KC, PAIRS], F16), sb("K_lo", [P, KC, PAIRS], F16)
        V_hi, V_lo = sb("V_hi", [P, PCH, KC, P], F16), sb("V_lo", [P, PCH, KC, P], F16)
        qT_hi, qT_lo = sb("qT_hi", [P, KC, TOK], F16), sb("qT_lo", [P, KC, TOK], F16)
        peak = sb("peak", [P, NT, 32])
        peakT = sb("peakT", [P, TOK], F16)
        smax, sden, snum = sb("smax", [P, NT]), sb("sden", [P, NT]), sb("snum", [P, 2, NT])
        film = sb("film", [P, 2, NT])
        combine = sb("combine", [P, 2, NT, EX])
        tile3 = sb("tile3", [P, 3, TOK])
        hid_hi, hid_lo = sb("hid_hi", [P, 4, TOK], F16), sb("hid_lo", [P, 4, TOK], F16)
        region = sb("region", [P, HRING * TOK])
        tanh_tiles = region[:, :].rearrange("p (n t) -> p n t", n=HRING)
        Ws = region[:, 0:512].rearrange("p (k d) -> p k d", k=KC)
        ctx_rows = region[:, 512:1536].rearrange("p (b d) -> p b d", b=B)
        ctxT = region[:, 1536:1536 + KC * B * TXT].rearrange("p (k t) -> p k t", k=KC)
        o0 = 1536 + KC * B * TXT
        mask_int = region[:, o0:o0 + B * TXT].bitcast(I32).rearrange("p (b t) -> p b t", b=B)
        o0 += B * TXT
        up_rows = region[:, o0:o0 + 100].rearrange("p (c u) -> p c u", c=2)
        lora_dT = region[:, o0 + 100:o0 + 104]
        lora_uT = region[:, o0 + 104:o0 + 154]
        down_aux = region[:, o0 + 154:o0 + 410]
        lora1 = region[:, o0 + 410:o0 + 666]
        lora2 = region[:, o0 + 666:o0 + 922]
        up_auxT = region[:, o0 + 922:o0 + 1178]
        rw_rows = region[:, o0 + 1178:o0 + 1434].rearrange("p (k d) -> p k d", k=KC)
        rwT = region[:, o0 + 1434:o0 + 1434 + KC * E].rearrange("p (k e) -> p k e", k=KC)
        ctx8_hi = region[:, 0:PAIRS].bitcast(F16).rearrange("p (k h t) -> p k h t", k=KC, h=HC)
        ctx8_lo = region[:, PAIRS:2 * PAIRS].bitcast(F16).rearrange("p (k h t) -> p k h t", k=KC, h=HC)
        kv32 = region[:, 2 * PAIRS:2 * PAIRS + 1024].rearrange("p (r n) -> p r n", r=2)
        rhoT = region[:, 0:TOK]
        sm = region[:, 512:512 + 3 * NT * SL].rearrange("p (r t s) -> p r t s", r=3, t=NT)
        p_hi = region[:, 0:2560].bitcast(F16).rearrange("p (m t) -> p m t", m=2 * PCH)
        p_lo = region[:, 2560:5120].bitcast(F16).rearrange("p (m t) -> p m t", m=2 * PCH)
        p32 = region[:, 5120:6144].rearrange("p (r t) -> p r t", r=2)
        rank_a = region[:, 0:1024].rearrange("p (t e f) -> p t e f", t=NT, e=E)
        rank_b = region[:, 1024:2048].rearrange("p (t e f) -> p t e f", t=NT, e=E)
        rs = region[:, 2048:2048 + 16 * NT * E].rearrange("p (r t e) -> p r t e", r=16, t=NT)
        xn_t = xn[:, :, :].rearrange("p a b -> p (a b)").rearrange("p (c t) -> p c t", c=2)
        stage = [tile3[:, n, :] for n in range(3)]
        stage2 = down[:, :, :, :, :].rearrange("p r a b c -> p r (a b c)")
        small_stage = stage + [stage2[:, n, :].bitcast(F32) for n in range(3)]
        down_tmp = [(hid_hi, hid_lo, n) for n in range(4)]

        psF = ctx.enter_context(nc.psum_tensor("psF", [P, 3, 512], F32))
        psG = ctx.enter_context(nc.psum_tensor("psG", [P, 2, 512], F32))
        psU = ctx.enter_context(nc.psum_tensor("psU", [P, 2, 512], F32))
        psY = ctx.enter_context(nc.psum_tensor("psY", [P, 2, D], F32))
        RHO = 2

        consts = sem("consts")
        x_loaded = [sem("x_loaded0"), sem("x_loaded1")]
        stored = [sem("stored0"), sem("stored1")]
        text_loaded, wc_loaded, lora_loaded, rows_loaded = (
            sem(n) for n in ("text_loaded", "wc_loaded", "lora_loaded", "rows_loaded"))
        small_loaded = [sem(f"small_loaded{n}") for n in range(6)]
        stage_loaded = [sem(f"stage_loaded{n}") for n in range(3)]
        split_done = sem("split_done")
        down_stored = [sem(f"down_stored{n}") for n in range(4)]
        setup_pe, setup_dve, setup_act, setup_chain, pool_chain = (
            sem(n) for n in ("setup_pe", "setup_dve", "setup_act", "setup_chain", "pool_chain"))
        ctx8_ready, kv_ps, kv_used, kv_chain = (
            sem(n) for n in ("ctx8_ready", "kv_ps", "kv_used", "kv_chain"))
        xn_ready = sem("xn_ready")
        xT_ps = sem("xT_ps")
        hi_ready = sem("hi_ready")
        lo_ready = sem("lo_ready")
        feat_ps = sem("feat_ps")
        h_ready = sem("h_ready")
        rho_part = sem("rho_part")
        rhoT_ready, rho_ps = sem("rhoT_ready"), sem("rho_ps")
        sm_sub, sm_exp = sem("sm_sub"), sem("sm_exp")
        film_in, film_ready = sem("film_in"), sem("film_ready")
        lin_ps = sem("lin_ps")
        q_ps, q32_ready, q_hi, q_lo = (sem(n) for n in ("q_ps", "q32_ready", "q_hi", "q_lo"))
        peak_ps, peak_used = sem("peak_ps"), sem("peak_used")
        peakT_ps, peakT_ready = sem("peakT_ps"), sem("peakT_ready")
        sc_ps, p_ready, p_hi_ready, p_lo_ready = (
            sem(n) for n in ("sc_ps", "p_ready", "p_hi_ready", "p_lo_ready"))
        pv_ps, o_ready, o_hi, o_lo = (sem(n) for n in ("pv_ps", "o_ready", "o_hi", "o_lo"))
        wo_ps = sem("wo_ps")
        logit_ps, score_ready = sem("logit_ps"), sem("score_ready")
        routed = sem("routed")
        front_chain = sem("front_chain")
        gu_ps, tanh_done, v_done, g_done, ghi_done, glo_done = (
            sem(n) for n in ("gu_ps", "tanh_done", "v_done", "g_done", "ghi_done", "glo_done"))
        y_ps, y_used = sem("y_ps"), sem("y_used")
        down_loaded = [sem(f"down_loaded{n}") for n in range(3)]

        HID = 2 * EX
        xv = a["x"].rearrange("b (h t p) d -> (b h) p t d", h=HALVES, p=P)
        ov = out.rearrange("b (h t p) d -> (b h) p t d", h=HALVES, p=P)

        def w256(w):
            return w.rearrange("(k p) n -> p k n", p=P)

        def expert(e, what):
            if e < E:
                return w256(a[f"L1_ffn_{what}_w"][e])
            s = e - E
            if what == "down":
                return w256(a["L1_ffn_sh_down_w"][s * D:(s + 1) * D, :])
            return w256(a[f"L1_ffn_sh_{what}_w"][:, s * D:(s + 1) * D])

        staged = [(e, what) for e in range(EX) for what in ("gate", "up", "down")]

        def run(eng, slot, after=None):
            def both(st, ex):
                for i in range(SLOTS):
                    slot(i, st, ex)
                if after and ex:
                    after(ex)

            both(Step(0), None)
            both(Step(1), Step(0))
            with eng.Fori(0, B - 1) as r:
                both(Step(2, r), Step(1, r))
                both(Step(3, r), Step(2, r))
            both(None, Step(STEPS - 1))

        block = ctx.enter_context(nc.Block())

        @block.sync
        def _(sp):
            def load_x(st):
                sp.dma_start(x[:, st.half], xv[st.index()]).then_inc(x_loaded[st.half], 16)

            load_x(Step(0))
            sp.dma_start(ctx_rows[0:TXT], a["ctx_1024"].rearrange("b t d -> t b d")).then_inc(text_loaded, 16)
            sp.dma_start(Ws, w256(a["L0_xattn_Ws"])).then_inc(text_loaded, 16)
            sp.dma_start(wcol[:, :], a["L0_xattn_w"].rearrange("(k p) o -> p (k o)", p=P)).then_inc(text_loaded, 16)
            sp.dma_start(bcol[:, :], a["L0_xattn_b"].rearrange("o (k p) -> p (k o)", p=P)).then_inc(text_loaded, 16)
            smalls = ["L0_xattn_W", "L0_ffn_W", "L1_xattn_Wk", "L1_xattn_Wv", "L1_xattn_Wq", "L1_xattn_Wo"]
            for n, name in enumerate(smalls):
                dst = small_stage[n].rearrange("p (k d) -> p k d", k=KC)
                sp.dma_start(dst, w256(a[name])).then_inc(small_loaded[n], 16)
            for n, name in enumerate(("Wcw", "Wcb")):
                sp.dma_start(wc_cols[:, n, :], a[f"L0_xattn_{name}"].rearrange("o (k p) -> p (o k)", p=P)).then_inc(wc_loaded, 16)
            for n, name in enumerate(("bcw", "bcb")):
                sp.dma_start(bc_row[:, n:n + 1], a[f"L0_xattn_{name}"].partition_broadcast(P)).then_inc(wc_loaded, 16)
            sp.dma_start(mask_int, a["mask_BxS2_ik0"].partition_broadcast(P)).then_inc(wc_loaded, 16)
            sp.dma_start(up_rows, a["L0_ffn_up_aux"].rearrange("(c p) u -> p c u", p=P)).then_inc(lora_loaded, 16)
            sp.dma_start(lora_dT[0:100], a["L0_ffn_lora_down"].rearrange("r d -> d r")).then_inc(lora_loaded, 16)
            sp.dma_start(lora_uT[0:4], a["L0_ffn_lora_up"].rearrange("u r -> r u")).then_inc(lora_loaded, 16)
            sp.dma_start(down_aux[0:100], a["L0_ffn_down_aux"]).then_inc(lora_loaded, 16)
            sp.dma_start(rw_rows[0:E], a["L1_ffn_router_w"].rearrange("e (k p) -> e k p", k=KC)).then_inc(lora_loaded, 16)
            for n, name in enumerate(("g_xattn", "g_ffn")):
                sp.dma_start(gains[:, 2 * n:2 * n + 2], a[name].partition_broadcast(P)).then_inc(rows_loaded, 16)
            for dst, name in ((bq, "L1_xattn_bq"), (bk, "L1_xattn_bk")):
                sp.dma_start(dst[:, :], a[name].rearrange("(k p) -> p k", p=P)).then_inc(rows_loaded, 16)
            for dst, name in ((b1_row, "L0_ffn_b"), (bo_row, "L1_xattn_bo"), (bv_row, "L1_xattn_bv"), (rbias, "L1_ffn_bias")):
                sp.dma_start(dst[:, :], a[name].partition_broadcast(P)).then_inc(rows_loaded, 16)
            load_x(Step(1))

            sp.wait_ge(setup_dve, 5)
            for n in range(len(staged) + 3):
                if n >= 3:
                    sp.wait_ge(split_done, n - 2)
                    e, what = staged[n - 3]
                    if what == "down":
                        src = down_tmp[e % 4]
                        sp.dma_start(down_dram[e, :, 0:TOK], src[0][:, e % 4, :]).then_inc(down_stored[e % 4], 16)
                        sp.dma_start(down_dram[e, :, TOK:2 * TOK], src[1][:, e % 4, :]).then_inc(down_stored[e % 4], 16)
                if n < len(staged):
                    e, what = staged[n]
                    sp.dma_start(stage[n % 3].rearrange("p (k d) -> p k d", k=KC), expert(e, what)).then_inc(stage_loaded[n % 3], 16)
            for n in range(4):
                sp.wait_ge(down_stored[n], 32 * len(range(n, EX, 4)))

            def load_down(st, e):
                if e < 3:
                    if st.const > 0 or st.r is not None:
                        sp.wait_ge(y_ps, st.at(HID, 2 * (e - 3) + 2))
                else:
                    sp.wait_ge(y_ps, st.at(HID, 2 * (e - 3) + 2))
                sp.dma_start(down[:, e % 3].rearrange("p a b c -> p (a b c)"), down_dram[e]).then_inc(down_loaded[e % 3], 16)

            for e in range(3):
                load_down(Step(0), e)

            def rest(st, more_x=True, more=True):
                for e in range(3, EX):
                    load_down(st, e)
                nxt = Step(st.const + 1, st.r)
                if more:
                    for e in range(3):
                        load_down(nxt, e)
                sp.wait_ge(y_used, st.at(HID, HID))
                sp.dma_start(ov[st.index()], x[:, st.half]).then_inc(stored[st.half], 16)
                sp.wait_ge(stored[st.half], st.batch_at(16, 16))
                if more_x:
                    load_x(Step(st.const + 2, st.r))

            rest(Step(0))
            with sp.Fori(0, B - 2) as r:
                rest(Step(1, r))
                rest(Step(2, r))
            rest(Step(STEPS - 3))
            rest(Step(STEPS - 2), more_x=False)
            rest(Step(STEPS - 1), more_x=False, more=False)

        @block.gpsimd
        def _(pool):
            cn = Chain(pool, pool_chain)
            cn.begin(lambda per, k: k)
            cn.link(pool.memset(ident[:, :], 0.0))
            pool.affine_select(out=ident[:, :], in_=ident[:, :], compare_op=ALU.not_equal, fill=1.0,
                               base=0, pattern=[[-1, P]], channel_multiplier=1).then_inc(consts, 1)
            cn.link(pool.memset(wslide[:, :, :], 0.0))
            pool.wait_ge(text_loaded, 64)
            for k in range(KC):
                last = pool.tensor_tensor(wslide[:, k, 31:32], wslide[:, k, 31:32], wcol[:, k:k + 1], ALU.add)
            last.then_inc(consts, 1)
            cn.link(pool.memset(head_mask[:, :, :], 1.0))
            cn.link(pool.affine_select(out=head_mask[:, :, :], in_=head_mask[:, :, :], compare_op=ALU.is_ge, fill=0.0,
                                       base=0, pattern=[[-DH, HC], [0, TXT]], channel_multiplier=1))
            pool.affine_select(out=head_mask[:, :, :], in_=head_mask[:, :, :], compare_op=ALU.is_ge, fill=0.0,
                               base=DH - 1, pattern=[[DH, HC], [0, TXT]], channel_multiplier=-1).then_inc(consts, 1)
            cn.link(pool.memset(pair_mask[:, :, :, :], 1.0))
            cn.link(pool.affine_select(out=pair_mask[:, :, :, :], in_=pair_mask[:, :, :, :], compare_op=ALU.is_ge, fill=0.0,
                                       base=0, pattern=[[P, PCH], [-TXT, HC], [0, DH]], channel_multiplier=1))
            pool.affine_select(out=pair_mask[:, :, :, :], in_=pair_mask[:, :, :, :], compare_op=ALU.is_ge, fill=0.0,
                               base=TXT - 1, pattern=[[-P, PCH], [TXT, HC], [0, DH]], channel_multiplier=-1).then_inc(consts, 1)
            cn.link(pool.memset(head_sel[:, :, :, :], 0.0))
            pool.affine_select(out=head_sel[:, :, :, :], in_=head_sel[:, :, :, :], compare_op=ALU.not_equal, fill=1.0,
                               base=0, pattern=[[-HC, KC], [-1, HC], [0, TXT]], channel_multiplier=1).then_inc(consts, 1)
            cn.link(pool.memset(lower[:, :, :], 1.0))
            pool.affine_select(out=lower[:, :, :], in_=lower[:, :, :], compare_op=ALU.is_ge, fill=0.0,
                               base=-1, pattern=[[1, E], [-1, E]], channel_multiplier=0).then_inc(consts, 1)
            pool.memset(peak[:, :, :], 0.0).then_inc(consts, 1)
            pool.memset(peakT[:, :], 0.0).then_inc(consts, 1)

            def slot(i, st, ex):
                if ex and i % 3 > 0:
                    q = 2 * (i // 3) + i % 3 - 1
                    pool.wait_ge(ghi_done, ex.at(HID, q + 1))
                    if q >= 4 or ex.const or ex.r is not None:
                        pool.wait_ge(y_ps, ex.at(HID, 2 * (q // 2) - 2))
                    pool.tensor_tensor(hid_lo[:, q % 4], tile3[:, q % 3], hid_hi[:, q % 4], ALU.subtract).then_inc(glo_done, 1)
                if st is None:
                    return
                for n, m0 in enumerate(range(0, 2 * PCH, 3)):
                    if i == SCORES + n:
                        for m in range(m0, min(m0 + 3, 2 * PCH)):
                            rows = ROWS[m % PCH]
                            pool.wait_ge(p_hi_ready, st.at(2 * PCH, m + 1))
                            pool.tensor_tensor(p_lo[0:rows, m], p32[0:rows, m % 2], p_hi[0:rows, m], ALU.subtract).then_inc(p_lo_ready, 1)

            run(pool, slot)

        @block.tensor
        def _(pe):
            def product(out_, terms):
                for n, (lh, ll, rh, rl) in enumerate(terms):
                    pe.matmul(out_, lh, rh, start=n == 0, stop=False)
                    pe.matmul(out_, lh, rl, start=False, stop=False)
                    last = pe.matmul(out_, ll, rh, start=False, stop=n == len(terms) - 1)
                return last

            def turn(out_, in_, rows=P):
                return pe.transpose(out_, in_, ident[0:rows, 0:rows])

            pe.wait_ge(consts, 1)
            pe.wait_ge(text_loaded, 64)
            for b in range(B):
                for k in range(KC):
                    last = turn(psG[:, k, b * TXT:(b + 1) * TXT], ctx_rows[0:TXT, b, k * P:(k + 1) * P], TXT)
            last.then_inc(setup_pe, 1)
            pe.wait_ge(setup_dve, 1)
            for c in range(KC):
                for k in range(KC):
                    last = pe.matmul(psU[:, c, 0:B * TXT], Ws[:, k, c * P:(c + 1) * P], ctxT[:, k, :],
                                     start=k == 0, stop=k == KC - 1)
            last.then_inc(setup_pe, 1)
            pe.wait_ge(wc_loaded, 80)
            for n in range(2):
                for k in range(KC):
                    last = pe.matmul(psG[:, n, 0:B * TXT], wc_cols[:, n, k:k + 1].to_broadcast([P, P]), ctxT[:, k, :],
                                     start=k == 0, stop=k == KC - 1)
            last.then_inc(setup_pe, 1)
            pe.wait_ge(lora_loaded, 80)
            for c in range(2):
                pe.transpose(psY[0:50, 0, c * P:(c + 1) * P], up_rows[:, c, :], ident[:, :])
            for k in range(KC):
                turn(psY[:, 1, 128 + k * E:128 + (k + 1) * E], rw_rows[0:E, k, :], E)
            pe.matmul(psF[0:4, 2, 0:D], lora_dT[0:100, :], down_aux[0:100, :], start=True, stop=True).then_inc(setup_pe, 1)
            pe.wait_ge(setup_dve, 3)
            pe.matmul(psF[0:50, 2, 0:D], lora_uT[0:4, 0:50], lora1[0:4, :], start=True, stop=True).then_inc(setup_pe, 1)
            pe.wait_ge(setup_dve, 4)
            pe.wait_ge(small_loaded[1], 16)
            wnat = small_stage[1].rearrange("p (o d) -> p o d", o=2)
            for k in range(KC):
                pe.matmul(psU[:, k, 0:D], lora2[0:50, k * P:(k + 1) * P], up_auxT[0:50, :], start=True, stop=False)
                for o in range(2):
                    last = pe.matmul(psU[:, k, o * P:(o + 1) * P], wnat[:, o, k * P:(k + 1) * P], ident[:, :],
                                     start=False, stop=o == 1)
            last.then_inc(setup_pe, 1)

            def gate_up(ex, q):
                e, f = q // 2, q % 2
                if q == 0:
                    pe.wait_ge(lo_ready, ex.at(8, 8))
                if ex.const == 0 and f == 0:
                    pe.wait_ge(split_done, 3 * e + 2)
                if q >= 2 or ex.const:
                    pe.wait_ge(g_done, ex.at(HID, q - 1))
                for ps, wh, wl in ((psG, gate_hi, gate_lo), (psU, up_hi, up_lo)):
                    last = product(ps[:, f], [(wh[:, e, k, f * P:(f + 1) * P], wl[:, e, k, f * P:(f + 1) * P],
                                               eT_hi[:, ex.half, k], eT_lo[:, ex.half, k]) for k in range(KC)])
                last.then_inc(gu_ps, 1)

            def down_half(ex, e, hf):
                if hf == 0:
                    pe.wait_ge(glo_done, ex.at(HID, 2 * e + 2))
                    pe.wait_ge(down_loaded[e % 3], ex.at(6 * 16, 16 * (e // 3 + 1)))
                if 2 * e + hf or ex.const:
                    pe.wait_ge(y_used, ex.at(HID, 2 * e + hf))
                for t in (2 * hf, 2 * hf + 1):
                    last = product(psY[:, t % 2], [(hid_hi[:, (2 * e + f) % 4, t * P:(t + 1) * P],
                                                    hid_lo[:, (2 * e + f) % 4, t * P:(t + 1) * P],
                                                    down[:, e % 3, 0, f], down[:, e % 3, 1, f]) for f in range(2)])
                last.then_inc(y_ps, 1)

            def transpose_x(st, n):
                pe.wait_ge(xn_ready, st.at(4, n + 1))
                for c in range(KC):
                    for t in range(NT):
                        last = turn(psF[:, c, t * P:(t + 1) * P], xn[:, t, c * P:(c + 1) * P])
                    last.then_inc(xT_ps, 1)

            def rho_set(st, g, c):
                js = range(min(4, TXT - 4 * g))
                pe.wait_ge(h_ready, st.at(2 * TXT, 8 * g + (c + 1) * len(js)))
                for j in js:
                    n = 8 * g + c * len(js) + j
                    last = pe.matmul(psF[32 * j:32 * j + 32, RHO, :], wslide[:, c, 31 - g:63 - g], tanh_tiles[:, n % HRING],
                                     start=g == 0 and c == 0, stop=c == 1 and 4 * (g + 1) + j >= TXT)
                last.then_inc(rho_part, 1)

            def slot(i, st, ex):
                if ex:
                    e, k = i // 3, i % 3
                    if k == 1 and e:
                        down_half(ex, e - 1, 0)
                    if k < 2:
                        gate_up(ex, 2 * e + k)
                    if k == 2 and e:
                        down_half(ex, e - 1, 1)
                if st is None:
                    return
                if st.half == 0 and KV < i <= KV + 3:
                    if i == KV + 1:
                        pe.wait_ge(ctx8_ready, st.batch_at(1, 1))
                        if st.const:
                            pe.wait_ge(lo_ready, st.at(8, 0))
                            pe.wait_ge(score_ready, st.at(1, 0))
                    flat_hi = ctx8_hi.rearrange("p k h t -> p k (h t)")
                    flat_lo = ctx8_lo.rearrange("p k h t -> p k (h t)")
                    for n in range(3 * (i - KV - 1), 3 * (i - KV)):
                        if n >= 3:
                            pe.wait_ge(kv_used, st.batch_at(9, n - 2))
                        if n < 4:
                            c, hf = n // 2, n % 2
                            last = product(psF[:, n % 3, 0:PH], [(Wkh[:, k, c * P:(c + 1) * P], Wkl[:, k, c * P:(c + 1) * P],
                                                                  flat_hi[:, k, hf * PH:(hf + 1) * PH],
                                                                  flat_lo[:, k, hf * PH:(hf + 1) * PH]) for k in range(KC)])
                        else:
                            m = n - 4
                            rows = ROWS[m]
                            last = product(psF[0:rows, n % 3, 0:D], [(flat_hi[:, k, m * P:m * P + rows],
                                                                      flat_lo[:, k, m * P:m * P + rows],
                                                                      Wvh[:, k, :], Wvl[:, k, :]) for k in range(KC)])
                        last.then_inc(kv_ps, 1)
                if i == LN1 + 1:
                    if st.half == 0:
                        pe.wait_ge(kv_used, st.batch_at(9, 9))
                    else:
                        pe.wait_ge(lo_ready, st.at(8, 0))
                        pe.wait_ge(score_ready, st.at(1, 0))
                    transpose_x(st, 0)
                if i == FEAT:
                    pe.wait_ge(lo_ready, st.at(8, 2))
                    for c in range(KC):
                        last = product(psF[:, c], [(W0h[:, k, c * P:(c + 1) * P], W0l[:, k, c * P:(c + 1) * P],
                                                    xT_hi[:, k], xT_lo[:, k]) for k in range(KC)])
                    last.then_inc(feat_ps, 1)
                for g in range(GRP):
                    if i == tanh_slot(g) + 1:
                        if g == 0 and st.const == 0:
                            pe.wait_ge(consts, 2)
                        for c in range(KC):
                            rho_set(st, g, c)
                if i == SOFT:
                    pe.wait_ge(rhoT_ready, st.at(1, 1))
                    for t in range(NT):
                        last = turn(psF[:, 0, t * P:(t + 1) * P], rhoT[:, t * P:(t + 1) * P])
                    last.then_inc(rho_ps, 1)
                if i == LN2:
                    transpose_x(st, 1)
                if i == LIN:
                    pe.wait_ge(lo_ready, st.at(8, 4))
                    for t in range(NT):
                        last = product(psF[:, t // 2, t % 2 * D:t % 2 * D + D],
                                       [(xT_hi[:, k, t * P:(t + 1) * P], xT_lo[:, k, t * P:(t + 1) * P],
                                         W1h[:, k, :], W1l[:, k, :]) for k in range(KC)])
                        if t % 2:
                            last.then_inc(lin_ps, 1)
                if i == LN3T:
                    transpose_x(st, 2)
                if i == QPROJ:
                    pe.wait_ge(lo_ready, st.at(8, 6))
                    for c in range(KC):
                        product(psF[:, c], [(Wqh[:, k, c * P:(c + 1) * P], Wql[:, k, c * P:(c + 1) * P],
                                             xT_hi[:, k], xT_lo[:, k]) for k in range(KC)]).then_inc(q_ps, 1)
                if i in (PEAK, PEAK + 1):
                    if i == PEAK:
                        pe.wait_ge(q_lo, st.at(2, 2))
                    for n in range(8 * (i - PEAK), 8 * (i - PEAK + 1)):
                        t, c, hf = n // 4, n // 2 % 2, n % 2
                        if n >= 3:
                            pe.wait_ge(peak_used, st.at(16, n - 2))
                        pe.matmul(psF[:, n % 3, 0:PH], qT_hi[:, c, t * P:(t + 1) * P], K_hi[:, c, hf * PH:(hf + 1) * PH],
                                  start=True, stop=True).then_inc(peak_ps, 1)
                if i == PEAKT:
                    pe.wait_ge(peak_used, st.at(16, 16))
                    for t in range(NT):
                        last = pe.transpose(psF[0:32, 0, t * P:(t + 1) * P], peak[:, t, :], ident[:, :])
                    last.then_inc(peakT_ps, 1)
                if SCORES <= i < SCORES + 4:
                    if i == SCORES:
                        pe.wait_ge(peakT_ready, st.at(1, 1))
                    for m in range(3 * (i - SCORES), min(3 * (i - SCORES) + 3, 2 * PCH)):
                        c, k, rows = m // PCH, m % PCH, ROWS[m % PCH]
                        if m >= 3:
                            pe.wait_ge(p_ready, st.at(2 * PCH, m - 2))
                        dst = psF[0:rows, (2, 0, 1)[m % 3]]
                        cut = slice(k * P, k * P + rows)
                        pe.matmul(dst, K_hi[:, c, cut], qT_hi[:, c], start=True, stop=False)
                        pe.matmul(dst, K_hi[:, c, cut], qT_lo[:, c], start=False, stop=False)
                        pe.matmul(dst, K_lo[:, c, cut], qT_hi[:, c], start=False, stop=False)
                        pe.matmul(dst, head_sel[:, c].rearrange("p h t -> p (h t)")[:, cut], peakT[:, :],
                                  start=False, stop=True).then_inc(sc_ps, 1)
                if i in (PV, PV + 1):
                    c = i - PV
                    pe.wait_ge(p_lo_ready, st.at(2 * PCH, PCH * (c + 1)))
                    if c == 0:
                        pe.wait_ge(p_ready, st.at(2 * PCH, 9))
                    else:
                        pe.wait_ge(o_ready, st.at(2, 1))
                    for k in range(PCH):
                        rows, m = ROWS[k], c * PCH + k
                        dst = psF[:, 2 * c]
                        pe.matmul(dst, V_hi[0:rows, k, c], p_hi[0:rows, m], start=k == 0, stop=False)
                        pe.matmul(dst, V_hi[0:rows, k, c], p_lo[0:rows, m], start=False, stop=False)
                        pe.matmul(dst, V_lo[0:rows, k, c], p_hi[0:rows, m], start=False, stop=k == PCH - 1)
                    for k in range(PCH):
                        rows, m = ROWS[k], c * PCH + k
                        ones = pair_mask[0:rows, k].rearrange("p h d -> p (h d)")
                        pe.matmul(psF[:, 1], ones, p_hi[0:rows, m], start=k == 0, stop=False)
                        last = pe.matmul(psF[:, 1], ones, p_lo[0:rows, m], start=False, stop=k == PCH - 1)
                    last.then_inc(pv_ps, 1)
                if i == WO:
                    pe.wait_ge(o_lo, st.at(2, 2))
                    for t in range(NT):
                        last = product(psF[:, t // 2, t % 2 * D:t % 2 * D + D],
                                       [(xT_hi[:, k, t * P:(t + 1) * P], xT_lo[:, k, t * P:(t + 1) * P],
                                         Woh[:, k, :], Wol[:, k, :]) for k in range(KC)])
                        if t % 2:
                            last.then_inc(wo_ps, 1)
                if i == LN4T:
                    transpose_x(st, 3)
                if i == ROUTE:
                    pe.wait_ge(lo_ready, st.at(8, 8))
                    for t in range(NT):
                        last = product(psF[:, 2, t * E:(t + 1) * E],
                                       [(eT_hi[:, st.half, k, t * P:(t + 1) * P], eT_lo[:, st.half, k, t * P:(t + 1) * P],
                                         RWh[:, k, :], RWl[:, k, :]) for k in range(KC)])
                    last.then_inc(logit_ps, 1)

            def after(ex):
                down_half(ex, EX - 1, 0)
                down_half(ex, EX - 1, 1)

            run(pe, slot, after)

        @block.scalar
        def _(act):
            act.wait_ge(rows_loaded, 128)
            act.activation(gains[:, :], gains[:, :], ACT.Tanh).then_inc(setup_act, 1)

            def high_half(st, n):
                dst = eT_hi[:, st.half] if n == 3 else xT_hi
                if n == 3 and (st.const >= 2):
                    act.wait_ge(gu_ps, st.at(HID, -HID))
                for c in range(KC):
                    act.wait_ge(xT_ps, st.at(8, 2 * n + c + 1))
                    act.copy(dst[:, c], psF[:, c]).then_inc(hi_ready, 1)

            def slot(i, st, ex):
                if ex:
                    if i % 3 > 0:
                        q = 2 * (i // 3) + i % 3 - 1
                        act.wait_ge(g_done, ex.at(HID, q + 1))
                        if q >= 4 or ex.const:
                            act.wait_ge(y_ps, ex.at(HID, 2 * (q // 2) - 2))
                        else:
                            act.wait_ge(down_stored[q], 32 * len(range(q, EX, 4)))
                        act.copy(hid_hi[:, q % 4], tile3[:, q % 3]).then_inc(ghi_done, 1)
                    if i % 3 < 2:
                        q = 2 * (i // 3) + i % 3
                        act.wait_ge(gu_ps, ex.at(HID, q + 1))
                        if q >= 3 or ex.const:
                            act.wait_ge(glo_done, ex.at(HID, q - 2))
                        else:
                            act.wait_ge(split_done, len(staged))
                        act.activation(tile3[:, q % 3], psG[:, q % 2], ACT.Tanh, scale=0.5).then_inc(tanh_done, 1)
                if st is None:
                    return
                if i == LN1 + 1:
                    high_half(st, 0)
                for g in range(GRP):
                    if i == tanh_slot(g):
                        if g == 0:
                            act.wait_ge(feat_ps, st.at(1, 1))
                            if st.const == 0:
                                act.wait_ge(setup_dve, 5)
                        js = range(min(4, TXT - 4 * g))
                        for c in range(KC):
                            if 2 * g + c >= 3:
                                act.wait_ge(rho_part, st.at(2 * GRP, 2 * g + c - 2))
                            for j in js:
                                n = 8 * g + c * len(js) + j
                                bias = text_now[:, c, 4 * g + j:4 * g + j + 1]
                                act.activation(tanh_tiles[:, n % HRING], psF[:, c], ACT.Tanh, bias=bias).then_inc(h_ready, 1)
                if i == SOFT:
                    act.wait_ge(sm_sub, st.at(1, 1))
                    act.activation(sm[:, 2], sm[:, 1], ACT.Exp).then_inc(sm_exp, 1)
                if i == SOFT + 1:
                    act.wait_ge(film_in, st.at(1, 1))
                    for n in range(2):
                        last = act.activation(film[:, n], film[:, n], ACT.Tanh, bias=bc_row[:, n:n + 1])
                    last.then_inc(film_ready, 1)
                if i == LN2:
                    high_half(st, 1)
                if i == LN3T:
                    high_half(st, 2)
                if i == QPROJ:
                    for c in range(KC):
                        act.wait_ge(q32_ready, st.at(2, c + 1))
                        act.copy(qT_hi[:, c], xn_t[:, c]).then_inc(q_hi, 1)
                if i == PEAKT:
                    act.wait_ge(peakT_ps, st.at(1, 1))
                    act.mul(peakT[0:32, :], psF[0:32, 0], -1.0).then_inc(peakT_ready, 1)
                if SCORES <= i < SCORES + 4:
                    for m in range(3 * (i - SCORES), min(3 * (i - SCORES) + 3, 2 * PCH)):
                        rows = ROWS[m % PCH]
                        act.wait_ge(sc_ps, st.at(2 * PCH, m + 1))
                        if m >= 2:
                            act.wait_ge(p_lo_ready, st.at(2 * PCH, m - 1))
                        act.activation(p32[0:rows, m % 2], psF[0:rows, (2, 0, 1)[m % 3]], ACT.Exp).then_inc(p_ready, 1)
                if i in (PV, PV + 1):
                    c = i - PV
                    act.wait_ge(o_ready, st.at(2, c + 1))
                    act.copy(xT_hi[:, c], xn_t[:, c]).then_inc(o_hi, 1)
                if i == LN4T:
                    high_half(st, 3)
                if i == ROUTE:
                    act.wait_ge(logit_ps, st.at(1, 1))
                    act.activation(rs[:, 0], psF[:, 2, 0:NT * E].rearrange("p (t e) -> p t e", t=NT), ACT.Tanh,
                                   scale=0.5).then_inc(score_ready, 1)

            run(act, slot)

        @block.vector
        def _(dve):
            su = Chain(dve, setup_chain)
            su.begin(lambda per, k: k)
            fr = Chain(dve, front_chain)
            kv = Chain(dve, kv_chain)

            def split(ch, hi, lo, src):
                ch.link(dve.tensor_copy(hi, src))
                return dve.tensor_tensor(lo, src, hi, ALU.subtract)

            su.link(dve.memset(coef_w[:, :, :], 0.0))
            su.link(dve.memset(coef_b[:, :, :], 0.0))
            su.link(dve.memset(text_mask[:, :, :], -3e38))
            dve.wait_ge(setup_pe, 1)
            su.link(dve.tensor_copy(ctxT, psG[:, :, 0:B * TXT]))
            split(su, ctxT_hi[:, :, :], ctxT_lo[:, :, :], ctxT).then_inc(setup_dve, 1)
            dve.wait_ge(setup_pe, 2)
            dve.wait_ge(text_loaded, 64)
            for c in range(KC):
                last = dve.tensor_scalar(text_bias[:, c, :], psU[:, c, 0:B * TXT], bcol[:, c:c + 1], None, ALU.add)
            last.then_inc(setup_dve, 1)

            def by_slot(dst, src, op):
                whole = TXT // 4
                d = dst.rearrange("p (j i) -> p i j", j=4)
                op(d[:, 0:whole, :], src[:, 0:4 * whole].rearrange("p (i j) -> p i j", j=4))
                su.link(op(d[:, whole, 0:TXT - 4 * whole], src[:, 4 * whole:TXT]))

            dve.wait_ge(setup_pe, 3)
            dve.wait_ge(wc_loaded, 80)
            for b in range(B):
                for n, dst in enumerate((coef_w, coef_b)):
                    by_slot(dst[:, b], psG[:, n, b * TXT:(b + 1) * TXT], lambda d, s: dve.tensor_copy(d, s))
                by_slot(text_mask[:, b], mask_int[:, b],
                        lambda d, s: dve.tensor_scalar(d, s, 1.0, -NEG, ALU.subtract, ALU.mult))
            dve.wait_ge(setup_pe, 4)
            dve.tensor_copy(up_auxT[0:50, :], psY[0:50, 0, :])
            split(su, RWh[:, :, :], RWl[:, :, :], psY[:, 1, 128:128 + KC * E].rearrange("p (k e) -> p k e", k=KC))
            dve.tensor_copy(lora1[0:4, :], psF[0:4, 2, 0:D]).then_inc(setup_dve, 1)
            dve.wait_ge(setup_pe, 5)
            dve.tensor_copy(lora2[0:50, :], psF[0:50, 2, 0:D]).then_inc(setup_dve, 1)
            for n, (hi, lo) in ((0, (W0h, W0l)), (2, (Wkh, Wkl)), (3, (Wvh, Wvl)), (4, (Wqh, Wql)), (5, (Woh, Wol))):
                dve.wait_ge(small_loaded[n], 16)
                split(su, hi[:, :, :], lo[:, :, :], small_stage[n].rearrange("p (k d) -> p k d", k=KC))
            dve.wait_ge(setup_pe, 6)
            split(su, W1h[:, :, :], W1l[:, :, :], psU[:, :, 0:D]).then_inc(setup_dve, 1)
            dve.wait_ge(setup_act, 1)
            dve.wait_ge(rows_loaded, 128)
            dve.tensor_scalar(b1_row[:, :], b1_row[:, :], gains[:, 2:3], None, ALU.mult)
            dve.tensor_scalar(bo_row[:, :], bo_row[:, :], gains[:, 1:2], None, ALU.mult)
            dve.tensor_scalar(bq[:, :], bq[:, :], float(DH) ** -0.5, None, ALU.mult)
            su.link(dve.memset(combine[:, :, :, E:EX], 0.5))
            su.link(dve.tensor_scalar(combine[:, :, :, E:EX], combine[:, :, :, E:EX], gains[:, 3:4], None, ALU.mult))
            dve.wait_ge(consts, 8)

            def split_expert(n):
                e, what = staged[n]
                dve.wait_ge(stage_loaded[n % 3], 16 * (n // 3 + 1))
                if what == "down":
                    if e >= 4:
                        dve.wait_ge(down_stored[e % 4], 32 * (e // 4))
                    hi, lo, src = hid_hi[:, e % 4], hid_lo[:, e % 4], stage[n % 3]
                else:
                    hi, lo = (gate_hi, gate_lo) if what == "gate" else (up_hi, up_lo)
                    hi, lo, src = hi[:, e], lo[:, e], stage[n % 3].rearrange("p (k d) -> p k d", k=KC)
                split(su, hi, lo, src).then_inc(split_done, 1)

            def layer_norm(st, src):
                for t in range(NT):
                    last = dve.bn_stats(stats[:, t, :], src[:, t, :])
                fr.link(last)
                dve.tensor_tensor(mv[:, 0], stats[:, :, 1], stats[:, :, 4], ALU.add)
                dve.tensor_tensor(mv[:, 1], stats[:, :, 1], stats[:, :, 4], ALU.subtract)
                fr.link(dve.tensor_tensor(veps[:, :], stats[:, :, 2], stats[:, :, 5], ALU.add))
                dve.tensor_scalar(mv[:, 0], mv[:, 0], 0.5, None, ALU.mult)
                dve.tensor_tensor(mv[:, 1], mv[:, 1], mv[:, 1], ALU.mult)
                fr.link(dve.tensor_scalar(veps[:, :], veps[:, :], 1.0 / D, EPS, ALU.mult, ALU.add))
                fr.link(dve.scalar_tensor_tensor(out=veps[:, :], in0=mv[:, 1], scalar=0.25, in1=veps[:, :],
                                                 op0=ALU.mult, op1=ALU.add))
                fr.link(dve.tensor_scalar(rstd[:, :].bitcast(I32), veps[:, :].bitcast(I32), -0.5, 1597463007.0,
                                          ALU.mult, ALU.add))
                for _ in range(4):
                    fr.link(dve.tensor_tensor(nwt[:, :], rstd[:, :], rstd[:, :], ALU.mult))
                    fr.link(dve.scalar_tensor_tensor(out=nwt[:, :], in0=nwt[:, :], scalar=-0.5, in1=veps[:, :],
                                                     op0=ALU.mult, op1=ALU.mult))
                    fr.link(dve.scalar_tensor_tensor(out=rstd[:, :], in0=nwt[:, :], scalar=1.5, in1=rstd[:, :],
                                                     op0=ALU.add, op1=ALU.mult))
                for t in range(NT):
                    last = dve.tensor_scalar(xn[:, t, :], src[:, t, :], mv[:, 0, t:t + 1], rstd[:, t:t + 1],
                                             ALU.subtract, ALU.mult)
                last.then_inc(xn_ready, 1)

            def low_half(st, n):
                hi, lo = (eT_hi[:, st.half], eT_lo[:, st.half]) if n == 3 else (xT_hi, xT_lo)
                for c in range(KC):
                    dve.wait_ge(hi_ready, st.at(8, 2 * n + c + 1))
                    dve.tensor_tensor(lo[:, c], psF[:, c], hi[:, c], ALU.subtract).then_inc(lo_ready, 1)

            def ranks(dst, v, n, a_, b_):
                mine = v.unsqueeze(3).to_broadcast([P, NT, n, n])
                theirs = v.unsqueeze(2).to_broadcast([P, NT, n, n])
                low = lower[:, 0:n, 0:n].unsqueeze(1).to_broadcast([P, NT, n, n])
                dve.tensor_tensor(a_, theirs, mine, ALU.is_gt)
                fr.link(dve.tensor_tensor(b_, theirs, mine, ALU.is_equal))
                fr.link(dve.tensor_tensor(b_, b_, low, ALU.mult))
                fr.link(dve.tensor_tensor(a_, a_, b_, ALU.add))
                fr.link(dve.tensor_reduce(dst, a_, AX, ALU.add))

            def route(st):
                dve.wait_ge(score_ready, st.at(1, 1))
                score, biased = rs[:, 1], rs[:, 2]
                fr.link(dve.tensor_scalar(score, rs[:, 0], 0.5, 0.5, ALU.mult, ALU.add))
                fr.link(dve.tensor_tensor(biased, score, rbias[:, :].unsqueeze(1).to_broadcast([P, NT, E]), ALU.add))
                by = biased.rearrange("p t (g n) -> p t g n", g=NG)
                q4 = [rs[:, 3, :, 4 * n:4 * n + 4] for n in range(4)]
                dve.tensor_tensor(q4[0], by[:, :, :, 0], by[:, :, :, 1], ALU.max)
                dve.tensor_tensor(q4[1], by[:, :, :, 0], by[:, :, :, 1], ALU.min)
                dve.tensor_tensor(q4[2], by[:, :, :, 2], by[:, :, :, 3], ALU.max)
                fr.link(dve.tensor_tensor(q4[3], by[:, :, :, 2], by[:, :, :, 3], ALU.min))
                top, mid, rest_, second = [rs[:, 4, :, 4 * n:4 * n + 4] for n in range(4)]
                dve.tensor_tensor(top, q4[0], q4[2], ALU.max)
                dve.tensor_tensor(mid, q4[0], q4[2], ALU.min)
                fr.link(dve.tensor_tensor(rest_, q4[1], q4[3], ALU.max))
                fr.link(dve.tensor_tensor(second, mid, rest_, ALU.max))
                gscore, grank, chosen, off = [rs[:, 5, :, 4 * n:4 * n + 4] for n in range(4)]
                fr.link(dve.tensor_tensor(gscore, top, second, ALU.add))
                a4, b4 = (region[:, n:n + NT * NG * NG].rearrange("p (t e f) -> p t e f", t=NT, e=NG) for n in (0, 1024))
                ranks(grank, gscore, NG, a4, b4)
                fr.link(dve.tensor_scalar(chosen, grank, float(TOPG), None, ALU.is_lt))
                fr.link(dve.tensor_scalar(off, chosen, 1.0, None, ALU.subtract))
                masked = rs[:, 6].rearrange("p t (g n) -> p t g n", g=NG)
                fr.link(dve.tensor_tensor(masked, by, chosen.unsqueeze(3).to_broadcast([P, NT, NG, EPG]), ALU.mult))
                fr.link(dve.tensor_tensor(masked, masked, off.unsqueeze(3).to_broadcast([P, NT, NG, EPG]), ALU.add))
                ranks(rs[:, 7], rs[:, 6], E, rank_a, rank_b)
                fr.link(dve.tensor_scalar(rs[:, 8], rs[:, 7], float(TOPK), None, ALU.is_lt))
                fr.link(dve.tensor_tensor(rs[:, 9], rs[:, 8], score, ALU.mult))
                total, inv = rs[:, 10, :, 0], rs[:, 10, :, 1]
                fr.link(dve.tensor_reduce(total, rs[:, 9], AX, ALU.add))
                fr.link(dve.tensor_scalar(total, total, 1e-20, None, ALU.add))
                fr.link(dve.reciprocal(inv, total))
                fr.link(dve.tensor_scalar(inv, inv, 0.5 * SCALE, gains[:, 3:4], ALU.mult, ALU.mult))
                dve.tensor_tensor(combine[:, st.half, :, 0:E], rs[:, 9],
                                  inv.unsqueeze(2).to_broadcast([P, NT, E]), ALU.mult).then_inc(routed, 1)

            def add_y(ex, e, hf):
                dve.wait_ge(y_ps, ex.at(HID, 2 * e + hf + 1))
                if e:
                    dve.wait_ge(y_used, ex.at(HID, 2 * (e - 1) + hf + 1))
                for t in (2 * hf, 2 * hf + 1):
                    xt = x[:, ex.half, t]
                    last = dve.scalar_tensor_tensor(out=xt, in0=psY[:, t % 2], scalar=combine[:, ex.half, t, e:e + 1],
                                                    in1=xt, op0=ALU.mult, op1=ALU.add)
                last.then_inc(y_used, 1)

            def slot(i, st, ex):
                if ex:
                    e, k = i // 3, i % 3
                    if i == 0:
                        dve.wait_ge(routed, ex.at(1, 1))
                    if k == 1 and e:
                        add_y(ex, e - 1, 0)
                    if k < 2:
                        q = 2 * e + k
                        dve.wait_ge(tanh_done, ex.at(HID, q + 1))
                        dve.scalar_tensor_tensor(out=tile3[:, q % 3], in0=tile3[:, q % 3], scalar=1.0, in1=psG[:, k],
                                                 op0=ALU.add, op1=ALU.mult).then_inc(v_done, 1)
                        dve.wait_ge(v_done, ex.at(HID, q + 1))
                        dve.tensor_tensor(tile3[:, q % 3], tile3[:, q % 3], psU[:, k], ALU.mult).then_inc(g_done, 1)
                    if k == 2 and e:
                        add_y(ex, e - 1, 1)
                if st is None:
                    return
                xs = x[:, st.half]
                if i == 0:
                    fr.begin(st.at)
                if st.half == 0 and i == KV:
                    kv.begin(st.batch_at)
                    t0 = st.batch() * TXT
                    for dst, src in ((ctx8_hi, ctxT_hi), (ctx8_lo, ctxT_lo)):
                        for k2 in range(KC):
                            s = src[:, k2, bass.ds(t0, TXT)].unsqueeze(1).to_broadcast([P, HC, TXT])
                            last = dve.tensor_copy(dst[:, k2], s)
                    last.then_inc(ctx8_ready, 1)
                if st.half == 0 and KV < i <= KV + 3:
                    for n in range(3 * (i - KV - 1), 3 * (i - KV)):
                        dve.wait_ge(kv_ps, st.batch_at(9, n + 1))
                        if n < 4:
                            c, hf = n // 2, n % 2
                            tmp = kv32[:, n % 2, 0:PH]
                            mask = head_mask[:, HC // 2 * hf:HC // 2 * (hf + 1)].rearrange("p h t -> p (h t)")
                            kv.link(dve.scalar_tensor_tensor(out=tmp, in0=psF[:, n % 3, 0:PH], scalar=bk[:, c:c + 1], in1=mask,
                                                             op0=ALU.add, op1=ALU.mult))
                            cut = slice(hf * PH, (hf + 1) * PH)
                            split(kv, K_hi[:, c, cut], K_lo[:, c, cut], tmp).then_inc(kv_used, 1)
                        else:
                            m, rows = n - 4, ROWS[n - 4]
                            tmp = kv32[0:rows, n % 2, 0:D]
                            kv.link(dve.tensor_tensor(tmp, psF[0:rows, n % 3, 0:D], bv_row[0:rows, :], ALU.add))
                            t3 = tmp.rearrange("p (c d) -> p c d", c=KC)
                            mask = pair_mask[0:rows, m].rearrange("p h d -> p (h d)").unsqueeze(1).to_broadcast([rows, KC, P])
                            kv.link(dve.tensor_tensor(t3, t3, mask, ALU.mult))
                            split(kv, V_hi[0:rows, m], V_lo[0:rows, m], t3).then_inc(kv_used, 1)
                    if i == KV + 3:
                        kv.end()
                if i == LN1:
                    fr.link(dve.tensor_copy(text_now[:, :, :], text_bias[:, :, bass.ds(st.batch() * TXT, TXT)]))
                    dve.wait_ge(x_loaded[st.half], st.batch_at(16, 16))
                    layer_norm(st, xs)
                if i == LN1 + 1:
                    low_half(st, 0)
                if st.const == 0 and TANH0 <= i < TAIL:
                    span = TAIL - TANH0
                    for n in range(len(staged) * (i - TANH0) // span, len(staged) * (i - TANH0 + 1) // span):
                        split_expert(n)
                if i == TAIL:
                    dve.wait_ge(rho_part, st.at(2 * GRP, 2 * GRP))
                    dve.tensor_copy(rhoT, psF[:, RHO]).then_inc(rhoT_ready, 1)
                b = st.batch()
                if i == SOFT:
                    dve.wait_ge(rho_ps, st.at(1, 1))
                    rho = psF[:, 0].rearrange("p (t j i) -> p t j i", t=NT, j=4)[:, :, :, 0:GRP]
                    mask = text_mask[:, bass.ds(b, 1), :].rearrange("p b (j i) -> p b j i", j=4).to_broadcast([P, NT, 4, GRP])
                    fr.link(dve.tensor_tensor(sm[:, 0].rearrange("p t (j i) -> p t j i", j=4), rho, mask, ALU.add))
                    fr.link(dve.tensor_reduce(smax[:, :], sm[:, 0], AX, ALU.max))
                    dve.tensor_tensor(sm[:, 1], sm[:, 0], smax[:, :].unsqueeze(2).to_broadcast([P, NT, SL]),
                                      ALU.subtract).then_inc(sm_sub, 1)
                if i == SOFT + 1:
                    dve.wait_ge(sm_exp, st.at(1, 1))
                    dve.tensor_reduce(sden[:, :], sm[:, 2], AX, ALU.add)
                    for n, coef in enumerate((coef_w, coef_b)):
                        cf = coef[:, bass.ds(b, 1), :].to_broadcast([P, NT, SL])
                        fr.link(dve.tensor_tensor(sm[:, n], sm[:, 2], cf, ALU.mult))
                        fr.link(dve.tensor_reduce(snum[:, n], sm[:, n], AX, ALU.add))
                    fr.link(dve.reciprocal(sden[:, :], sden[:, :]))
                    dve.tensor_tensor(film[:, :, :], snum[:, :, :], sden[:, :].unsqueeze(1).to_broadcast([P, 2, NT]),
                                      ALU.mult).then_inc(film_in, 1)
                    dve.wait_ge(film_ready, st.at(1, 1))
                    fr.link(dve.tensor_scalar(film[:, :, :], film[:, :, :], gains[:, 0:1], None, ALU.mult))
                    for t in range(NT):
                        last = dve.scalar_tensor_tensor(out=xs[:, t], in0=xn[:, t], scalar=film[:, 0, t:t + 1], in1=xs[:, t],
                                                        op0=ALU.mult, op1=ALU.add)
                    fr.link(last)
                    for t in range(NT):
                        last = dve.tensor_scalar(xs[:, t], xs[:, t], film[:, 1, t:t + 1], None, ALU.add)
                    fr.link(last)
                    layer_norm(st, xs)
                if i == LN2:
                    low_half(st, 1)
                    fr.link(dve.tensor_tensor(xs, xs, b1_row[:, :].unsqueeze(1).to_broadcast([P, NT, D]), ALU.add))
                if i == LIN:
                    for j in range(2):
                        dve.wait_ge(lin_ps, st.at(2, j + 1))
                        xj = xs[:, 2 * j:2 * j + 2].rearrange("p t d -> p (t d)")
                        last = dve.scalar_tensor_tensor(out=xj, in0=psF[:, j], scalar=gains[:, 2:3], in1=xj,
                                                        op0=ALU.mult, op1=ALU.add)
                    fr.link(last)
                    layer_norm(st, xs)
                if i == LN3T:
                    low_half(st, 2)
                if i == QPROJ:
                    for c in range(KC):
                        dve.wait_ge(q_ps, st.at(2, c + 1))
                        dve.tensor_scalar(xn_t[:, c], psF[:, c], float(DH) ** -0.5, bq[:, c:c + 1], ALU.mult,
                                          ALU.add).then_inc(q32_ready, 1)
                    for c in range(KC):
                        dve.wait_ge(q_hi, st.at(2, c + 1))
                        dve.tensor_tensor(qT_lo[:, c], xn_t[:, c], qT_hi[:, c], ALU.subtract).then_inc(q_lo, 1)
                if i in (PEAK, PEAK + 1):
                    for n in range(8 * (i - PEAK), 8 * (i - PEAK + 1)):
                        t, c, hf = n // 4, n // 2 % 2, n % 2
                        h0 = HC * c + HC // 2 * hf
                        dve.wait_ge(peak_ps, st.at(16, n + 1))
                        dve.tensor_reduce(peak[:, t, h0:h0 + HC // 2],
                                          psF[:, n % 3, 0:PH].rearrange("p (h t) -> p h t", t=TXT), AX,
                                          ALU.max).then_inc(peak_used, 1)
                    if i == PEAK + 1:
                        fr.link(dve.tensor_tensor(xs, xs, bo_row[:, :].unsqueeze(1).to_broadcast([P, NT, D]), ALU.add))
                if SCORES <= i < SCORES + 4:
                    for m in range(3 * (i - SCORES), min(3 * (i - SCORES) + 3, 2 * PCH)):
                        rows = ROWS[m % PCH]
                        dve.wait_ge(p_ready, st.at(2 * PCH, m + 1))
                        dve.tensor_copy(p_hi[0:rows, m], p32[0:rows, m % 2]).then_inc(p_hi_ready, 1)
                if i in (PV, PV + 1):
                    c = i - PV
                    dve.wait_ge(pv_ps, st.at(2, c + 1))
                    fr.link(dve.reciprocal(xn_t[:, c], psF[:, 1]))
                    dve.tensor_tensor(xn_t[:, c], xn_t[:, c], psF[:, 2 * c], ALU.mult).then_inc(o_ready, 1)
                    dve.wait_ge(o_hi, st.at(2, c + 1))
                    dve.tensor_tensor(xT_lo[:, c], xn_t[:, c], xT_hi[:, c], ALU.subtract).then_inc(o_lo, 1)
                if i == WO:
                    for j in range(2):
                        dve.wait_ge(wo_ps, st.at(2, j + 1))
                        xj = xs[:, 2 * j:2 * j + 2].rearrange("p t d -> p (t d)")
                        last = dve.scalar_tensor_tensor(out=xj, in0=psF[:, j], scalar=gains[:, 1:2], in1=xj,
                                                        op0=ALU.mult, op1=ALU.add)
                    fr.link(last)
                    layer_norm(st, xs)
                if i == LN4T:
                    low_half(st, 3)
                if i == ROUTE:
                    route(st)
                    fr.end()

            def after(ex):
                add_y(ex, EX - 1, 0)
                add_y(ex, EX - 1, 1)

            run(dve, slot, after)


INPUTS = ["x", "ctx_1024", "mask_BxS2_ik0", "g_xattn", "g_ffn",
          "L0_xattn_Ws", "L0_xattn_W", "L0_xattn_w", "L0_xattn_b", "L0_xattn_Wcw", "L0_xattn_bcw",
          "L0_xattn_Wcb", "L0_xattn_bcb", "L0_ffn_W", "L0_ffn_b", "L0_ffn_lora_down", "L0_ffn_lora_up",
          "L0_ffn_down_aux", "L0_ffn_up_aux", "L1_xattn_Wq", "L1_xattn_bq", "L1_xattn_Wk", "L1_xattn_bk",
          "L1_xattn_Wv", "L1_xattn_bv", "L1_xattn_Wo", "L1_xattn_bo", "L1_ffn_router_w", "L1_ffn_bias",
          "L1_ffn_gate_w", "L1_ffn_up_w", "L1_ffn_down_w", "L1_ffn_sh_gate_w", "L1_ffn_sh_up_w",
          "L1_ffn_sh_down_w"]


def kernel(**inputs):
    import concourse.bacc as bacc
    from concourse.bass_utils import run_bass_kernel_spmd

    nc = bacc.Bacc("TRN2", target_bir_lowering=False, num_devices=1)
    arrays, args = {}, {}
    for name in INPUTS:
        v = np.ascontiguousarray(inputs[name])
        arrays[f"in_{name}"] = v
        args[name] = nc.dram_tensor(f"in_{name}", v.shape, mybir.dt.from_np(v.dtype), kind="ExternalInput").ap()
    out = nc.dram_tensor("out_x", (B, S, D), F32, kind="ExternalOutput").ap()
    build(nc, args, out)
    r = run_bass_kernel_spmd(nc, [arrays], core_ids=[0])
    return r.results[0]["out_x"]
```

```python
from contextlib import ExitStack

import numpy as np
import concourse.bass as bass
from concourse import mybir

F32 = mybir.dt.float32
F16 = mybir.dt.float16
I32 = mybir.dt.int32
ALU = mybir.AluOpType
ACT = mybir.ActivationFunctionType
AX = mybir.AxisListType.X

P = 128
D = 256
KC = D // P
B, S, TXT = 4, 1024, 77
TOK = 512
NT = TOK // P
STEPS = B * S // TOK
HALVES = S // TOK
HEADS, DH = 16, 16
HC = P // DH
PAIRS = HC * TXT
PH = PAIRS // 2
PCH = -(-PAIRS // P)
ROWS = [min(P, PAIRS - P * k) for k in range(PCH)]
GRP = -(-TXT // 4)
SL = 4 * GRP
E, NG, EPG, TOPG, TOPK = 16, 4, 4, 2, 4
EX = E + 2
NEG = -1e30
SCALE = 2.5
EPS = 1e-5
HRING = 8

SETS = 2 * GRP

SLOTS = 3 * EX
LN1, LN1T, FEAT = 0, 3, 5
SOFT, FILM, KV, KVN, X1, LN2, LN2T, LIN, LN3, LN3T, QPROJ, PEAK, PEAKT, SCORES, PV, WO, LN4, LN4T, ROUTE = (
    1, 4, 7, 5, 8, 9, 12, 14, 15, 18, 20, 22, 29, (30, 37), (35, 41), 44, 45, 48, 50)
PEAK_SLOTS = [PEAK, PEAK + 1, PEAK + 1, PEAK + 2, PEAK + 3, PEAK + 4, PEAK + 4, PEAK + 5]
SCORE_SLOTS = [first + k // 2 for first in SCORES for k in range(PCH)]
TANH_SLOTS = [i for i in range(7, 53) if i not in SCORE_SLOTS][:SETS]


class Step:

    def __init__(self, const, r=None):
        self.const, self.r, self.half = const, r, const % HALVES

    def at(self, per, k):
        return self.const * per + k if self.r is None else self.r * (2 * per) + (self.const * per + k)

    def batch_at(self, per, k):
        return self.batch() * per + k if self.r is None else self.r * per + (self.const // 2 * per + k)

    def batch(self):
        return self.const // 2 if self.r is None else self.r + self.const // 2

    def index(self):
        return self.const if self.r is None else self.r * 2 + self.const


class Chain:

    def __init__(self, eng, sem):
        self.eng, self.sem, self.n, self.per, self.at = eng, sem, 0, None, None

    def begin(self, at):
        self.at, self.n = at, 0

    def end(self):
        assert self.per in (None, self.n)
        self.per = self.n

    def link(self, ins):
        ins.then_inc(self.sem, 1)
        self.n += 1
        self.eng.wait_ge(self.sem, self.at(self.per or 0, self.n))


def build(nc, a, out):
    ctx = ExitStack()
    with ctx:
        ctx.enter_context(nc.allow_non_contiguous_dma(reason="small vectors and matrices, once"))

        def sb(name, shape, dt=F32):
            return ctx.enter_context(nc.sbuf_tensor(name, shape, dt))

        def sem(name):
            return ctx.enter_context(nc.semaphore(name))

        gate_hi, gate_lo, up_hi, up_lo = (sb(n, [P, EX, KC, D], F16) for n in
                                          ("gate_hi", "gate_lo", "up_hi", "up_lo"))
        down_dram = nc.dram_tensor("down_split", [EX, P, 2 * KC * D], F16, kind="Internal").ap()
        down = sb("down", [P, 3, 2, KC, D], F16)
        W0h, W0l, W1h, W1l, Wqh, Wql, Wkh, Wkl, Wvh, Wvl, Woh, Wol = (
            sb(n, [P, KC, D], F16) for n in ("W0h", "W0l", "W1h", "W1l", "Wqh", "Wql",
                                             "Wkh", "Wkl", "Wvh", "Wvl", "Woh", "Wol"))
        RWh, RWl = sb("RWh", [P, KC, E], F16), sb("RWl", [P, KC, E], F16)
        ident = sb("ident", [P, P])
        head_mask = sb("head_mask", [P, HC, TXT], F16)
        pair_mask = sb("pair_mask", [P, PCH, HC, DH], F16)
        head_sel = sb("head_sel", [P, KC, HC, TXT], F16)
        lower = sb("lower", [P, E, E], F16)
        text_bias = sb("text_bias", [P, KC, B * TXT])
        scan_norm = sb("scan_norm", [P, 2, 2, NT])
        text_now = sb("text_now", [P, KC, TXT])
        wcol = sb("wcol", [P, KC])
        wslide = sb("wslide", [P, KC, 63])
        coef_w, coef_b = sb("coef_w", [P, B, SL]), sb("coef_b", [P, B, SL])
        text_mask = sb("text_mask", [P, B, SL])
        ctxT_hi, ctxT_lo = sb("ctxT_hi", [P, KC, B * TXT], F16), sb("ctxT_lo", [P, KC, B * TXT], F16)
        gains = sb("gains", [P, 4])
        bcol = sb("bcol", [P, KC])
        bq, bk = sb("bq", [P, KC]), sb("bk", [P, KC])
        wc_cols = sb("wc_cols", [P, 2, KC])
        bc_row = sb("bc_row", [P, 2])
        b1_row, bo_row, bv_row = sb("b1_row", [P, D]), sb("bo_row", [P, D]), sb("bv_row", [P, D])
        rbias = sb("rbias", [P, E])
        x = sb("x", [P, 2, NT, D])
        xin = sb("xin", [P, NT, D])
        xscan = sb("xscan", [P, NT, D])
        xn = sb("xn", [P, NT, D])
        xT_hi, xT_lo = sb("xT_hi", [P, KC, TOK], F16), sb("xT_lo", [P, KC, TOK], F16)
        eT_hi, eT_lo = sb("eT_hi", [P, 2, KC, TOK], F16), sb("eT_lo", [P, 2, KC, TOK], F16)
        stats, norm = sb("stats", [P, NT, 6]), sb("norm", [P, 2, NT])
        veps, dif, nwt = sb("veps", [P, NT]), sb("dif", [P, NT]), sb("nwt", [P, NT])
        K_hi, K_lo = sb("K_hi", [P, KC, PAIRS], F16), sb("K_lo", [P, KC, PAIRS], F16)
        V_hi, V_lo = sb("V_hi", [P, PCH, KC, P], F16), sb("V_lo", [P, PCH, KC, P], F16)
        qT_hi, qT_lo = sb("qT_hi", [P, KC, TOK], F16), sb("qT_lo", [P, KC, TOK], F16)
        peak = sb("peak", [P, NT, 32])
        peakT = sb("peakT", [P, TOK], F16)
        smax, sden, snum = sb("smax", [P, NT]), sb("sden", [P, NT]), sb("snum", [P, 2, NT])
        film = sb("film", [P, 2, NT])
        combine = sb("combine", [P, 2, NT, EX])
        tile3 = sb("tile3", [P, 3, TOK])
        hid_hi, hid_lo = sb("hid_hi", [P, 4, TOK], F16), sb("hid_lo", [P, 4, TOK], F16)
        feat = xscan[:, :, :].rearrange("p a b -> p (a b)").rearrange("p (c t) -> p c t", c=KC)
        region = sb("region", [P, HRING * TOK])
        tanh_tiles = region[:, :].rearrange("p (n t) -> p n t", n=HRING)
        Ws = region[:, 0:512].rearrange("p (k d) -> p k d", k=KC)
        ctx_rows = region[:, 512:1536].rearrange("p (b d) -> p b d", b=B)
        ctxT = region[:, 1536:1536 + KC * B * TXT].rearrange("p (k t) -> p k t", k=KC)
        o0 = 1536 + KC * B * TXT
        mask_int = region[:, o0:o0 + B * TXT].bitcast(I32).rearrange("p (b t) -> p b t", b=B)
        o0 += B * TXT
        up_rows = region[:, o0:o0 + 100].rearrange("p (c u) -> p c u", c=2)
        lora_dT = region[:, o0 + 100:o0 + 104]
        lora_uT = region[:, o0 + 104:o0 + 154]
        down_aux = region[:, o0 + 154:o0 + 410]
        lora1 = region[:, o0 + 410:o0 + 666]
        lora2 = region[:, o0 + 666:o0 + 922]
        up_auxT = region[:, o0 + 922:o0 + 1178]
        rw_rows = region[:, o0 + 1178:o0 + 1434].rearrange("p (k d) -> p k d", k=KC)
        rwT = region[:, o0 + 1434:o0 + 1434 + KC * E].rearrange("p (k e) -> p k e", k=KC)
        work = sb("work", [P, 7 * TOK])
        ctx8_hi = work[:, 0:PAIRS].bitcast(F16).rearrange("p (k h t) -> p k h t", k=KC, h=HC)
        ctx8_lo = work[:, PAIRS:2 * PAIRS].bitcast(F16).rearrange("p (k h t) -> p k h t", k=KC, h=HC)
        kv32 = work[:, 2 * PAIRS:2 * PAIRS + 1024].rearrange("p (r n) -> p r n", r=2)
        rhoT = work[:, 6 * TOK:7 * TOK]
        sm = work[:, 0:3 * NT * SL].rearrange("p (r t s) -> p r t s", r=3, t=NT)
        half = PCH * TOK // 2
        p_hi = work[:, 0:half].bitcast(F16).rearrange("p (m t) -> p m t", m=PCH)
        p_lo = work[:, half:2 * half].bitcast(F16).rearrange("p (m t) -> p m t", m=PCH)
        p32 = work[:, 2 * half:2 * half + 2 * TOK].rearrange("p (r t) -> p r t", r=2)
        rank_a = work[:, 0:1024].rearrange("p (t e f) -> p t e f", t=NT, e=E)
        rank_b = work[:, 1024:2048].rearrange("p (t e f) -> p t e f", t=NT, e=E)
        rs = work[:, 2048:2048 + 11 * NT * E].rearrange("p (r t e) -> p r t e", r=11, t=NT)
        xn_t = xn[:, :, :].rearrange("p a b -> p (a b)").rearrange("p (c t) -> p c t", c=2)
        stage = [tile3[:, n, :] for n in range(3)]
        stage2 = down[:, :, :, :, :].rearrange("p r a b c -> p r (a b c)")
        small_stage = stage + [stage2[:, n, :].bitcast(F32) for n in range(3)]
        down_tmp = [(hid_hi, hid_lo, n) for n in range(4)]

        psF = ctx.enter_context(nc.psum_tensor("psF", [P, 3, 512], F32))
        psG = ctx.enter_context(nc.psum_tensor("psG", [P, 2, 512], F32))
        psU = ctx.enter_context(nc.psum_tensor("psU", [P, 2, 512], F32))
        psY = ctx.enter_context(nc.psum_tensor("psY", [P, 2, D], F32))
        RHO = 2

        consts = sem("consts")
        x_loaded = sem("x_loaded")
        xscan_loaded = sem("xscan_loaded")
        stored = [sem("stored0"), sem("stored1")]
        text_loaded, wc_loaded, lora_loaded, rows_loaded = (
            sem(n) for n in ("text_loaded", "wc_loaded", "lora_loaded", "rows_loaded"))
        small_loaded = [sem(f"small_loaded{n}") for n in range(6)]
        stage_loaded = [sem(f"stage_loaded{n}") for n in range(3)]
        split_done = sem("split_done")
        down_stored = [sem(f"down_stored{n}") for n in range(4)]
        setup_pe, setup_dve, setup_act, setup_chain, pool_chain = (
            sem(n) for n in ("setup_pe", "setup_dve", "setup_act", "setup_chain", "pool_chain"))
        ctx8_ready, kv_ps, kv_hi, kv_lo, kv_chain = (
            sem(n) for n in ("ctx8_ready", "kv_ps", "kv_hi", "kv_lo", "kv_chain"))
        xn_scan, xT_scan, hi_scan, lo_scan = (sem(n) for n in ("xn_scan", "xT_scan", "hi_scan", "lo_scan"))
        feat_ready = sem("feat_ready")
        scan_chain = sem("scan_chain")
        xn_ready = sem("xn_ready")
        xT_ps = sem("xT_ps")
        hi_ready = sem("hi_ready")
        lo_ready = sem("lo_ready")
        feat_ps = sem("feat_ps")
        h_ready = sem("h_ready")
        rho_part = sem("rho_part")
        rhoT_ready, rho_ps = sem("rhoT_ready"), sem("rho_ps")
        sm_sub, sm_exp = sem("sm_sub"), sem("sm_exp")
        film_in, film_ready = sem("film_in"), sem("film_ready")
        lin_ps = sem("lin_ps")
        q_ps, q32_ready, q_hi, q_lo = (sem(n) for n in ("q_ps", "q32_ready", "q_hi", "q_lo"))
        peak_ps, peak_used = sem("peak_ps"), sem("peak_used")
        peakT_ps, peakT_ready = sem("peakT_ps"), sem("peakT_ready")
        sc_ps, p_ready, p_hi_ready, p_lo_ready = (
            sem(n) for n in ("sc_ps", "p_ready", "p_hi_ready", "p_lo_ready"))
        pv_ps, o_ready, o_hi, o_lo = (sem(n) for n in ("pv_ps", "o_ready", "o_hi", "o_lo"))
        wo_ps = sem("wo_ps")
        logit_ps, score_ready = sem("logit_ps"), sem("score_ready")
        routed = sem("routed")
        front_chain = sem("front_chain")
        gu_ps, tanh_done, v_done, g_done, ghi_done, glo_done = (
            sem(n) for n in ("gu_ps", "tanh_done", "v_done", "g_done", "ghi_done", "glo_done"))
        y_ps, y_used = sem("y_ps"), sem("y_used")
        down_loaded = [sem(f"down_loaded{n}") for n in range(3)]

        HID = 2 * EX
        xv = a["x"].rearrange("b (h t p) d -> (b h) p t d", h=HALVES, p=P)
        ov = out.rearrange("b (h t p) d -> (b h) p t d", h=HALVES, p=P)

        def w256(w):
            return w.rearrange("(k p) n -> p k n", p=P)

        def expert(e, what):
            if e < E:
                return w256(a[f"L1_ffn_{what}_w"][e])
            s = e - E
            if what == "down":
                return w256(a["L1_ffn_sh_down_w"][s * D:(s + 1) * D, :])
            return w256(a[f"L1_ffn_sh_{what}_w"][:, s * D:(s + 1) * D])

        staged = [(e, what) for e in range(EX) for what in ("gate", "up", "down")]

        def run(eng, slot):
            def side_by_side(sc, mi, ex):
                for i in range(SLOTS):
                    slot(i, sc, mi, ex)

            side_by_side(Step(0), None, None)
            side_by_side(Step(1), Step(0), None)
            side_by_side(Step(2), Step(1), Step(0))
            side_by_side(Step(3), Step(2), Step(1))
            with eng.Fori(0, STEPS // 2 - 2) as r:
                side_by_side(Step(4, r), Step(3, r), Step(2, r))
                side_by_side(Step(5, r), Step(4, r), Step(3, r))
            side_by_side(None, Step(STEPS - 1), Step(STEPS - 2))
            side_by_side(None, None, Step(STEPS - 1))

        def earlier(ex, e):
            if e >= 0:
                return ex, e
            return (Step(ex.const - 1, ex.r), e + EX) if ex.const else None

        def halves_at(ex, i):
            e, k = i // 3, i % 3
            if k == 0:
                return None
            due = earlier(ex, e - 3 + k)
            return (*due, 2 - k) if due else None

        last_halves = [(EX - 2, 1), (EX - 1, 0), (EX - 1, 1)]

        def kv_parts(n):
            if n < 4:
                c, cut = n // 2, slice(n % 2 * PH, (n % 2 + 1) * PH)
                return K_lo[:, c, cut], K_hi[:, c, cut], kv32[:, n % 2, 0:PH]
            m, rows = n - 4, ROWS[n - 4]
            return (V_lo[0:rows, m], V_hi[0:rows, m],
                    kv32[0:rows, n % 2, 0:D].rearrange("p (c d) -> p c d", c=KC))

        block = ctx.enter_context(nc.Block())

        @block.sync
        def _(sp):
            def load_x(st):
                if st.const:
                    sp.wait_ge(xn_ready, st.at(3, -2))
                sp.dma_start(xin[:, :, :], xv[st.index()]).then_inc(x_loaded, 16)

            def load_scan(st):
                sp.dma_start(xscan[:, :, :], xv[st.index()]).then_inc(xscan_loaded, 16)

            load_scan(Step(0))
            sp.dma_start(ctx_rows[0:TXT], a["ctx_1024"].rearrange("b t d -> t b d")).then_inc(text_loaded, 16)
            sp.dma_start(Ws, w256(a["L0_xattn_Ws"])).then_inc(text_loaded, 16)
            sp.dma_start(wcol[:, :], a["L0_xattn_w"].rearrange("(k p) o -> p (k o)", p=P)).then_inc(text_loaded, 16)
            sp.dma_start(bcol[:, :], a["L0_xattn_b"].rearrange("o (k p) -> p (k o)", p=P)).then_inc(text_loaded, 16)
            smalls = ["L0_xattn_W", "L0_ffn_W", "L1_xattn_Wk", "L1_xattn_Wv", "L1_xattn_Wq", "L1_xattn_Wo"]
            for n, name in enumerate(smalls):
                dst = small_stage[n].rearrange("p (k d) -> p k d", k=KC)
                sp.dma_start(dst, w256(a[name])).then_inc(small_loaded[n], 16)
            for n, name in enumerate(("Wcw", "Wcb")):
                sp.dma_start(wc_cols[:, n, :], a[f"L0_xattn_{name}"].rearrange("o (k p) -> p (o k)", p=P)).then_inc(wc_loaded, 16)
            for n, name in enumerate(("bcw", "bcb")):
                sp.dma_start(bc_row[:, n:n + 1], a[f"L0_xattn_{name}"].partition_broadcast(P)).then_inc(wc_loaded, 16)
            sp.dma_start(mask_int, a["mask_BxS2_ik0"].partition_broadcast(P)).then_inc(wc_loaded, 16)
            sp.dma_start(up_rows, a["L0_ffn_up_aux"].rearrange("(c p) u -> p c u", p=P)).then_inc(lora_loaded, 16)
            sp.dma_start(lora_dT[0:100], a["L0_ffn_lora_down"].rearrange("r d -> d r")).then_inc(lora_loaded, 16)
            sp.dma_start(lora_uT[0:4], a["L0_ffn_lora_up"].rearrange("u r -> r u")).then_inc(lora_loaded, 16)
            sp.dma_start(down_aux[0:100], a["L0_ffn_down_aux"]).then_inc(lora_loaded, 16)
            sp.dma_start(rw_rows[0:E], a["L1_ffn_router_w"].rearrange("e (k p) -> e k p", k=KC)).then_inc(lora_loaded, 16)
            for n, name in enumerate(("g_xattn", "g_ffn")):
                sp.dma_start(gains[:, 2 * n:2 * n + 2], a[name].partition_broadcast(P)).then_inc(rows_loaded, 16)
            for dst, name in ((bq, "L1_xattn_bq"), (bk, "L1_xattn_bk")):
                sp.dma_start(dst[:, :], a[name].rearrange("(k p) -> p k", p=P)).then_inc(rows_loaded, 16)
            for dst, name in ((b1_row, "L0_ffn_b"), (bo_row, "L1_xattn_bo"), (bv_row, "L1_xattn_bv"), (rbias, "L1_ffn_bias")):
                sp.dma_start(dst[:, :], a[name].partition_broadcast(P)).then_inc(rows_loaded, 16)
            load_x(Step(0))

            sp.wait_ge(setup_dve, 5)
            for n in range(len(staged) + 3):
                if n >= 3:
                    sp.wait_ge(split_done, n - 2)
                    e, what = staged[n - 3]
                    if what == "down":
                        src = down_tmp[e % 4]
                        sp.dma_start(down_dram[e, :, 0:TOK], src[0][:, e % 4, :]).then_inc(down_stored[e % 4], 16)
                        sp.dma_start(down_dram[e, :, TOK:2 * TOK], src[1][:, e % 4, :]).then_inc(down_stored[e % 4], 16)
                if n < len(staged):
                    e, what = staged[n]
                    sp.dma_start(stage[n % 3].rearrange("p (k d) -> p k d", k=KC), expert(e, what)).then_inc(stage_loaded[n % 3], 16)
            for n in range(4):
                sp.wait_ge(down_stored[n], 32 * len(range(n, EX, 4)))

            def load_down(st, e):
                if e < 3:
                    if st.const > 0 or st.r is not None:
                        sp.wait_ge(y_ps, st.at(HID, 2 * (e - 3) + 2))
                else:
                    sp.wait_ge(y_ps, st.at(HID, 2 * (e - 3) + 2))
                sp.dma_start(down[:, e % 3].rearrange("p a b c -> p (a b c)"), down_dram[e]).then_inc(down_loaded[e % 3], 16)

            def rest(ex, scan=True):
                if scan:
                    sc = Step(ex.const + 2, ex.r)
                    sp.wait_ge(h_ready, sc.at(2 * TXT, 0))
                    load_scan(sc)
                for e in range(3):
                    load_down(ex, e)
                if ex.const:
                    before = Step(ex.const - 1, ex.r)
                    sp.wait_ge(y_used, before.at(HID, HID))
                    sp.dma_start(ov[before.index()], x[:, before.half]).then_inc(stored[before.half], 16)
                for e in range(3, EX):
                    load_down(ex, e)
                    if e == 6 and scan:
                        load_x(sc)

            sp.wait_ge(h_ready, 2 * TXT)
            load_scan(Step(1))
            load_x(Step(1))
            rest(Step(0))
            rest(Step(1))
            with sp.Fori(0, STEPS // 2 - 2) as r:
                rest(Step(2, r))
                rest(Step(3, r))
            rest(Step(STEPS - 2), scan=False)
            rest(Step(STEPS - 1), scan=False)
            sp.wait_ge(y_used, STEPS * HID)
            sp.dma_start(ov[STEPS - 1], x[:, 1]).then_inc(stored[1], 16)
            for h in range(2):
                sp.wait_ge(stored[h], 16 * B)

        @block.gpsimd
        def _(pool):
            cn = Chain(pool, pool_chain)
            cn.begin(lambda per, k: k)
            cn.link(pool.memset(ident[:, :], 0.0))
            pool.affine_select(out=ident[:, :], in_=ident[:, :], compare_op=ALU.not_equal, fill=1.0,
                               base=0, pattern=[[-1, P]], channel_multiplier=1).then_inc(consts, 1)
            cn.link(pool.memset(wslide[:, :, :], 0.0))
            pool.wait_ge(text_loaded, 64)
            for k in range(KC):
                last = pool.tensor_tensor(wslide[:, k, 31:32], wslide[:, k, 31:32], wcol[:, k:k + 1], ALU.add)
            last.then_inc(consts, 1)
            cn.link(pool.memset(head_mask[:, :, :], 1.0))
            cn.link(pool.affine_select(out=head_mask[:, :, :], in_=head_mask[:, :, :], compare_op=ALU.is_ge, fill=0.0,
                                       base=0, pattern=[[-DH, HC], [0, TXT]], channel_multiplier=1))
            pool.affine_select(out=head_mask[:, :, :], in_=head_mask[:, :, :], compare_op=ALU.is_ge, fill=0.0,
                               base=DH - 1, pattern=[[DH, HC], [0, TXT]], channel_multiplier=-1).then_inc(consts, 1)
            cn.link(pool.memset(pair_mask[:, :, :, :], 1.0))
            cn.link(pool.affine_select(out=pair_mask[:, :, :, :], in_=pair_mask[:, :, :, :], compare_op=ALU.is_ge, fill=0.0,
                                       base=0, pattern=[[P, PCH], [-TXT, HC], [0, DH]], channel_multiplier=1))
            pool.affine_select(out=pair_mask[:, :, :, :], in_=pair_mask[:, :, :, :], compare_op=ALU.is_ge, fill=0.0,
                               base=TXT - 1, pattern=[[-P, PCH], [TXT, HC], [0, DH]], channel_multiplier=-1).then_inc(consts, 1)
            cn.link(pool.memset(head_sel[:, :, :, :], 0.0))
            pool.affine_select(out=head_sel[:, :, :, :], in_=head_sel[:, :, :, :], compare_op=ALU.not_equal, fill=1.0,
                               base=0, pattern=[[-HC, KC], [-1, HC], [0, TXT]], channel_multiplier=1).then_inc(consts, 1)
            cn.link(pool.memset(lower[:, :, :], 1.0))
            pool.affine_select(out=lower[:, :, :], in_=lower[:, :, :], compare_op=ALU.is_ge, fill=0.0,
                               base=-1, pattern=[[1, E], [-1, E]], channel_multiplier=0).then_inc(consts, 1)
            pool.memset(peak[:, :, :], 0.0).then_inc(consts, 1)
            pool.memset(peakT[:, :], 0.0).then_inc(consts, 1)

            def slot(i, sc, st, ex):
                if ex and i % 3 > 0:
                    q = 2 * (i // 3) + i % 3 - 1
                    pool.wait_ge(ghi_done, ex.at(HID, q + 1))
                    if q >= 4 or ex.const or ex.r is not None:
                        pool.wait_ge(y_ps, ex.at(HID, 2 * (q // 2) - 2))
                    pool.tensor_tensor(hid_lo[:, q % 4], tile3[:, q % 3], hid_hi[:, q % 4], ALU.subtract).then_inc(glo_done, 1)
                if st is None:
                    return
                if st.half == 0 and KV <= i < KV + KVN:
                    for n in range(2 * (i - KV), min(2 * (i - KV + 1), 9)):
                        pool.wait_ge(kv_hi, st.batch_at(9, n + 1))
                        lo, hi, src = kv_parts(n)
                        pool.tensor_tensor(lo, src, hi, ALU.subtract).then_inc(kv_lo, 1)
                for m in range(2 * PCH):
                    if i == SCORE_SLOTS[m]:
                        k, rows = m % PCH, ROWS[m % PCH]
                        pool.wait_ge(p_hi_ready, st.at(2 * PCH, m + 1))
                        pool.tensor_tensor(p_lo[0:rows, k], p32[0:rows, m % 2], p_hi[0:rows, k], ALU.subtract).then_inc(p_lo_ready, 1)

            run(pool, slot)

        @block.tensor
        def _(pe):
            def product(out_, terms):
                for n, (lh, ll, rh, rl) in enumerate(terms):
                    pe.matmul(out_, lh, rh, start=n == 0, stop=False)
                    pe.matmul(out_, lh, rl, start=False, stop=False)
                    last = pe.matmul(out_, ll, rh, start=False, stop=n == len(terms) - 1)
                return last

            def turn(out_, in_, rows=P):
                return pe.transpose(out_, in_, ident[0:rows, 0:rows])

            pe.wait_ge(consts, 1)
            pe.wait_ge(text_loaded, 64)
            for b in range(B):
                for k in range(KC):
                    last = turn(psG[:, k, b * TXT:(b + 1) * TXT], ctx_rows[0:TXT, b, k * P:(k + 1) * P], TXT)
            last.then_inc(setup_pe, 1)
            pe.wait_ge(setup_dve, 1)
            for c in range(KC):
                for k in range(KC):
                    last = pe.matmul(psU[:, c, 0:B * TXT], Ws[:, k, c * P:(c + 1) * P], ctxT[:, k, :],
                                     start=k == 0, stop=k == KC - 1)
            last.then_inc(setup_pe, 1)
            pe.wait_ge(wc_loaded, 80)
            for n in range(2):
                for k in range(KC):
                    last = pe.matmul(psG[:, n, 0:B * TXT], wc_cols[:, n, k:k + 1].to_broadcast([P, P]), ctxT[:, k, :],
                                     start=k == 0, stop=k == KC - 1)
            last.then_inc(setup_pe, 1)
            pe.wait_ge(lora_loaded, 80)
            for c in range(2):
                pe.transpose(psY[0:50, 0, c * P:(c + 1) * P], up_rows[:, c, :], ident[:, :])
            for k in range(KC):
                turn(psY[:, 1, 128 + k * E:128 + (k + 1) * E], rw_rows[0:E, k, :], E)
            pe.matmul(psF[0:4, 2, 0:D], lora_dT[0:100, :], down_aux[0:100, :], start=True, stop=True).then_inc(setup_pe, 1)
            pe.wait_ge(setup_dve, 3)
            pe.matmul(psF[0:50, 2, 0:D], lora_uT[0:4, 0:50], lora1[0:4, :], start=True, stop=True).then_inc(setup_pe, 1)
            pe.wait_ge(setup_dve, 4)
            pe.wait_ge(small_loaded[1], 16)
            wnat = small_stage[1].rearrange("p (o d) -> p o d", o=2)
            for k in range(KC):
                pe.matmul(psU[:, k, 0:D], lora2[0:50, k * P:(k + 1) * P], up_auxT[0:50, :], start=True, stop=False)
                for o in range(2):
                    last = pe.matmul(psU[:, k, o * P:(o + 1) * P], wnat[:, o, k * P:(k + 1) * P], ident[:, :],
                                     start=False, stop=o == 1)
            last.then_inc(setup_pe, 1)

            def gate_up(ex, q):
                e, f = q // 2, q % 2
                if q == 0:
                    pe.wait_ge(lo_ready, ex.at(6, 6))
                if ex.const == 0 and f == 0:
                    pe.wait_ge(split_done, 3 * e + 2)
                if q >= 2 or ex.const:
                    pe.wait_ge(g_done, ex.at(HID, q - 1))
                for ps, wh, wl in ((psG, gate_hi, gate_lo), (psU, up_hi, up_lo)):
                    last = product(ps[:, f], [(wh[:, e, k, f * P:(f + 1) * P], wl[:, e, k, f * P:(f + 1) * P],
                                               eT_hi[:, ex.half, k], eT_lo[:, ex.half, k]) for k in range(KC)])
                last.then_inc(gu_ps, 1)

            def down_half(ex, e, hf):
                if hf == 0:
                    pe.wait_ge(glo_done, ex.at(HID, 2 * e + 2))
                    pe.wait_ge(down_loaded[e % 3], ex.at(6 * 16, 16 * (e // 3 + 1)))
                if 2 * e + hf or ex.const:
                    pe.wait_ge(y_used, ex.at(HID, 2 * e + hf))
                for t in (2 * hf, 2 * hf + 1):
                    last = product(psY[:, t % 2], [(hid_hi[:, (2 * e + f) % 4, t * P:(t + 1) * P],
                                                    hid_lo[:, (2 * e + f) % 4, t * P:(t + 1) * P],
                                                    down[:, e % 3, 0, f], down[:, e % 3, 1, f]) for f in range(2)])
                last.then_inc(y_ps, 1)

            def transpose_x(done):
                for c in range(KC):
                    for t in range(NT):
                        last = turn(psF[:, c, t * P:(t + 1) * P], xn[:, t, c * P:(c + 1) * P])
                    last.then_inc(done, 1)

            def rho_set(st, g, c):
                js = range(min(4, TXT - 4 * g))
                pe.wait_ge(h_ready, st.at(2 * TXT, 8 * g + (c + 1) * len(js)))
                for j in js:
                    n = 8 * g + c * len(js) + j
                    last = pe.matmul(psF[32 * j:32 * j + 32, RHO, :], wslide[:, c, 31 - g:63 - g], tanh_tiles[:, n % HRING],
                                     start=g == 0 and c == 0, stop=c == 1 and 4 * (g + 1) + j >= TXT)
                last.then_inc(rho_part, 1)

            def scan(i, st):
                if i == LN1T:
                    pe.wait_ge(xn_scan, st.at(1, 1))
                    if st.const:
                        pe.wait_ge(sm_sub, st.at(1, 0))
                    transpose_x(xT_scan)
                if i == FEAT:
                    pe.wait_ge(lo_scan, st.at(2, 2))
                    for c in range(KC):
                        last = product(psF[:, c], [(W0h[:, k, c * P:(c + 1) * P], W0l[:, k, c * P:(c + 1) * P],
                                                    xT_hi[:, k], xT_lo[:, k]) for k in range(KC)])
                    last.then_inc(feat_ps, 1)
                for s in range(SETS):
                    if i == TANH_SLOTS[s] + 1:
                        if s == 0:
                            if st.const == 0:
                                pe.wait_ge(consts, 2)
                            else:
                                pe.wait_ge(rhoT_ready, st.at(1, 0))
                        rho_set(st, s // 2, s % 2)

            def slot(i, sc, st, ex):
                if ex:
                    k = i % 3
                    due = halves_at(ex, i)
                    if due:
                        down_half(*due)
                    if k < 2:
                        gate_up(ex, 2 * (i // 3) + k)
                if sc:
                    scan(i, sc)
                if st is None:
                    return
                if st.half == 0 and KV <= i < KV + KVN:
                    if i == KV:
                        pe.wait_ge(ctx8_ready, st.batch_at(1, 1))
                        pe.wait_ge(feat_ready, st.at(1, 2))
                    flat_hi = ctx8_hi.rearrange("p k h t -> p k (h t)")
                    flat_lo = ctx8_lo.rearrange("p k h t -> p k (h t)")
                    for n in range(2 * (i - KV), min(2 * (i - KV + 1), 9)):
                        if n >= 2:
                            pe.wait_ge(kv_hi, st.batch_at(9, n - 1))
                        if n < 4:
                            c, hf = n // 2, n % 2
                            last = product(psF[:, n % 2, 0:PH], [(Wkh[:, k, c * P:(c + 1) * P], Wkl[:, k, c * P:(c + 1) * P],
                                                                  flat_hi[:, k, hf * PH:(hf + 1) * PH],
                                                                  flat_lo[:, k, hf * PH:(hf + 1) * PH]) for k in range(KC)])
                        else:
                            m = n - 4
                            rows = ROWS[m]
                            last = product(psF[0:rows, n % 2, 0:D], [(flat_hi[:, k, m * P:m * P + rows],
                                                                      flat_lo[:, k, m * P:m * P + rows],
                                                                      Wvh[:, k, :], Wvl[:, k, :]) for k in range(KC)])
                        last.then_inc(kv_ps, 1)
                if i == SOFT:
                    pe.wait_ge(rhoT_ready, st.at(1, 1))
                    if st.const:
                        pe.wait_ge(score_ready, st.at(1, 0))
                    else:
                        pe.wait_ge(feat_ready, 1)
                    for t in range(NT):
                        last = turn(psF[:, 0, t * P:(t + 1) * P], rhoT[:, t * P:(t + 1) * P])
                    last.then_inc(rho_ps, 1)
                if i == LN2T:
                    if st.half == 0:
                        pe.wait_ge(kv_hi, st.batch_at(9, 9))
                    elif st.const < STEPS - 1:
                        pe.wait_ge(feat_ready, st.at(1, 2))
                    pe.wait_ge(xn_ready, st.at(3, 1))
                    transpose_x(xT_ps)
                if i == LIN:
                    pe.wait_ge(lo_ready, st.at(6, 2))
                    for t in range(NT):
                        last = product(psF[:, t // 2, t % 2 * D:t % 2 * D + D],
                                       [(xT_hi[:, k, t * P:(t + 1) * P], xT_lo[:, k, t * P:(t + 1) * P],
                                         W1h[:, k, :], W1l[:, k, :]) for k in range(KC)])
                        if t % 2:
                            last.then_inc(lin_ps, 1)
                if i == LN3T:
                    pe.wait_ge(xn_ready, st.at(3, 2))
                    transpose_x(xT_ps)
                if i == QPROJ:
                    pe.wait_ge(lo_ready, st.at(6, 4))
                    for c in range(KC):
                        product(psF[:, c], [(Wqh[:, k, c * P:(c + 1) * P], Wql[:, k, c * P:(c + 1) * P],
                                             xT_hi[:, k], xT_lo[:, k]) for k in range(KC)]).then_inc(q_ps, 1)
                for u in range(8):
                    if i == PEAK_SLOTS[u]:
                        t, c = u // 2, u % 2
                        if u == 0:
                            pe.wait_ge(q_lo, st.at(2, 2))
                            if st.half == 0:
                                pe.wait_ge(kv_lo, st.batch_at(9, 9))
                        else:
                            pe.wait_ge(peak_used, st.at(8, u))
                        for hf in range(2):
                            last = pe.matmul(psF[:, hf, 0:PH], qT_hi[:, c, t * P:(t + 1) * P],
                                             K_hi[:, c, hf * PH:(hf + 1) * PH], start=True, stop=True)
                        last.then_inc(peak_ps, 1)
                if i == PEAKT:
                    pe.wait_ge(peak_used, st.at(8, 8))
                    for t in range(NT):
                        last = pe.transpose(psF[0:32, 0, t * P:(t + 1) * P], peak[:, t, :], ident[:, :])
                    last.then_inc(peakT_ps, 1)
                for m in range(2 * PCH):
                    if i == SCORE_SLOTS[m]:
                        c, k, rows = m // PCH, m % PCH, ROWS[m % PCH]
                        if m == 0:
                            pe.wait_ge(peakT_ready, st.at(1, 1))
                        elif k == 0:
                            pe.wait_ge(o_ready, st.at(2, 1))
                        elif k >= 2:
                            pe.wait_ge(p_ready, st.at(2 * PCH, m - 1))
                        dst = psF[0:rows, k % 2]
                        cut = slice(k * P, k * P + rows)
                        pe.matmul(dst, K_hi[:, c, cut], qT_hi[:, c], start=True, stop=False)
                        pe.matmul(dst, K_hi[:, c, cut], qT_lo[:, c], start=False, stop=False)
                        pe.matmul(dst, K_lo[:, c, cut], qT_hi[:, c], start=False, stop=False)
                        pe.matmul(dst, head_sel[:, c].rearrange("p h t -> p (h t)")[:, cut], peakT[:, :],
                                  start=False, stop=True).then_inc(sc_ps, 1)
                if i in PV:
                    c = PV.index(i)
                    pe.wait_ge(p_lo_ready, st.at(2 * PCH, PCH * (c + 1)))
                    for k in range(PCH):
                        rows, m, dst = ROWS[k], k, psF[:, 0]
                        pe.matmul(dst, V_hi[0:rows, k, c], p_hi[0:rows, m], start=k == 0, stop=False)
                        pe.matmul(dst, V_hi[0:rows, k, c], p_lo[0:rows, m], start=False, stop=False)
                        pe.matmul(dst, V_lo[0:rows, k, c], p_hi[0:rows, m], start=False, stop=k == PCH - 1)
                    for k in range(PCH):
                        rows, m = ROWS[k], k
                        ones = pair_mask[0:rows, k].rearrange("p h d -> p (h d)")
                        pe.matmul(psF[:, 1], ones, p_hi[0:rows, m], start=k == 0, stop=False)
                        last = pe.matmul(psF[:, 1], ones, p_lo[0:rows, m], start=False, stop=k == PCH - 1)
                    last.then_inc(pv_ps, 1)
                if i == WO:
                    pe.wait_ge(o_lo, st.at(2, 2))
                    for t in range(NT):
                        last = product(psF[:, t // 2, t % 2 * D:t % 2 * D + D],
                                       [(xT_hi[:, k, t * P:(t + 1) * P], xT_lo[:, k, t * P:(t + 1) * P],
                                         Woh[:, k, :], Wol[:, k, :]) for k in range(KC)])
                        if t % 2:
                            last.then_inc(wo_ps, 1)
                if i == LN4T:
                    pe.wait_ge(xn_ready, st.at(3, 3))
                    transpose_x(xT_ps)
                if i == ROUTE:
                    pe.wait_ge(lo_ready, st.at(6, 6))
                    for t in range(NT):
                        last = product(psF[:, 0, t * E:(t + 1) * E],
                                       [(eT_hi[:, st.half, k, t * P:(t + 1) * P], eT_lo[:, st.half, k, t * P:(t + 1) * P],
                                         RWh[:, k, :], RWl[:, k, :]) for k in range(KC)])
                    last.then_inc(logit_ps, 1)

            run(pe, slot)
            for e, hf in last_halves:
                down_half(Step(STEPS - 1), e, hf)

        @block.scalar
        def _(act):
            act.wait_ge(rows_loaded, 128)
            act.activation(gains[:, :], gains[:, :], ACT.Tanh).then_inc(setup_act, 1)

            def high_half(dst, ready, per, n, st, done):
                for c in range(KC):
                    act.wait_ge(ready, st.at(per, 2 * n + c + 1))
                    act.copy(dst[:, c], psF[:, c]).then_inc(done, 1)

            def scan(i, st):
                for s in range(SETS):
                    if i == TANH_SLOTS[s]:
                        g, c = s // 2, s % 2
                        if s == 0:
                            act.wait_ge(feat_ready, st.at(1, 1))
                            if st.const == 0:
                                act.wait_ge(setup_dve, 5)
                        js = range(min(4, TXT - 4 * g))
                        if s >= 2:
                            act.wait_ge(rho_part, st.at(SETS, s - 1))
                        for j in js:
                            n = 8 * g + c * len(js) + j
                            act.activation(tanh_tiles[:, n % HRING], feat[:, c], ACT.Tanh,
                                           bias=text_now[:, c, 4 * g + j:4 * g + j + 1]).then_inc(h_ready, 1)

            def slot(i, sc, st, ex):
                if sc:
                    scan(i, sc)
                if ex:
                    if i % 3 > 0:
                        q = 2 * (i // 3) + i % 3 - 1
                        act.wait_ge(g_done, ex.at(HID, q + 1))
                        if q >= 4 or ex.const:
                            act.wait_ge(y_ps, ex.at(HID, 2 * (q // 2) - 2))
                        else:
                            act.wait_ge(down_stored[q], 32 * len(range(q, EX, 4)))
                        act.copy(hid_hi[:, q % 4], tile3[:, q % 3]).then_inc(ghi_done, 1)
                    if i % 3 < 2:
                        q = 2 * (i // 3) + i % 3
                        act.wait_ge(gu_ps, ex.at(HID, q + 1))
                        if q >= 3 or ex.const:
                            act.wait_ge(glo_done, ex.at(HID, q - 2))
                        else:
                            act.wait_ge(split_done, len(staged))
                        act.activation(tile3[:, q % 3], psG[:, q % 2], ACT.Tanh, scale=0.5).then_inc(tanh_done, 1)
                if sc and i == LN1T:
                    high_half(xT_hi, xT_scan, 2, 0, sc, hi_scan)
                if st is None:
                    return
                if i == SOFT + 1:
                    act.wait_ge(sm_sub, st.at(1, 1))
                    act.activation(sm[:, 2], sm[:, 1], ACT.Exp).then_inc(sm_exp, 1)
                if i == FILM:
                    act.wait_ge(film_in, st.at(1, 1))
                    for n in range(2):
                        last = act.activation(film[:, n], film[:, n], ACT.Tanh, bias=bc_row[:, n:n + 1])
                    last.then_inc(film_ready, 1)
                if i == LN2T:
                    high_half(xT_hi, xT_ps, 6, 0, st, hi_ready)
                if i == LN3T:
                    high_half(xT_hi, xT_ps, 6, 1, st, hi_ready)
                if i == QPROJ:
                    for c in range(KC):
                        act.wait_ge(q32_ready, st.at(2, c + 1))
                        act.copy(qT_hi[:, c], xn_t[:, c]).then_inc(q_hi, 1)
                if i == PEAKT:
                    act.wait_ge(peakT_ps, st.at(1, 1))
                    act.mul(peakT[0:32, :], psF[0:32, 0], -1.0).then_inc(peakT_ready, 1)
                for m in range(2 * PCH):
                    if i == SCORE_SLOTS[m]:
                        k, rows = m % PCH, ROWS[m % PCH]
                        act.wait_ge(sc_ps, st.at(2 * PCH, m + 1))
                        if m >= 2:
                            act.wait_ge(p_lo_ready, st.at(2 * PCH, m - 1))
                        act.activation(p32[0:rows, m % 2], psF[0:rows, k % 2], ACT.Exp).then_inc(p_ready, 1)
                if i - 1 in PV:
                    c = PV.index(i - 1)
                    act.wait_ge(o_ready, st.at(2, c + 1))
                    act.copy(xT_hi[:, c], xn_t[:, c]).then_inc(o_hi, 1)
                if i == LN4T:
                    if st.const >= 2:
                        act.wait_ge(gu_ps, st.at(HID, -HID))
                    high_half(eT_hi[:, st.half], xT_ps, 6, 2, st, hi_ready)
                if i == ROUTE:
                    act.wait_ge(logit_ps, st.at(1, 1))
                    act.activation(rs[:, 0], psF[:, 0, 0:NT * E].rearrange("p (t e) -> p t e", t=NT), ACT.Tanh,
                                   scale=0.5).then_inc(score_ready, 1)

            run(act, slot)

        @block.vector
        def _(dve):
            su = Chain(dve, setup_chain)
            su.begin(lambda per, k: k)
            fr = Chain(dve, front_chain)
            sn = Chain(dve, scan_chain)
            kv = Chain(dve, kv_chain)

            def split(ch, hi, lo, src):
                ch.link(dve.tensor_copy(hi, src))
                return dve.tensor_tensor(lo, src, hi, ALU.subtract)

            su.link(dve.memset(coef_w[:, :, :], 0.0))
            su.link(dve.memset(coef_b[:, :, :], 0.0))
            su.link(dve.memset(text_mask[:, :, :], -3e38))
            dve.wait_ge(setup_pe, 1)
            su.link(dve.tensor_copy(ctxT, psG[:, :, 0:B * TXT]))
            split(su, ctxT_hi[:, :, :], ctxT_lo[:, :, :], ctxT).then_inc(setup_dve, 1)
            dve.wait_ge(setup_pe, 2)
            dve.wait_ge(text_loaded, 64)
            for c in range(KC):
                last = dve.tensor_scalar(text_bias[:, c, :], psU[:, c, 0:B * TXT], bcol[:, c:c + 1], None, ALU.add)
            last.then_inc(setup_dve, 1)

            def by_slot(dst, src, op):
                whole = TXT // 4
                d = dst.rearrange("p (j i) -> p i j", j=4)
                op(d[:, 0:whole, :], src[:, 0:4 * whole].rearrange("p (i j) -> p i j", j=4))
                su.link(op(d[:, whole, 0:TXT - 4 * whole], src[:, 4 * whole:TXT]))

            dve.wait_ge(setup_pe, 3)
            dve.wait_ge(wc_loaded, 80)
            for b in range(B):
                for n, dst in enumerate((coef_w, coef_b)):
                    by_slot(dst[:, b], psG[:, n, b * TXT:(b + 1) * TXT], lambda d, s: dve.tensor_copy(d, s))
                by_slot(text_mask[:, b], mask_int[:, b],
                        lambda d, s: dve.tensor_scalar(d, s, 1.0, -NEG, ALU.subtract, ALU.mult))
            dve.wait_ge(setup_pe, 4)
            dve.tensor_copy(up_auxT[0:50, :], psY[0:50, 0, :])
            split(su, RWh[:, :, :], RWl[:, :, :], psY[:, 1, 128:128 + KC * E].rearrange("p (k e) -> p k e", k=KC))
            dve.tensor_copy(lora1[0:4, :], psF[0:4, 2, 0:D]).then_inc(setup_dve, 1)
            dve.wait_ge(setup_pe, 5)
            dve.tensor_copy(lora2[0:50, :], psF[0:50, 2, 0:D]).then_inc(setup_dve, 1)
            for n, (hi, lo) in ((0, (W0h, W0l)), (2, (Wkh, Wkl)), (3, (Wvh, Wvl)), (4, (Wqh, Wql)), (5, (Woh, Wol))):
                dve.wait_ge(small_loaded[n], 16)
                split(su, hi[:, :, :], lo[:, :, :], small_stage[n].rearrange("p (k d) -> p k d", k=KC))
            dve.wait_ge(setup_pe, 6)
            split(su, W1h[:, :, :], W1l[:, :, :], psU[:, :, 0:D]).then_inc(setup_dve, 1)
            dve.wait_ge(setup_act, 1)
            dve.wait_ge(rows_loaded, 128)
            dve.tensor_scalar(b1_row[:, :], b1_row[:, :], gains[:, 2:3], None, ALU.mult)
            dve.tensor_scalar(bo_row[:, :], bo_row[:, :], gains[:, 1:2], None, ALU.mult)
            dve.tensor_scalar(bq[:, :], bq[:, :], float(DH) ** -0.5, None, ALU.mult)
            su.link(dve.memset(combine[:, :, :, E:EX], 0.5))
            su.link(dve.tensor_scalar(combine[:, :, :, E:EX], combine[:, :, :, E:EX], gains[:, 3:4], None, ALU.mult))
            dve.wait_ge(consts, 8)

            def split_expert(n):
                e, what = staged[n]
                dve.wait_ge(stage_loaded[n % 3], 16 * (n // 3 + 1))
                if what == "down":
                    if e >= 4:
                        dve.wait_ge(down_stored[e % 4], 32 * (e // 4))
                    hi, lo, src = hid_hi[:, e % 4], hid_lo[:, e % 4], stage[n % 3]
                else:
                    hi, lo = (gate_hi, gate_lo) if what == "gate" else (up_hi, up_lo)
                    hi, lo, src = hi[:, e], lo[:, e], stage[n % 3].rearrange("p (k d) -> p k d", k=KC)
                split(su, hi, lo, src).then_inc(split_done, 1)

            def moments(ch, src, norm):
                mean, rstd = norm[:, 0], norm[:, 1]
                for t in range(NT):
                    last = dve.bn_stats(stats[:, t, :], src[:, t, :])
                ch.link(last)
                dve.tensor_tensor(mean, stats[:, :, 1], stats[:, :, 4], ALU.add)
                dve.tensor_tensor(dif[:, :], stats[:, :, 1], stats[:, :, 4], ALU.subtract)
                ch.link(dve.tensor_tensor(veps[:, :], stats[:, :, 2], stats[:, :, 5], ALU.add))
                dve.tensor_scalar(mean, mean, 0.5, None, ALU.mult)
                dve.tensor_tensor(dif[:, :], dif[:, :], dif[:, :], ALU.mult)
                ch.link(dve.tensor_scalar(veps[:, :], veps[:, :], 1.0 / D, EPS, ALU.mult, ALU.add))
                ch.link(dve.scalar_tensor_tensor(out=veps[:, :], in0=dif[:, :], scalar=0.25, in1=veps[:, :],
                                                 op0=ALU.mult, op1=ALU.add))
                ch.link(dve.tensor_scalar(rstd.bitcast(I32), veps[:, :].bitcast(I32), -0.5, 1597463007.0,
                                          ALU.mult, ALU.add))
                for _ in range(3):
                    ch.link(dve.tensor_tensor(nwt[:, :], rstd, rstd, ALU.mult))
                    ch.link(dve.scalar_tensor_tensor(out=nwt[:, :], in0=nwt[:, :], scalar=-0.5, in1=veps[:, :],
                                                     op0=ALU.mult, op1=ALU.mult))
                    ch.link(dve.scalar_tensor_tensor(out=rstd, in0=nwt[:, :], scalar=1.5, in1=rstd,
                                                     op0=ALU.add, op1=ALU.mult))

            def normalise(src, norm, done):
                for t in range(NT):
                    last = dve.tensor_scalar(xn[:, t, :], src[:, t, :], norm[:, 0, t:t + 1], norm[:, 1, t:t + 1],
                                             ALU.subtract, ALU.mult)
                last.then_inc(done, 1)

            def low_half(hi, lo, ready, per, n, st, done):
                for c in range(KC):
                    dve.wait_ge(ready, st.at(per, 2 * n + c + 1))
                    dve.tensor_tensor(lo[:, c], psF[:, c], hi[:, c], ALU.subtract).then_inc(done, 1)

            def compare(v, n, a_, b_):
                mine = v.unsqueeze(3).to_broadcast([P, NT, n, n])
                theirs = v.unsqueeze(2).to_broadcast([P, NT, n, n])
                low = lower[:, 0:n, 0:n].unsqueeze(1).to_broadcast([P, NT, n, n])
                dve.tensor_tensor(a_, theirs, mine, ALU.is_gt)
                fr.link(dve.tensor_tensor(b_, theirs, mine, ALU.is_equal))
                fr.link(dve.tensor_tensor(b_, b_, low, ALU.mult))

            def count(dst, a_, b_):
                fr.link(dve.tensor_tensor(a_, a_, b_, ALU.add))
                fr.link(dve.tensor_reduce(dst, a_, AX, ALU.add))

            def route(part, st):
                score, biased = rs[:, 1], rs[:, 2]
                by = biased.rearrange("p t (g n) -> p t g n", g=NG)
                if part == 0:
                    dve.wait_ge(score_ready, st.at(1, 1))
                    fr.link(dve.tensor_scalar(score, rs[:, 0], 0.5, 0.5, ALU.mult, ALU.add))
                    fr.link(dve.tensor_tensor(biased, score, rbias[:, :].unsqueeze(1).to_broadcast([P, NT, E]), ALU.add))
                    group_part(by)
                if part == 1:
                    compare(rs[:, 6], E, rank_a, rank_b)
                if part == 2:
                    count(rs[:, 7], rank_a, rank_b)
                if part == 3:
                    choose(st, score)

            def group_part(by):
                q4 = [rs[:, 3, :, 4 * n:4 * n + 4] for n in range(4)]
                dve.tensor_tensor(q4[0], by[:, :, :, 0], by[:, :, :, 1], ALU.max)
                dve.tensor_tensor(q4[1], by[:, :, :, 0], by[:, :, :, 1], ALU.min)
                dve.tensor_tensor(q4[2], by[:, :, :, 2], by[:, :, :, 3], ALU.max)
                fr.link(dve.tensor_tensor(q4[3], by[:, :, :, 2], by[:, :, :, 3], ALU.min))
                top, mid, rest_, second = [rs[:, 4, :, 4 * n:4 * n + 4] for n in range(4)]
                dve.tensor_tensor(top, q4[0], q4[2], ALU.max)
                dve.tensor_tensor(mid, q4[0], q4[2], ALU.min)
                fr.link(dve.tensor_tensor(rest_, q4[1], q4[3], ALU.max))
                fr.link(dve.tensor_tensor(second, mid, rest_, ALU.max))
                gscore, grank, chosen, off = [rs[:, 5, :, 4 * n:4 * n + 4] for n in range(4)]
                fr.link(dve.tensor_tensor(gscore, top, second, ALU.add))
                a4, b4 = (work[:, n:n + NT * NG * NG].rearrange("p (t e f) -> p t e f", t=NT, e=NG) for n in (0, 1024))
                compare(gscore, NG, a4, b4)
                count(grank, a4, b4)
                fr.link(dve.tensor_scalar(chosen, grank, float(TOPG), None, ALU.is_lt))
                fr.link(dve.tensor_scalar(off, chosen, 1.0, None, ALU.subtract))
                masked = rs[:, 6].rearrange("p t (g n) -> p t g n", g=NG)
                fr.link(dve.tensor_tensor(masked, by, chosen.unsqueeze(3).to_broadcast([P, NT, NG, EPG]), ALU.mult))
                fr.link(dve.tensor_tensor(masked, masked, off.unsqueeze(3).to_broadcast([P, NT, NG, EPG]), ALU.add))

            def choose(st, score):
                fr.link(dve.tensor_scalar(rs[:, 8], rs[:, 7], float(TOPK), None, ALU.is_lt))
                fr.link(dve.tensor_tensor(rs[:, 9], rs[:, 8], score, ALU.mult))
                total, inv = rs[:, 10, :, 0], rs[:, 10, :, 1]
                fr.link(dve.tensor_reduce(total, rs[:, 9], AX, ALU.add))
                fr.link(dve.tensor_scalar(total, total, 1e-20, None, ALU.add))
                fr.link(dve.reciprocal(inv, total))
                fr.link(dve.tensor_scalar(inv, inv, 0.5 * SCALE, gains[:, 3:4], ALU.mult, ALU.mult))
                dve.tensor_tensor(combine[:, st.half, :, 0:E], rs[:, 9],
                                  inv.unsqueeze(2).to_broadcast([P, NT, E]), ALU.mult).then_inc(routed, 1)

            def add_y(ex, e, hf):
                dve.wait_ge(y_ps, ex.at(HID, 2 * e + hf + 1))
                if e:
                    dve.wait_ge(y_used, ex.at(HID, 2 * (e - 1) + hf + 1))
                for t in (2 * hf, 2 * hf + 1):
                    xt = x[:, ex.half, t]
                    last = dve.scalar_tensor_tensor(out=xt, in0=psY[:, t % 2], scalar=combine[:, ex.half, t, e:e + 1],
                                                    in1=xt, op0=ALU.mult, op1=ALU.add)
                last.then_inc(y_used, 1)

            def scan(i, st):
                if i == 0:
                    sn.begin(st.at)
                if i == LN1:
                    sn.link(dve.tensor_copy(text_now[:, :, :], text_bias[:, :, bass.ds(st.batch() * TXT, TXT)]))
                    dve.wait_ge(xscan_loaded, st.at(16, 16))
                    moments(sn, xscan, scan_norm[:, st.half])
                if i == LN1 + 1:
                    normalise(xscan, scan_norm[:, st.half], xn_scan)
                if i == LN1T:
                    low_half(xT_hi, xT_lo, hi_scan, 2, 0, st, lo_scan)
                if i == FEAT:
                    dve.wait_ge(feat_ps, st.at(1, 1))
                    dve.tensor_copy(feat, psF[:, 0:KC]).then_inc(feat_ready, 1)
                if st.const == 0:
                    for n in range(len(staged) * i // SLOTS, len(staged) * (i + 1) // SLOTS):
                        split_expert(n)
                if i == SLOTS - 1:
                    sn.end()

            def slot(i, sc, st, ex):
                if ex:
                    e, k = i // 3, i % 3
                    due = halves_at(ex, i)
                    if due:
                        add_y(*due)
                    if k < 2:
                        q = 2 * e + k
                        dve.wait_ge(tanh_done, ex.at(HID, q + 1))
                        dve.scalar_tensor_tensor(out=tile3[:, q % 3], in0=tile3[:, q % 3], scalar=1.0, in1=psG[:, k],
                                                 op0=ALU.add, op1=ALU.mult).then_inc(v_done, 1)
                        dve.wait_ge(v_done, ex.at(HID, q + 1))
                        dve.tensor_tensor(tile3[:, q % 3], tile3[:, q % 3], psU[:, k], ALU.mult).then_inc(g_done, 1)
                if st and i == 0:
                    fr.begin(st.at)
                    dve.wait_ge(rho_part, st.at(SETS, SETS))
                    dve.tensor_copy(rhoT, psF[:, RHO]).then_inc(rhoT_ready, 1)
                if sc:
                    scan(i, sc)
                if st is None:
                    return
                xs = x[:, st.half]
                if st.half == 0 and i == KV - 2:
                    kv.begin(st.batch_at)
                    t0 = st.batch() * TXT
                    for dst, src in ((ctx8_hi, ctxT_hi), (ctx8_lo, ctxT_lo)):
                        for k2 in range(KC):
                            s = src[:, k2, bass.ds(t0, TXT)].unsqueeze(1).to_broadcast([P, HC, TXT])
                            last = dve.tensor_copy(dst[:, k2], s)
                    last.then_inc(ctx8_ready, 1)
                if st.half == 0 and KV <= i < KV + KVN:
                    for n in range(2 * (i - KV), min(2 * (i - KV + 1), 9)):
                        lo, hi, tmp = kv_parts(n)
                        dve.wait_ge(kv_ps, st.batch_at(9, n + 1))
                        if n >= 2:
                            dve.wait_ge(kv_lo, st.batch_at(9, n - 1))
                        if n < 4:
                            c, hf = n // 2, n % 2
                            mask = head_mask[:, HC // 2 * hf:HC // 2 * (hf + 1)].rearrange("p h t -> p (h t)")
                            kv.link(dve.scalar_tensor_tensor(out=tmp, in0=psF[:, n % 2, 0:PH], scalar=bk[:, c:c + 1], in1=mask,
                                                             op0=ALU.add, op1=ALU.mult))
                        else:
                            m, rows = n - 4, ROWS[n - 4]
                            kv.link(dve.tensor_tensor(kv32[0:rows, n % 2, 0:D], psF[0:rows, n % 2, 0:D], bv_row[0:rows, :],
                                                      ALU.add))
                            mask = pair_mask[0:rows, m].rearrange("p h d -> p (h d)").unsqueeze(1).to_broadcast([rows, KC, P])
                            kv.link(dve.tensor_tensor(tmp, tmp, mask, ALU.mult))
                        dve.tensor_copy(hi, tmp).then_inc(kv_hi, 1)
                    if i == KV + KVN - 1:
                        kv.end()
                b = st.batch()
                if i == SOFT:
                    dve.wait_ge(rho_ps, st.at(1, 1))
                    rho = psF[:, 0].rearrange("p (t j i) -> p t j i", t=NT, j=4)[:, :, :, 0:GRP]
                    mask = text_mask[:, bass.ds(b, 1), :].rearrange("p b (j i) -> p b j i", j=4).to_broadcast([P, NT, 4, GRP])
                    fr.link(dve.tensor_tensor(sm[:, 0].rearrange("p t (j i) -> p t j i", j=4), rho, mask, ALU.add))
                    fr.link(dve.tensor_reduce(smax[:, :], sm[:, 0], AX, ALU.max))
                    dve.tensor_tensor(sm[:, 1], sm[:, 0], smax[:, :].unsqueeze(2).to_broadcast([P, NT, SL]),
                                      ALU.subtract).then_inc(sm_sub, 1)
                if i == SOFT + 1:
                    dve.wait_ge(sm_exp, st.at(1, 1))
                    dve.tensor_reduce(sden[:, :], sm[:, 2], AX, ALU.add)
                    for n, coef in enumerate((coef_w, coef_b)):
                        cf = coef[:, bass.ds(b, 1), :].to_broadcast([P, NT, SL])
                        fr.link(dve.tensor_tensor(sm[:, n], sm[:, 2], cf, ALU.mult))
                        fr.link(dve.tensor_reduce(snum[:, n], sm[:, n], AX, ALU.add))
                    fr.link(dve.reciprocal(sden[:, :], sden[:, :]))
                    dve.tensor_tensor(film[:, :, :], snum[:, :, :], sden[:, :].unsqueeze(1).to_broadcast([P, 2, NT]),
                                      ALU.mult).then_inc(film_in, 1)
                if i == FILM:
                    dve.wait_ge(film_ready, st.at(1, 1))
                    mean, rstd = scan_norm[:, st.half, 0], scan_norm[:, st.half, 1]
                    fr.link(dve.tensor_scalar(film[:, :, :], film[:, :, :], gains[:, 0:1], None, ALU.mult))
                    fr.link(dve.tensor_tensor(film[:, 0], film[:, 0], rstd, ALU.mult))
                    fr.link(dve.tensor_tensor(nwt[:, :], film[:, 0], mean, ALU.mult))
                    dve.tensor_scalar(film[:, 0], film[:, 0], 1.0, None, ALU.add)
                    fr.link(dve.tensor_tensor(film[:, 1], film[:, 1], nwt[:, :], ALU.subtract))
                if i == X1:
                    dve.wait_ge(x_loaded, st.at(16, 16))
                    if st.const >= 2:
                        dve.wait_ge(stored[st.half], st.batch_at(16, 0))
                    for t in range(NT):
                        last = dve.tensor_scalar(xs[:, t], xin[:, t], film[:, 0, t:t + 1], film[:, 1, t:t + 1],
                                                 ALU.mult, ALU.add)
                    fr.link(last)
                for first in (LN2, LN3, LN4):
                    if i == first:
                        moments(fr, xs, norm)
                    if i == first + 1:
                        normalise(xs, norm, xn_ready)
                if i == LN2T:
                    low_half(xT_hi, xT_lo, hi_ready, 6, 0, st, lo_ready)
                    fr.link(dve.tensor_tensor(xs, xs, b1_row[:, :].unsqueeze(1).to_broadcast([P, NT, D]), ALU.add))
                if i == LIN:
                    for j in range(2):
                        dve.wait_ge(lin_ps, st.at(2, j + 1))
                        xj = xs[:, 2 * j:2 * j + 2].rearrange("p t d -> p (t d)")
                        last = dve.scalar_tensor_tensor(out=xj, in0=psF[:, j], scalar=gains[:, 2:3], in1=xj,
                                                        op0=ALU.mult, op1=ALU.add)
                    fr.link(last)
                if i == LN3T:
                    low_half(xT_hi, xT_lo, hi_ready, 6, 1, st, lo_ready)
                if i == QPROJ:
                    for c in range(KC):
                        dve.wait_ge(q_ps, st.at(2, c + 1))
                        dve.tensor_scalar(xn_t[:, c], psF[:, c], float(DH) ** -0.5, bq[:, c:c + 1], ALU.mult,
                                          ALU.add).then_inc(q32_ready, 1)
                    for c in range(KC):
                        dve.wait_ge(q_hi, st.at(2, c + 1))
                        dve.tensor_tensor(qT_lo[:, c], xn_t[:, c], qT_hi[:, c], ALU.subtract).then_inc(q_lo, 1)
                for u in range(8):
                    if i == PEAK_SLOTS[u]:
                        dve.wait_ge(peak_ps, st.at(8, u + 1))
                        dve.tensor_reduce(peak[:, u // 2, HC * (u % 2):HC * (u % 2 + 1)].rearrange("p (b h) -> p b h", b=2),
                                          psF[:, 0:2, 0:PH].rearrange("p b (h t) -> p b h t", t=TXT), AX,
                                          ALU.max).then_inc(peak_used, 1)
                if i == PEAKT:
                    fr.link(dve.tensor_tensor(xs, xs, bo_row[:, :].unsqueeze(1).to_broadcast([P, NT, D]), ALU.add))
                for m in range(2 * PCH):
                    if i == SCORE_SLOTS[m]:
                        k, rows = m % PCH, ROWS[m % PCH]
                        dve.wait_ge(p_ready, st.at(2 * PCH, m + 1))
                        dve.tensor_copy(p_hi[0:rows, k], p32[0:rows, m % 2]).then_inc(p_hi_ready, 1)
                if i in PV:
                    c = PV.index(i)
                    dve.wait_ge(pv_ps, st.at(2, c + 1))
                    fr.link(dve.reciprocal(xn_t[:, c], psF[:, 1]))
                if i - 1 in PV:
                    c = PV.index(i - 1)
                    dve.tensor_tensor(xn_t[:, c], xn_t[:, c], psF[:, 0], ALU.mult).then_inc(o_ready, 1)
                    dve.wait_ge(o_hi, st.at(2, c + 1))
                    dve.tensor_tensor(xT_lo[:, c], xn_t[:, c], xT_hi[:, c], ALU.subtract).then_inc(o_lo, 1)
                if i == WO:
                    for j in range(2):
                        dve.wait_ge(wo_ps, st.at(2, j + 1))
                        xj = xs[:, 2 * j:2 * j + 2].rearrange("p t d -> p (t d)")
                        last = dve.scalar_tensor_tensor(out=xj, in0=psF[:, j], scalar=gains[:, 1:2], in1=xj,
                                                        op0=ALU.mult, op1=ALU.add)
                    fr.link(last)
                if i == LN4T:
                    low_half(eT_hi[:, st.half], eT_lo[:, st.half], hi_ready, 6, 2, st, lo_ready)
                if ROUTE <= i < SLOTS:
                    route(i - ROUTE, st)
                if i == SLOTS - 1:
                    fr.end()

            run(dve, slot)
            for e, hf in last_halves:
                add_y(Step(STEPS - 1), e, hf)


INPUTS = ["x", "ctx_1024", "mask_BxS2_ik0", "g_xattn", "g_ffn",
          "L0_xattn_Ws", "L0_xattn_W", "L0_xattn_w", "L0_xattn_b", "L0_xattn_Wcw", "L0_xattn_bcw",
          "L0_xattn_Wcb", "L0_xattn_bcb", "L0_ffn_W", "L0_ffn_b", "L0_ffn_lora_down", "L0_ffn_lora_up",
          "L0_ffn_down_aux", "L0_ffn_up_aux", "L1_xattn_Wq", "L1_xattn_bq", "L1_xattn_Wk", "L1_xattn_bk",
          "L1_xattn_Wv", "L1_xattn_bv", "L1_xattn_Wo", "L1_xattn_bo", "L1_ffn_router_w", "L1_ffn_bias",
          "L1_ffn_gate_w", "L1_ffn_up_w", "L1_ffn_down_w", "L1_ffn_sh_gate_w", "L1_ffn_sh_up_w",
          "L1_ffn_sh_down_w"]


def kernel(**inputs):
    import concourse.bacc as bacc
    from concourse.bass_utils import run_bass_kernel_spmd

    nc = bacc.Bacc("TRN2", target_bir_lowering=False, num_devices=1)
    arrays, args = {}, {}
    for name in INPUTS:
        v = np.ascontiguousarray(inputs[name])
        arrays[f"in_{name}"] = v
        args[name] = nc.dram_tensor(f"in_{name}", v.shape, mybir.dt.from_np(v.dtype), kind="ExternalInput").ap()
    out = nc.dram_tensor("out_x", (B, S, D), F32, kind="ExternalOutput").ap()
    build(nc, args, out)
    r = run_bass_kernel_spmd(nc, [arrays], core_ids=[0])
    return r.results[0]["out_x"]
```

```python
from contextlib import ExitStack

import numpy as np
import concourse.bass as bass
from concourse import mybir

F32 = mybir.dt.float32
F16 = mybir.dt.float16
I32 = mybir.dt.int32
ALU = mybir.AluOpType
ACT = mybir.ActivationFunctionType
AX = mybir.AxisListType.X

P = 128
D = 256
KC = D // P
B, S, TXT = 4, 1024, 77
TOK = 512
NT = TOK // P
STEPS = B * S // TOK
HALVES = S // TOK
HEADS, DH = 16, 16
HC = P // DH
PAIRS = HC * TXT
PH = PAIRS // 2
PCH = -(-PAIRS // P)
ROWS = [min(P, PAIRS - P * k) for k in range(PCH)]
GRP = -(-TXT // 4)
SL = 4 * GRP
E, NG, EPG, TOPG, TOPK = 16, 4, 4, 2, 4
EX = E + 2
NEG = -1e30
SCALE = 2.5
EPS = 1e-5
HRING = 8
SETS = 2 * GRP

SLOTS = 3 * EX
SOFT, FILM, KV, KVN, X1, LN2, LN2T, LIN, LN3, LN3T, QPROJ, PEAK, PEAKT, SCORES, PV, OT, WO, LN4, LN4T, ROUTE = (
    1, 4, 6, 5, 8, 9, 12, 14, 15, 18, 20, 22, 30, (31, 36), (35, 41), 42, 44, 45, 48, 50)
PEAK_SLOTS = [PEAK + u for u in range(NT * KC)]
SCORE_SLOTS = [first + k // 2 for first in SCORES for k in range(PCH)]
ROUTE_SLOTS = [ROUTE, ROUTE + 2, ROUTE + 3]
CHOOSE = 3
NORM1, NORM1T, FEAT, COPY = 0, 3, 5, 6
PRELUDE = [48, 49, 51, 53, 53]
PRELUDE0 = [42, 43, 45, 47, 53]
PHASES = [NORM1, NORM1 + 1, NORM1T, FEAT, COPY]
BUSY = (LN2T, LN3T, QPROJ, SCORES[0], SCORES[0] + 1, SCORES[0] + 2, SCORES[1], SCORES[1] + 1, OT, LN4T, PRELUDE[2])
BUSY1 = (2, 5, LN2T, PEAK, PEAK + 2, PEAK + 4, PEAK + 6, SCORES[0], SCORES[0] + 1, SCORES[0] + 2, SCORES[1] + 1)
TANH_SLOTS, TANH_SLOTS1 = ([i for i in range(1, SLOTS - 2) if i not in busy][:SETS] for busy in (BUSY, BUSY1))
KV0 = 20


class Step:

    def __init__(self, const, r=None):
        self.const, self.r, self.half = const, r, const % HALVES

    def at(self, per, k):
        return self.const * per + k if self.r is None else self.r * (2 * per) + (self.const * per + k)

    def batch_at(self, per, k):
        return self.batch() * per + k if self.r is None else self.r * per + (self.const // 2 * per + k)

    def batch(self):
        return self.const // 2 if self.r is None else self.r + self.const // 2

    def index(self):
        return self.const if self.r is None else self.r * 2 + self.const


def tanh_slots(st):
    return TANH_SLOTS1 if st.const == 1 and st.r is None else TANH_SLOTS


def on_dve(last, st):
    return st.r is None and st.const <= last


def preludes(i, sc):
    if sc is None or (sc.const == STEPS - 1 and sc.r is None):
        return []
    slots = PRELUDE if sc.const or sc.r is not None else PRELUDE0
    return [(phase, Step(sc.const + 1, sc.r)) for phase, at in zip(PHASES, slots) if at == i]


class Chain:

    def __init__(self, eng, sem):
        self.eng, self.sem, self.n, self.per, self.at = eng, sem, 0, None, None

    def begin(self, at):
        self.at, self.n = at, 0

    def end(self):
        assert self.per in (None, self.n)
        self.per = self.n

    def link(self, ins):
        ins.then_inc(self.sem, 1)
        self.n += 1
        self.eng.wait_ge(self.sem, self.at(self.per or 0, self.n))


def build(nc, a, out):
    ctx = ExitStack()
    with ctx:
        ctx.enter_context(nc.allow_non_contiguous_dma(reason="small vectors and matrices, once"))

        def sb(name, shape, dt=F32):
            return ctx.enter_context(nc.sbuf_tensor(name, shape, dt))

        def sem(name):
            return ctx.enter_context(nc.semaphore(name))

        gate_hi, gate_lo, up_hi, up_lo = (sb(n, [P, EX, KC, D], F16) for n in
                                          ("gate_hi", "gate_lo", "up_hi", "up_lo"))
        down_dram = nc.dram_tensor("down_split", [EX, P, 2 * KC * D], F16, kind="Internal").ap()
        down = sb("down", [P, 3, 2, KC, D], F16)
        W0h, W0l, W1h, W1l, Wqh, Wql, Wkh, Wkl, Wvh, Wvl, Woh, Wol = (
            sb(n, [P, KC, D], F16) for n in ("W0h", "W0l", "W1h", "W1l", "Wqh", "Wql",
                                             "Wkh", "Wkl", "Wvh", "Wvl", "Woh", "Wol"))
        RWh, RWl = sb("RWh", [P, KC, E], F16), sb("RWl", [P, KC, E], F16)
        ident = sb("ident", [P, P])
        head_mask = sb("head_mask", [P, HC, TXT], F16)
        pair_mask = sb("pair_mask", [P, PCH, HC, DH], F16)
        head_sel = sb("head_sel", [P, KC, HC, TXT], F16)
        lower = sb("lower", [P, E, E], F16)
        text_bias = sb("text_bias", [P, KC, B * TXT])
        scan_norm = sb("scan_norm", [P, 2, 2, NT])
        text_now = sb("text_now", [P, KC, TXT])
        wcol = sb("wcol", [P, KC])
        wslide = sb("wslide", [P, KC, 63])
        coef_w, coef_b = sb("coef_w", [P, B, SL]), sb("coef_b", [P, B, SL])
        text_mask = sb("text_mask", [P, B, SL])
        ctxT_hi, ctxT_lo = sb("ctxT_hi", [P, KC, B * TXT], F16), sb("ctxT_lo", [P, KC, B * TXT], F16)
        gains = sb("gains", [P, 4])
        bcol = sb("bcol", [P, KC])
        bq, bk = sb("bq", [P, KC]), sb("bk", [P, KC])
        wc_cols = sb("wc_cols", [P, 2, KC])
        bc_row = sb("bc_row", [P, 2])
        b1_row, bo_row, bv_row = sb("b1_row", [P, D]), sb("bo_row", [P, D]), sb("bv_row", [P, D])
        rbias = sb("rbias", [P, E])
        x = sb("x", [P, 2, NT, D])
        xin = sb("xin", [P, NT, D])
        xscan = sb("xscan", [P, NT, D])
        feat = sb("feat", [P, KC, TOK])
        xn = sb("xn", [P, NT, D])
        xT_hi, xT_lo = sb("xT_hi", [P, KC, TOK], F16), sb("xT_lo", [P, KC, TOK], F16)
        eT_hi, eT_lo = sb("eT_hi", [P, 2, KC, TOK], F16), sb("eT_lo", [P, 2, KC, TOK], F16)
        stats, norm = sb("stats", [P, NT, 6]), sb("norm", [P, 2, NT])
        veps, dif, nwt = sb("veps", [P, NT]), sb("dif", [P, NT]), sb("nwt", [P, NT])
        K_hi, K_lo = sb("K_hi", [P, KC, PAIRS], F16), sb("K_lo", [P, KC, PAIRS], F16)
        V_hi = sb("V_hi", [P, PCH, KC, P + HC], F16)
        V_lo = sb("V_lo", [P, PCH, KC, P], F16)
        qT_hi, qT_lo = sb("qT_hi", [P, KC, TOK], F16), sb("qT_lo", [P, KC, TOK], F16)
        peak = sb("peak", [P, NT, 32])
        peakT = sb("peakT", [P, TOK], F16)
        inv = sb("inv", [P, KC, NT, HC])
        smax, sden, snum = sb("smax", [P, NT]), sb("sden", [P, NT]), sb("snum", [P, 2, NT])
        film = sb("film", [P, 2, NT])
        combine = sb("combine", [P, 2, NT, EX])
        tile3 = sb("tile3", [P, 3, TOK])
        hid_hi, hid_lo = sb("hid_hi", [P, 4, TOK], F16), sb("hid_lo", [P, 4, TOK], F16)
        tanh_tiles = sb("tanh_tiles", [P, HRING, TOK])
        work = sb("work", [P, 7 * TOK])
        x_flat = x[:, :, :, :].rearrange("p h t d -> p (h t d)")
        Ws = x_flat[:, 0:512].rearrange("p (k d) -> p k d", k=KC)
        ctx_rows = x_flat[:, 512:1536].rearrange("p (b d) -> p b d", b=B)
        ctxT = work[:, 0:KC * B * TXT].rearrange("p (k t) -> p k t", k=KC)
        o0 = KC * B * TXT
        mask_int = work[:, o0:o0 + B * TXT].bitcast(I32).rearrange("p (b t) -> p b t", b=B)
        o0 += B * TXT
        up_rows = work[:, o0:o0 + 100].rearrange("p (c u) -> p c u", c=2)
        lora_dT = work[:, o0 + 100:o0 + 104]
        lora_uT = work[:, o0 + 104:o0 + 154]
        down_aux = work[:, o0 + 154:o0 + 410]
        lora1 = work[:, o0 + 410:o0 + 666]
        lora2 = work[:, o0 + 666:o0 + 922]
        up_auxT = work[:, o0 + 922:o0 + 1178]
        rw_rows = work[:, o0 + 1178:o0 + 1434].rearrange("p (k d) -> p k d", k=KC)
        ctx8_hi = work[:, 0:PAIRS].bitcast(F16).rearrange("p (k h t) -> p k h t", k=KC, h=HC)
        ctx8_lo = work[:, PAIRS:2 * PAIRS].bitcast(F16).rearrange("p (k h t) -> p k h t", k=KC, h=HC)
        kv32 = work[:, 2 * PAIRS:2 * PAIRS + 1024].rearrange("p (r n) -> p r n", r=2)
        rhoT = work[:, 6 * TOK:7 * TOK]
        assert 3 * NT * SL <= 1024
        sm = work[:, 0:3 * NT * SL].rearrange("p (r t s) -> p r t s", r=3, t=NT)
        half = PCH * TOK // 2
        p_hi = work[:, 0:half].bitcast(F16).rearrange("p (m t) -> p m t", m=PCH)
        p_lo = work[:, half:2 * half].bitcast(F16).rearrange("p (m t) -> p m t", m=PCH)
        p32 = work[:, 2 * half:2 * half + 2 * TOK].rearrange("p (r t) -> p r t", r=2)
        rank_a = work[:, 1024:1536].bitcast(F16).rearrange("p (t e f) -> p t e f", t=NT, e=E)
        rank_b = work[:, 1536:2048].bitcast(F16).rearrange("p (t e f) -> p t e f", t=NT, e=E)
        rs = work[:, 2048:2048 + 11 * NT * E].rearrange("p (r t e) -> p r t e", r=11, t=NT)
        xn_t = xn[:, :, :].rearrange("p a b -> p (a b)").rearrange("p (c t) -> p c t", c=2)
        xn_o = xn[:, :, :].rearrange("p t (c h d) -> p c t h d", c=KC, h=HC)
        stage = [tile3[:, n, :] for n in range(3)]
        stage += [down[:, n].rearrange("p a b c -> p (a b c)").bitcast(F32) for n in range(3)]
        small_stage = [t[:, h].rearrange("p k t -> p (k t)").bitcast(F32) for t in (eT_hi, eT_lo) for h in range(2)]
        small_stage += [t[:, :, :].rearrange("p k t -> p (k t)").bitcast(F32) for t in (qT_hi, qT_lo)]
        RING = len(stage)
        down_tmp = [(hid_hi, hid_lo, n) for n in range(4)]

        psF = ctx.enter_context(nc.psum_tensor("psF", [P, 3, 512], F32))
        psG = ctx.enter_context(nc.psum_tensor("psG", [P, 2, 512], F32))
        psU = ctx.enter_context(nc.psum_tensor("psU", [P, 2, 512], F32))
        psY = ctx.enter_context(nc.psum_tensor("psY", [P, 2, D], F32))
        RHO = 2

        consts = sem("consts")
        x_loaded = sem("x_loaded")
        xscan_loaded = sem("xscan_loaded")
        stored = [sem("stored0"), sem("stored1")]
        text_loaded, wc_loaded, lora_loaded, rows_loaded = (
            sem(n) for n in ("text_loaded", "wc_loaded", "lora_loaded", "rows_loaded"))
        small_loaded = [sem(f"small_loaded{n}") for n in range(6)]
        stage_loaded = [sem(f"stage_loaded{n}") for n in range(RING)]
        split_done = sem("split_done")
        down_stored = [sem(f"down_stored{n}") for n in range(4)]
        setup_pe, setup_dve, setup_act, setup_chain, pool_chain = (
            sem(n) for n in ("setup_pe", "setup_dve", "setup_act", "setup_chain", "pool_chain"))
        ctx8_ready, kv_ps, kv_hi, kv_lo, kv_chain = (
            sem(n) for n in ("ctx8_ready", "kv_ps", "kv_hi", "kv_lo", "kv_chain"))
        xn_scan, xT_scan, hi_scan, lo_scan = (sem(n) for n in ("xn_scan", "xT_scan", "hi_scan", "lo_scan"))
        feat_ready = sem("feat_ready")
        scan_chain = sem("scan_chain")
        xn_ready = sem("xn_ready")
        xT_ps = sem("xT_ps")
        hi_ready = sem("hi_ready")
        lo_ready = sem("lo_ready")
        feat_ps = sem("feat_ps")
        h_ready = sem("h_ready")
        rho_part = sem("rho_part")
        rhoT_ready, rho_ps = sem("rhoT_ready"), sem("rho_ps")
        sm_sub, sm_exp = sem("sm_sub"), sem("sm_exp")
        film_in, film_ready = sem("film_in"), sem("film_ready")
        lin_ps = sem("lin_ps")
        q_ps, q32_ready, q_hi, q_lo = (sem(n) for n in ("q_ps", "q32_ready", "q_hi", "q_lo"))
        peak_ps, peak_used = sem("peak_ps"), sem("peak_used")
        peakT_ps, peakT_ready = sem("peakT_ps"), sem("peakT_ready")
        sc_ps, p_ready, p_hi_ready, p_lo_ready = (
            sem(n) for n in ("sc_ps", "p_ready", "p_hi_ready", "p_lo_ready"))
        pv_ps, o_ready = sem("pv_ps"), sem("o_ready")
        wo_ps = sem("wo_ps")
        logit_ps, score_ready = sem("logit_ps"), sem("score_ready")
        rank_chain = sem("rank_chain")
        compared, ranked = sem("compared"), sem("ranked")
        front_chain, route_chain = sem("front_chain"), sem("route_chain")
        gu_ps, tanh_done, v_done, g_done, ghi_done, glo_done = (
            sem(n) for n in ("gu_ps", "tanh_done", "v_done", "g_done", "ghi_done", "glo_done"))
        y_ps, y_used = sem("y_ps"), sem("y_used")
        down_loaded = [sem(f"down_loaded{n}") for n in range(3)]

        HID = 2 * EX
        xv = a["x"].rearrange("b (h t p) d -> (b h) p t d", h=HALVES, p=P)
        ov = out.rearrange("b (h t p) d -> (b h) p t d", h=HALVES, p=P)

        def w256(w):
            return w.rearrange("(k p) n -> p k n", p=P)

        def expert(e, what):
            if e < E:
                return w256(a[f"L1_ffn_{what}_w"][e])
            s = e - E
            if what == "down":
                return w256(a["L1_ffn_sh_down_w"][s * D:(s + 1) * D, :])
            return w256(a[f"L1_ffn_sh_{what}_w"][:, s * D:(s + 1) * D])

        staged = [(e, what) for e in range(EX) for what in ("gate", "up", "down")]

        def run(eng, prelude, slot):
            def side_by_side(sc, mi, ex):
                for i in range(SLOTS):
                    slot(i, sc, mi, ex)

            if prelude:
                for phase in PHASES:
                    prelude(phase, Step(0))
            side_by_side(Step(0), None, None)
            side_by_side(Step(1), Step(0), None)
            side_by_side(Step(2), Step(1), Step(0))
            with eng.Fori(0, STEPS // 2 - 2) as r:
                side_by_side(Step(3, r), Step(2, r), Step(1, r))
                side_by_side(Step(4, r), Step(3, r), Step(2, r))
            side_by_side(Step(STEPS - 1), Step(STEPS - 2), Step(STEPS - 3))
            side_by_side(None, Step(STEPS - 1), Step(STEPS - 2))
            side_by_side(None, None, Step(STEPS - 1))

        def earlier(ex, e):
            if e >= 0:
                return ex, e
            return (Step(ex.const - 1, ex.r), e + EX) if ex.const else None

        def halves_at(ex, i):
            e, k = i // 3, i % 3
            if k == 0:
                return None
            due = earlier(ex, e - 3 + k)
            return (*due, 2 - k) if due else None

        last_halves = [(EX - 2, 1), (EX - 1, 0), (EX - 1, 1)]

        def kv_stage(i, sc, st):
            if st is None:
                return (sc, i - KV0) if sc and sc.const == 0 else (None, 0)
            return (st, i - KV) if st.half == 0 and st.const else (None, 0)

        def kv_parts(n):
            if n < 4:
                c, cut = n // 2, slice(n % 2 * PH, (n % 2 + 1) * PH)
                return K_lo[:, c, cut], K_hi[:, c, cut], kv32[:, n % 2, 0:PH]
            m, rows = n - 4, ROWS[n - 4]
            return (V_lo[0:rows, m], V_hi[0:rows, m, :, 0:P],
                    kv32[0:rows, n % 2, 0:D].rearrange("p (c d) -> p c d", c=KC))

        block = ctx.enter_context(nc.Block())

        @block.sync
        def _(sp):
            def load_x(st):
                if st.const:
                    sp.wait_ge(xn_ready, st.at(3, -2))
                sp.dma_start(xin[:, :, :], xv[st.index()]).then_inc(x_loaded, 16)

            def load_scan(st):
                if st.const:
                    sp.wait_ge(xn_scan, st.at(1, 0))
                sp.dma_start(xscan[:, :, :], xv[st.index()]).then_inc(xscan_loaded, 16)

            load_scan(Step(0))
            sp.dma_start(ctx_rows[0:TXT], a["ctx_1024"].rearrange("b t d -> t b d")).then_inc(text_loaded, 16)
            sp.dma_start(Ws, w256(a["L0_xattn_Ws"])).then_inc(text_loaded, 16)
            sp.dma_start(wcol[:, :], a["L0_xattn_w"].rearrange("(k p) o -> p (k o)", p=P)).then_inc(text_loaded, 16)
            sp.dma_start(bcol[:, :], a["L0_xattn_b"].rearrange("o (k p) -> p (k o)", p=P)).then_inc(text_loaded, 16)
            smalls = ["L0_xattn_W", "L0_ffn_W", "L1_xattn_Wk", "L1_xattn_Wv", "L1_xattn_Wq", "L1_xattn_Wo"]
            for n, name in enumerate(smalls):
                dst = small_stage[n].rearrange("p (k d) -> p k d", k=KC)
                sp.dma_start(dst, w256(a[name])).then_inc(small_loaded[n], 16)
            for n, name in enumerate(("Wcw", "Wcb")):
                sp.dma_start(wc_cols[:, n, :], a[f"L0_xattn_{name}"].rearrange("o (k p) -> p (o k)", p=P)).then_inc(wc_loaded, 16)
            for n, name in enumerate(("bcw", "bcb")):
                sp.dma_start(bc_row[:, n:n + 1], a[f"L0_xattn_{name}"].partition_broadcast(P)).then_inc(wc_loaded, 16)
            sp.dma_start(mask_int, a["mask_BxS2_ik0"].partition_broadcast(P)).then_inc(wc_loaded, 16)
            sp.dma_start(up_rows, a["L0_ffn_up_aux"].rearrange("(c p) u -> p c u", p=P)).then_inc(lora_loaded, 16)
            sp.dma_start(lora_dT[0:100], a["L0_ffn_lora_down"].rearrange("r d -> d r")).then_inc(lora_loaded, 16)
            sp.dma_start(lora_uT[0:4], a["L0_ffn_lora_up"].rearrange("u r -> r u")).then_inc(lora_loaded, 16)
            sp.dma_start(down_aux[0:100], a["L0_ffn_down_aux"]).then_inc(lora_loaded, 16)
            sp.dma_start(rw_rows[0:E], a["L1_ffn_router_w"].rearrange("e (k p) -> e k p", k=KC)).then_inc(lora_loaded, 16)
            for n, name in enumerate(("g_xattn", "g_ffn")):
                sp.dma_start(gains[:, 2 * n:2 * n + 2], a[name].partition_broadcast(P)).then_inc(rows_loaded, 16)
            for dst, name in ((bq, "L1_xattn_bq"), (bk, "L1_xattn_bk")):
                sp.dma_start(dst[:, :], a[name].rearrange("(k p) -> p k", p=P)).then_inc(rows_loaded, 16)
            for dst, name in ((b1_row, "L0_ffn_b"), (bo_row, "L1_xattn_bo"), (bv_row, "L1_xattn_bv"), (rbias, "L1_ffn_bias")):
                sp.dma_start(dst[:, :], a[name].partition_broadcast(P)).then_inc(rows_loaded, 16)
            load_scan(Step(1))
            load_x(Step(0))

            for n in range(len(staged) + RING):
                if n >= RING:
                    sp.wait_ge(split_done, n - RING + 1)
                    e, what = staged[n - RING]
                    if what == "down":
                        src = down_tmp[e % 4]
                        sp.dma_start(down_dram[e, :, 0:TOK], src[0][:, e % 4, :]).then_inc(down_stored[e % 4], 16)
                        sp.dma_start(down_dram[e, :, TOK:2 * TOK], src[1][:, e % 4, :]).then_inc(down_stored[e % 4], 16)
                if n < len(staged):
                    e, what = staged[n]
                    sp.dma_start(stage[n % RING].rearrange("p (k d) -> p k d", k=KC), expert(e, what)).then_inc(stage_loaded[n % RING], 16)
            for n in range(4):
                sp.wait_ge(down_stored[n], 32 * len(range(n, EX, 4)))

            def load_down(st, e):
                if e < 3:
                    if st.const:
                        sp.wait_ge(y_ps, st.at(HID, 2 * (e - 3) + 2))
                else:
                    sp.wait_ge(y_ps, st.at(HID, 2 * (e - 3) + 2))
                sp.dma_start(down[:, e % 3].rearrange("p a b c -> p (a b c)"), down_dram[e]).then_inc(down_loaded[e % 3], 16)

            def rest(ex, load_next_scan=True, load_middle=True):
                if load_next_scan:
                    load_scan(Step(ex.const + 3, ex.r))
                for e in range(3):
                    load_down(ex, e)
                if ex.const:
                    before = Step(ex.const - 1, ex.r)
                    sp.wait_ge(y_used, before.at(HID, HID))
                    sp.dma_start(ov[before.index()], x[:, before.half]).then_inc(stored[before.half], 16)
                for e in range(3, EX):
                    load_down(ex, e)
                    if e == 6 and load_middle:
                        load_x(Step(ex.const + 2, ex.r))

            load_scan(Step(2))
            load_x(Step(1))
            rest(Step(0))
            with sp.Fori(0, STEPS // 2 - 2) as r:
                rest(Step(1, r))
                rest(Step(2, r))
            rest(Step(STEPS - 3), load_next_scan=False)
            rest(Step(STEPS - 2), load_next_scan=False, load_middle=False)
            rest(Step(STEPS - 1), load_next_scan=False, load_middle=False)
            sp.wait_ge(y_used, STEPS * HID)
            sp.dma_start(ov[STEPS - 1], x[:, 1]).then_inc(stored[1], 16)
            for h in range(2):
                sp.wait_ge(stored[h], 16 * B)

        @block.gpsimd
        def _(pool):
            cn = Chain(pool, pool_chain)
            rk = Chain(pool, rank_chain)
            cn.begin(lambda per, k: k)
            cn.link(pool.memset(ident[:, :], 0.0))
            pool.affine_select(out=ident[:, :], in_=ident[:, :], compare_op=ALU.not_equal, fill=1.0,
                               base=0, pattern=[[-1, P]], channel_multiplier=1).then_inc(consts, 1)
            cn.link(pool.memset(wslide[:, :, :], 0.0))
            pool.wait_ge(text_loaded, 64)
            for k in range(KC):
                last = pool.tensor_tensor(wslide[:, k, 31:32], wslide[:, k, 31:32], wcol[:, k:k + 1], ALU.add)
            last.then_inc(consts, 1)
            cn.link(pool.memset(head_mask[:, :, :], 1.0))
            cn.link(pool.affine_select(out=head_mask[:, :, :], in_=head_mask[:, :, :], compare_op=ALU.is_ge, fill=0.0,
                                       base=0, pattern=[[-DH, HC], [0, TXT]], channel_multiplier=1))
            pool.affine_select(out=head_mask[:, :, :], in_=head_mask[:, :, :], compare_op=ALU.is_ge, fill=0.0,
                               base=DH - 1, pattern=[[DH, HC], [0, TXT]], channel_multiplier=-1).then_inc(consts, 1)
            cn.link(pool.memset(pair_mask[:, :, :, :], 1.0))
            cn.link(pool.affine_select(out=pair_mask[:, :, :, :], in_=pair_mask[:, :, :, :], compare_op=ALU.is_ge, fill=0.0,
                                       base=0, pattern=[[P, PCH], [-TXT, HC], [0, DH]], channel_multiplier=1))
            pool.affine_select(out=pair_mask[:, :, :, :], in_=pair_mask[:, :, :, :], compare_op=ALU.is_ge, fill=0.0,
                               base=TXT - 1, pattern=[[-P, PCH], [TXT, HC], [0, DH]], channel_multiplier=-1).then_inc(consts, 1)
            cn.link(pool.memset(head_sel[:, :, :, :], 0.0))
            pool.affine_select(out=head_sel[:, :, :, :], in_=head_sel[:, :, :, :], compare_op=ALU.not_equal, fill=1.0,
                               base=0, pattern=[[-HC, KC], [-1, HC], [0, TXT]], channel_multiplier=1).then_inc(consts, 1)
            cn.link(pool.memset(lower[:, :, :], 1.0))
            pool.affine_select(out=lower[:, :, :], in_=lower[:, :, :], compare_op=ALU.is_ge, fill=0.0,
                               base=-1, pattern=[[1, E], [-1, E]], channel_multiplier=0).then_inc(consts, 1)
            last = pool.tensor_copy(V_hi[:, :, :, P:P + HC], pair_mask[:, :, :, 0].unsqueeze(2).to_broadcast([P, PCH, KC, HC]))
            last.then_inc(consts, 1)
            pool.memset(peak[:, :, :], 0.0).then_inc(consts, 1)
            pool.memset(peakT[:, :], 0.0).then_inc(consts, 1)

            def slot(i, sc, st, ex):
                if ex and i == 0:
                    rk.begin(ex.at)
                    low = lower[:, :, :].unsqueeze(1).to_broadcast([P, NT, E, E])
                    pool.wait_ge(compared, ex.at(1, 1))
                    rk.link(pool.tensor_tensor(rank_b, rank_b, low, ALU.mult))
                    pool.tensor_tensor(rank_a, rank_a, rank_b, ALU.add).then_inc(ranked, 1)
                    rk.end()
                if ex and i % 3 > 0:
                    q = 2 * (i // 3) + i % 3 - 1
                    pool.wait_ge(ghi_done, ex.at(HID, q + 1))
                    if q >= 4 or ex.const:
                        pool.wait_ge(y_ps, ex.at(HID, 2 * (q // 2) - 2))
                    pool.tensor_tensor(hid_lo[:, q % 4], tile3[:, q % 3], hid_hi[:, q % 4], ALU.subtract).then_inc(glo_done, 1)
                kst, k0 = kv_stage(i, sc, st)
                if kst and 0 <= k0 < KVN:
                    for n in range(2 * k0, min(2 * (k0 + 1), 9)):
                        pool.wait_ge(kv_hi, kst.batch_at(9, n + 1))
                        lo, hi, src = kv_parts(n)
                        pool.tensor_tensor(lo, src, hi, ALU.subtract).then_inc(kv_lo, 1)
                if st is None:
                    return
                for m in range(2 * PCH):
                    if i == SCORE_SLOTS[m]:
                        k, rows = m % PCH, ROWS[m % PCH]
                        pool.wait_ge(p_hi_ready, st.at(2 * PCH, m + 1))
                        pool.tensor_tensor(p_lo[0:rows, k], p32[0:rows, m % 2], p_hi[0:rows, k], ALU.subtract).then_inc(p_lo_ready, 1)

            run(pool, None, slot)

        @block.tensor
        def _(pe):
            def product(out_, terms):
                for n, (lh, ll, rh, rl) in enumerate(terms):
                    pe.matmul(out_, lh, rh, start=n == 0, stop=False)
                    pe.matmul(out_, lh, rl, start=False, stop=False)
                    last = pe.matmul(out_, ll, rh, start=False, stop=n == len(terms) - 1)
                return last

            def turn(out_, in_, rows=P):
                return pe.transpose(out_, in_, ident[0:rows, 0:rows])

            pe.wait_ge(consts, 1)
            pe.wait_ge(text_loaded, 64)
            for b in range(B):
                for k in range(KC):
                    last = turn(psG[:, k, b * TXT:(b + 1) * TXT], ctx_rows[0:TXT, b, k * P:(k + 1) * P], TXT)
            last.then_inc(setup_pe, 1)

            def setup(part):
                if part == 0:
                    pe.wait_ge(setup_dve, 2)
                    for c in range(KC):
                        for k in range(KC):
                            last = pe.matmul(psU[:, c, 0:B * TXT], Ws[:, k, c * P:(c + 1) * P], ctxT[:, k, :],
                                             start=k == 0, stop=k == KC - 1)
                    last.then_inc(setup_pe, 1)
                if part == 1:
                    pe.wait_ge(wc_loaded, 80)
                    for n in range(2):
                        for k in range(KC):
                            last = pe.matmul(psG[:, n, 0:B * TXT], wc_cols[:, n, k:k + 1].to_broadcast([P, P]), ctxT[:, k, :],
                                             start=k == 0, stop=k == KC - 1)
                    last.then_inc(setup_pe, 1)
                if part == 2:
                    pe.wait_ge(lora_loaded, 80)
                    pe.wait_ge(feat_ready, 2)
                    for c in range(2):
                        pe.transpose(psY[0:50, 0, c * P:(c + 1) * P], up_rows[:, c, :], ident[:, :])
                    for k in range(KC):
                        turn(psY[:, 1, 128 + k * E:128 + (k + 1) * E], rw_rows[0:E, k, :], E)
                    pe.matmul(psF[0:4, 0, 0:D], lora_dT[0:100, :], down_aux[0:100, :], start=True, stop=True).then_inc(setup_pe, 1)
                if part == 3:
                    pe.wait_ge(setup_dve, 4)
                    pe.matmul(psF[0:50, 0, 0:D], lora_uT[0:4, 0:50], lora1[0:4, :], start=True, stop=True).then_inc(setup_pe, 1)
                if part == 4:
                    pe.wait_ge(setup_dve, 5)
                    pe.wait_ge(small_loaded[1], 16)
                    wnat = small_stage[1].rearrange("p (o d) -> p o d", o=2)
                    for k in range(KC):
                        pe.matmul(psU[:, k, 0:D], lora2[0:50, k * P:(k + 1) * P], up_auxT[0:50, :], start=True, stop=False)
                        for o in range(2):
                            last = pe.matmul(psU[:, k, o * P:(o + 1) * P], wnat[:, o, k * P:(k + 1) * P], ident[:, :],
                                             start=False, stop=o == 1)
                    last.then_inc(setup_pe, 1)

            def gate_up(ex, q):
                e, f = q // 2, q % 2
                if q == 0:
                    pe.wait_ge(lo_ready, ex.at(8, 8))
                if ex.const == 0 and f == 0:
                    pe.wait_ge(split_done, 3 * e + 2)
                if q >= 2 or ex.const:
                    pe.wait_ge(g_done, ex.at(HID, q - 1))
                for ps, wh, wl in ((psG, gate_hi, gate_lo), (psU, up_hi, up_lo)):
                    last = product(ps[:, f], [(wh[:, e, k, f * P:(f + 1) * P], wl[:, e, k, f * P:(f + 1) * P],
                                               eT_hi[:, ex.half, k], eT_lo[:, ex.half, k]) for k in range(KC)])
                last.then_inc(gu_ps, 1)

            def down_half(ex, e, hf):
                if hf == 0:
                    pe.wait_ge(glo_done, ex.at(HID, 2 * e + 2))
                    pe.wait_ge(down_loaded[e % 3], ex.at(6 * 16, 16 * (e // 3 + 1)))
                if 2 * e + hf or ex.const:
                    pe.wait_ge(y_used, ex.at(HID, 2 * e + hf))
                for t in (2 * hf, 2 * hf + 1):
                    last = product(psY[:, t % 2], [(hid_hi[:, (2 * e + f) % 4, t * P:(t + 1) * P],
                                                    hid_lo[:, (2 * e + f) % 4, t * P:(t + 1) * P],
                                                    down[:, e % 3, 0, f], down[:, e % 3, 1, f]) for f in range(2)])
                last.then_inc(y_ps, 1)

            def transpose_x(done):
                for c in range(KC):
                    for t in range(NT):
                        last = turn(psF[:, c, t * P:(t + 1) * P], xn[:, t, c * P:(c + 1) * P])
                    last.then_inc(done, 1)

            def rho_set(st, g, c):
                js = range(min(4, TXT - 4 * g))
                pe.wait_ge(h_ready, st.at(2 * TXT, 8 * g + (c + 1) * len(js)))
                for j in js:
                    n = 8 * g + c * len(js) + j
                    last = pe.matmul(psF[32 * j:32 * j + 32, RHO, :], wslide[:, c, 31 - g:63 - g], tanh_tiles[:, n % HRING],
                                     start=g == 0 and c == 0, stop=c == 1 and 4 * (g + 1) + j >= TXT)
                last.then_inc(rho_part, 1)

            def prelude(j, st):
                if j == NORM1T:
                    pe.wait_ge(xn_scan, st.at(1, 1))
                    if st.const == 1:
                        pe.wait_ge(kv_hi, 9)
                    if st.const >= 2:
                        pe.wait_ge(score_ready, st.at(1, -1))
                    transpose_x(xT_scan)
                    if st.const == 0:
                        setup(0)
                if j == FEAT:
                    if st.const == 0:
                        pe.wait_ge(setup_dve, 1)
                    pe.wait_ge(lo_scan, st.at(2, 2))
                    for c in range(KC):
                        last = product(psF[:, c], [(W0h[:, k, c * P:(c + 1) * P], W0l[:, k, c * P:(c + 1) * P],
                                                    xT_hi[:, k], xT_lo[:, k]) for k in range(KC)])
                    last.then_inc(feat_ps, 1)
                    if st.const == 0:
                        setup(1)

            def scan(i, st):
                for s in range(SETS):
                    if i == tanh_slots(st)[s] + 1:
                        if s == 0:
                            if st.const == 0:
                                pe.wait_ge(consts, 2)
                            else:
                                pe.wait_ge(rhoT_ready, st.at(1, 0))
                        rho_set(st, s // 2, s % 2)

            def slot(i, sc, st, ex):
                if ex:
                    k = i % 3
                    due = halves_at(ex, i)
                    if due:
                        down_half(*due)
                    if k < 2:
                        gate_up(ex, 2 * (i // 3) + k)
                if sc:
                    scan(i, sc)
                for phase, nx in preludes(i, sc):
                    prelude(phase, nx)
                if sc and sc.const == 0 and i in (2, 6, 9):
                    setup((2, 6, 9).index(i) + 2)
                kst, k0 = kv_stage(i, sc, st)
                if kst and 0 <= k0 < KVN:
                    if k0 == 0:
                        pe.wait_ge(ctx8_ready, kst.batch_at(1, 1))
                        if kst.const:
                            pe.wait_ge(sm_sub, kst.at(1, 1))
                        else:
                            pe.wait_ge(feat_ready, 2)
                    flat_hi = ctx8_hi.rearrange("p k h t -> p k (h t)")
                    flat_lo = ctx8_lo.rearrange("p k h t -> p k (h t)")
                    for n in range(2 * k0, min(2 * (k0 + 1), 9)):
                        if n >= 2:
                            pe.wait_ge(kv_hi, kst.batch_at(9, n - 1))
                        if n < 4:
                            c, hf = n // 2, n % 2
                            last = product(psF[:, n % 2, 0:PH], [(Wkh[:, k, c * P:(c + 1) * P], Wkl[:, k, c * P:(c + 1) * P],
                                                                  flat_hi[:, k, hf * PH:(hf + 1) * PH],
                                                                  flat_lo[:, k, hf * PH:(hf + 1) * PH]) for k in range(KC)])
                        else:
                            m = n - 4
                            rows = ROWS[m]
                            last = product(psF[0:rows, n % 2, 0:D], [(flat_hi[:, k, m * P:m * P + rows],
                                                                      flat_lo[:, k, m * P:m * P + rows],
                                                                      Wvh[:, k, :], Wvl[:, k, :]) for k in range(KC)])
                        last.then_inc(kv_ps, 1)
                if st is None:
                    return
                if i == SOFT:
                    pe.wait_ge(rhoT_ready, st.at(1, 1))
                    if st.const < STEPS - 1:
                        pe.wait_ge(feat_ready, st.at(2, 4))
                    else:
                        pe.wait_ge(score_ready, st.at(1, 0))
                    for t in range(NT):
                        last = turn(psF[:, 0, t * P:(t + 1) * P], rhoT[:, t * P:(t + 1) * P])
                    last.then_inc(rho_ps, 1)
                if i == LN2T:
                    if st.half == 0 and st.const:
                        pe.wait_ge(kv_hi, st.batch_at(9, 9))
                    else:
                        pe.wait_ge(sm_sub, st.at(1, 1))
                    pe.wait_ge(xn_ready, st.at(3, 1))
                    transpose_x(xT_ps)
                if i == LIN:
                    pe.wait_ge(lo_ready, st.at(8, 2))
                    for t in range(NT):
                        last = product(psF[:, t // 2, t % 2 * D:t % 2 * D + D],
                                       [(xT_hi[:, k, t * P:(t + 1) * P], xT_lo[:, k, t * P:(t + 1) * P],
                                         W1h[:, k, :], W1l[:, k, :]) for k in range(KC)])
                        if t % 2:
                            last.then_inc(lin_ps, 1)
                if i == LN3T:
                    pe.wait_ge(xn_ready, st.at(3, 2))
                    transpose_x(xT_ps)
                if i == QPROJ:
                    pe.wait_ge(lo_ready, st.at(8, 4))
                    for c in range(KC):
                        product(psF[:, c], [(Wqh[:, k, c * P:(c + 1) * P], Wql[:, k, c * P:(c + 1) * P],
                                             xT_hi[:, k], xT_lo[:, k]) for k in range(KC)]).then_inc(q_ps, 1)
                for u in range(8):
                    if i == PEAK_SLOTS[u]:
                        t, c = u // 2, u % 2
                        if u == 0:
                            pe.wait_ge(q_lo, st.at(2, 2))
                            if st.half == 0:
                                pe.wait_ge(kv_lo, st.batch_at(9, 9))
                        else:
                            pe.wait_ge(peak_used, st.at(8, u))
                        for hf in range(2):
                            last = pe.matmul(psF[:, hf, 0:PH], qT_hi[:, c, t * P:(t + 1) * P],
                                             K_hi[:, c, hf * PH:(hf + 1) * PH], start=True, stop=True)
                        last.then_inc(peak_ps, 1)
                if i == PEAKT:
                    pe.wait_ge(peak_used, st.at(8, 8))
                    for t in range(NT):
                        last = pe.transpose(psF[0:32, 0, t * P:(t + 1) * P], peak[:, t, :], ident[:, :])
                    last.then_inc(peakT_ps, 1)
                for m in range(2 * PCH):
                    if i == SCORE_SLOTS[m]:
                        c, k, rows = m // PCH, m % PCH, ROWS[m % PCH]
                        if m == 0:
                            pe.wait_ge(peakT_ready, st.at(1, 1))
                        elif k == 0:
                            pe.wait_ge(o_ready, st.at(2, 1))
                        elif k >= 2:
                            pe.wait_ge(p_ready, st.at(2 * PCH, m - 1))
                        dst = psF[0:rows, k % 2]
                        cut = slice(k * P, k * P + rows)
                        pe.matmul(dst, K_hi[:, c, cut], qT_hi[:, c], start=True, stop=False)
                        pe.matmul(dst, K_hi[:, c, cut], qT_lo[:, c], start=False, stop=False)
                        pe.matmul(dst, K_lo[:, c, cut], qT_hi[:, c], start=False, stop=False)
                        pe.matmul(dst, head_sel[:, c].rearrange("p h t -> p (h t)")[:, cut], peakT[:, :],
                                  start=False, stop=True).then_inc(sc_ps, 1)
                if i in PV:
                    c = PV.index(i)
                    pe.wait_ge(p_lo_ready, st.at(2 * PCH, PCH * (c + 1)))
                    for t in range(NT):
                        cut, col = slice(t * P, (t + 1) * P), t % 2 * (P + HC)
                        for k in range(PCH):
                            rows = ROWS[k]
                            pe.matmul(psF[:, t // 2, col:col + P + HC], p_hi[0:rows, k, cut], V_hi[0:rows, k, c],
                                      start=k == 0, stop=False)
                            pe.matmul(psF[:, t // 2, col:col + P], p_hi[0:rows, k, cut], V_lo[0:rows, k, c],
                                      start=False, stop=False)
                            last = pe.matmul(psF[:, t // 2, col:col + P + HC], p_lo[0:rows, k, cut], V_hi[0:rows, k, c],
                                             start=False, stop=k == PCH - 1)
                    last.then_inc(pv_ps, 1)
                if i == OT:
                    pe.wait_ge(o_ready, st.at(2, 2))
                    transpose_x(xT_ps)
                if i == WO:
                    pe.wait_ge(lo_ready, st.at(8, 6))
                    for t in range(NT):
                        last = product(psF[:, t // 2, t % 2 * D:t % 2 * D + D],
                                       [(xT_hi[:, k, t * P:(t + 1) * P], xT_lo[:, k, t * P:(t + 1) * P],
                                         Woh[:, k, :], Wol[:, k, :]) for k in range(KC)])
                        if t % 2:
                            last.then_inc(wo_ps, 1)
                if i == LN4T:
                    pe.wait_ge(xn_ready, st.at(3, 3))
                    transpose_x(xT_ps)
                if i == ROUTE:
                    pe.wait_ge(lo_ready, st.at(8, 8))
                    for t in range(NT):
                        last = product(psF[:, 0, t * E:(t + 1) * E],
                                       [(eT_hi[:, st.half, k, t * P:(t + 1) * P], eT_lo[:, st.half, k, t * P:(t + 1) * P],
                                         RWh[:, k, :], RWl[:, k, :]) for k in range(KC)])
                    last.then_inc(logit_ps, 1)

            run(pe, prelude, slot)
            for e, hf in last_halves:
                down_half(Step(STEPS - 1), e, hf)

        @block.scalar
        def _(act):
            def high_half(dst, ready, per, n, st, done, last=0):
                if on_dve(last, st):
                    return
                for c in range(KC):
                    act.wait_ge(ready, st.at(per, 2 * n + c + 1))
                    act.copy(dst[:, c], psF[:, c]).then_inc(done, 1)

            def prelude(j, st):
                if j == NORM1T:
                    high_half(xT_hi, xT_scan, 2, 0, st, hi_scan, last=2)

            def scan(i, st):
                for s in range(SETS):
                    if i == tanh_slots(st)[s]:
                        g, c = s // 2, s % 2
                        if s == 0:
                            act.wait_ge(feat_ready, st.at(2, 2))
                            if st.const:
                                act.wait_ge(rho_part, st.at(SETS, 0))
                            if st.const == 0:
                                act.wait_ge(rows_loaded, 128)
                                act.activation(gains[:, :], gains[:, :], ACT.Tanh).then_inc(setup_act, 1)
                        js = range(min(4, TXT - 4 * g))
                        if s >= 2:
                            act.wait_ge(rho_part, st.at(SETS, s - 1))
                        for j in js:
                            n = 8 * g + c * len(js) + j
                            act.activation(tanh_tiles[:, n % HRING], feat[:, c], ACT.Tanh,
                                           bias=text_now[:, c, 4 * g + j:4 * g + j + 1]).then_inc(h_ready, 1)

            def slot(i, sc, st, ex):
                if sc:
                    scan(i, sc)
                if ex:
                    if i % 3 > 0:
                        q = 2 * (i // 3) + i % 3 - 1
                        act.wait_ge(g_done, ex.at(HID, q + 1))
                        if q >= 4 or ex.const:
                            act.wait_ge(y_ps, ex.at(HID, 2 * (q // 2) - 2))
                        else:
                            act.wait_ge(down_stored[q], 32 * len(range(q, EX, 4)))
                        act.copy(hid_hi[:, q % 4], tile3[:, q % 3]).then_inc(ghi_done, 1)
                    if i % 3 < 2:
                        q = 2 * (i // 3) + i % 3
                        act.wait_ge(gu_ps, ex.at(HID, q + 1))
                        if q >= 3 or ex.const:
                            act.wait_ge(glo_done, ex.at(HID, q - 2))
                        else:
                            act.wait_ge(split_done, len(staged))
                        act.activation(tile3[:, q % 3], psG[:, q % 2], ACT.Tanh, scale=0.5).then_inc(tanh_done, 1)
                for phase, nx in preludes(i, sc):
                    prelude(phase, nx)
                if st is None:
                    return
                if i == SOFT + 1:
                    act.wait_ge(sm_sub, st.at(1, 1))
                    act.activation(sm[:, 2], sm[:, 1], ACT.Exp).then_inc(sm_exp, 1)
                if i == FILM:
                    act.wait_ge(film_in, st.at(1, 1))
                    for n in range(2):
                        last = act.activation(film[:, n], film[:, n], ACT.Tanh, bias=bc_row[:, n:n + 1])
                    last.then_inc(film_ready, 1)
                if i == LN2T:
                    high_half(xT_hi, xT_ps, 8, 0, st, hi_ready)
                if i == LN3T:
                    high_half(xT_hi, xT_ps, 8, 1, st, hi_ready)
                if i == QPROJ and not on_dve(0, st):
                    for c in range(KC):
                        act.wait_ge(q32_ready, st.at(2, c + 1))
                        act.copy(qT_hi[:, c], xn_t[:, c]).then_inc(q_hi, 1)
                if i == PEAKT:
                    act.wait_ge(peakT_ps, st.at(1, 1))
                    act.mul(peakT[0:32, :], psF[0:32, 0], -1.0).then_inc(peakT_ready, 1)
                for m in range(2 * PCH):
                    if i == SCORE_SLOTS[m]:
                        k, rows = m % PCH, ROWS[m % PCH]
                        act.wait_ge(sc_ps, st.at(2 * PCH, m + 1))
                        if m >= 2:
                            act.wait_ge(p_lo_ready, st.at(2 * PCH, m - 1))
                        act.activation(p32[0:rows, m % 2], psF[0:rows, k % 2], ACT.Exp).then_inc(p_ready, 1)
                if i == OT:
                    high_half(xT_hi, xT_ps, 8, 2, st, hi_ready)
                if i == LN4T:
                    if st.const >= 2:
                        act.wait_ge(gu_ps, st.at(HID, -HID))
                    high_half(eT_hi[:, st.half], xT_ps, 8, 3, st, hi_ready)
                if i == ROUTE:
                    act.wait_ge(logit_ps, st.at(1, 1))
                    act.activation(rs[:, 0], psF[:, 0, 0:NT * E].rearrange("p (t e) -> p t e", t=NT), ACT.Tanh,
                                   scale=0.5).then_inc(score_ready, 1)

            run(act, prelude, slot)

        @block.vector
        def _(dve):
            su = Chain(dve, setup_chain)
            su.begin(lambda per, k: k)
            fr = Chain(dve, front_chain)
            rc = Chain(dve, route_chain)
            sn = Chain(dve, scan_chain)
            kv = Chain(dve, kv_chain)

            def split(ch, hi, lo, src):
                ch.link(dve.tensor_copy(hi, src))
                return dve.tensor_tensor(lo, src, hi, ALU.subtract)

            su.link(dve.memset(coef_w[:, :, :], 0.0))
            su.link(dve.memset(coef_b[:, :, :], 0.0))
            su.link(dve.memset(text_mask[:, :, :], -3e38))
            def by_slot(dst, src, op):
                whole = TXT // 4
                d = dst.rearrange("p (j i) -> p i j", j=4)
                op(d[:, 0:whole, :], src[:, 0:4 * whole].rearrange("p (i j) -> p i j", j=4))
                su.link(op(d[:, whole, 0:TXT - 4 * whole], src[:, 4 * whole:TXT]))

            def setup(part):
                if part == 0:
                    dve.wait_ge(small_loaded[0], 16)
                    split(su, W0h[:, :, :], W0l[:, :, :],
                          small_stage[0].rearrange("p (k d) -> p k d", k=KC)).then_inc(setup_dve, 1)
                    dve.wait_ge(setup_pe, 1)
                    su.link(dve.tensor_copy(ctxT, psG[:, :, 0:B * TXT]))
                    split(su, ctxT_hi[:, :, :], ctxT_lo[:, :, :], ctxT).then_inc(setup_dve, 1)
                if part == 1:
                    dve.wait_ge(setup_pe, 2)
                    dve.wait_ge(text_loaded, 64)
                    for c in range(KC):
                        last = dve.tensor_scalar(text_bias[:, c, :], psU[:, c, 0:B * TXT], bcol[:, c:c + 1], None, ALU.add)
                    last.then_inc(setup_dve, 1)
                    dve.wait_ge(setup_dve, 3)
                if part == 2:
                    dve.wait_ge(setup_pe, 3)
                    dve.wait_ge(wc_loaded, 80)
                    for b in range(B):
                        for n, dst in enumerate((coef_w, coef_b)):
                            by_slot(dst[:, b], psG[:, n, b * TXT:(b + 1) * TXT], lambda d, s: dve.tensor_copy(d, s))
                        by_slot(text_mask[:, b], mask_int[:, b],
                                lambda d, s: dve.tensor_scalar(d, s, 1.0, -NEG, ALU.subtract, ALU.mult))
                    for n, (hi, lo) in ((2, (Wkh, Wkl)), (3, (Wvh, Wvl)), (4, (Wqh, Wql)), (5, (Woh, Wol))):
                        dve.wait_ge(small_loaded[n], 16)
                        split(su, hi[:, :, :], lo[:, :, :], small_stage[n].rearrange("p (k d) -> p k d", k=KC))
                if part == 3:
                    dve.wait_ge(setup_pe, 4)
                    dve.tensor_copy(up_auxT[0:50, :], psY[0:50, 0, :])
                    split(su, RWh[:, :, :], RWl[:, :, :], psY[:, 1, 128:128 + KC * E].rearrange("p (k e) -> p k e", k=KC))
                    dve.tensor_copy(lora1[0:4, :], psF[0:4, 0, 0:D]).then_inc(setup_dve, 1)
                if part == 4:
                    dve.wait_ge(setup_pe, 5)
                    dve.tensor_copy(lora2[0:50, :], psF[0:50, 0, 0:D]).then_inc(setup_dve, 1)
                if part == 5:
                    dve.wait_ge(setup_pe, 6)
                    split(su, W1h[:, :, :], W1l[:, :, :], psU[:, :, 0:D]).then_inc(setup_dve, 1)
                    dve.wait_ge(setup_act, 1)
                    dve.wait_ge(rows_loaded, 128)
                    dve.tensor_scalar(b1_row[:, :], b1_row[:, :], gains[:, 2:3], None, ALU.mult)
                    dve.tensor_scalar(bo_row[:, :], bo_row[:, :], gains[:, 1:2], None, ALU.mult)
                    dve.tensor_scalar(bq[:, :], bq[:, :], float(DH) ** -0.5, None, ALU.mult)
                    su.link(dve.memset(combine[:, :, :, E:EX], 0.5))
                    su.link(dve.tensor_scalar(combine[:, :, :, E:EX], combine[:, :, :, E:EX], gains[:, 3:4], None, ALU.mult))
                    dve.wait_ge(consts, 9)

            def split_expert(n):
                e, what = staged[n]
                dve.wait_ge(stage_loaded[n % RING], 16 * (n // RING + 1))
                if what == "down":
                    if e >= 4:
                        dve.wait_ge(down_stored[e % 4], 32 * (e // 4))
                    hi, lo, src = hid_hi[:, e % 4], hid_lo[:, e % 4], stage[n % RING]
                else:
                    hi, lo = (gate_hi, gate_lo) if what == "gate" else (up_hi, up_lo)
                    hi, lo, src = hi[:, e], lo[:, e], stage[n % RING].rearrange("p (k d) -> p k d", k=KC)
                split(su, hi, lo, src).then_inc(split_done, 1)

            def moments(ch, src, norm):
                mean = norm[:, 0]
                for t in range(NT):
                    last = dve.bn_stats(stats[:, t, :], src[:, t, :])
                ch.link(last)
                dve.tensor_tensor(mean, stats[:, :, 1], stats[:, :, 4], ALU.add)
                dve.tensor_tensor(dif[:, :], stats[:, :, 1], stats[:, :, 4], ALU.subtract)
                ch.link(dve.tensor_tensor(veps[:, :], stats[:, :, 2], stats[:, :, 5], ALU.add))
                dve.tensor_scalar(mean, mean, 0.5, None, ALU.mult)
                dve.tensor_tensor(dif[:, :], dif[:, :], dif[:, :], ALU.mult)
                ch.link(dve.tensor_scalar(veps[:, :], veps[:, :], 1.0 / D, EPS, ALU.mult, ALU.add))
                ch.link(dve.scalar_tensor_tensor(out=veps[:, :], in0=dif[:, :], scalar=0.25, in1=veps[:, :],
                                                 op0=ALU.mult, op1=ALU.add))

            def inverse_root(ch, rstd):
                ch.link(dve.tensor_scalar(rstd.bitcast(I32), veps[:, :].bitcast(I32), -0.5, 1597463007.0,
                                          ALU.mult, ALU.add))
                for _ in range(3):
                    ch.link(dve.tensor_tensor(nwt[:, :], rstd, rstd, ALU.mult))
                    ch.link(dve.scalar_tensor_tensor(out=nwt[:, :], in0=nwt[:, :], scalar=-0.5, in1=veps[:, :],
                                                     op0=ALU.mult, op1=ALU.mult))
                    ch.link(dve.scalar_tensor_tensor(out=rstd, in0=nwt[:, :], scalar=1.5, in1=rstd,
                                                     op0=ALU.add, op1=ALU.mult))

            def normalise(ch, src, norm, done):
                inverse_root(ch, norm[:, 1])
                for t in range(NT):
                    last = dve.tensor_scalar(xn[:, t, :], src[:, t, :], norm[:, 0, t:t + 1], norm[:, 1, t:t + 1],
                                             ALU.subtract, ALU.mult)
                last.then_inc(done, 1)

            def low_half(hi, lo, ready, per, n, st, done, turned=xT_ps, last=0):
                for c in range(KC):
                    if on_dve(last, st):
                        dve.wait_ge(turned, st.at(per, 2 * n + c + 1))
                        dve.tensor_copy(hi[:, c], psF[:, c]).then_inc(ready, 1)
                    dve.wait_ge(ready, st.at(per, 2 * n + c + 1))
                    dve.tensor_tensor(lo[:, c], psF[:, c], hi[:, c], ALU.subtract).then_inc(done, 1)

            def compare(v, n, a_, b_):
                mine = v.unsqueeze(3).to_broadcast([P, NT, n, n])
                theirs = v.unsqueeze(2).to_broadcast([P, NT, n, n])
                dve.tensor_tensor(a_, theirs, mine, ALU.is_gt)
                return dve.tensor_tensor(b_, theirs, mine, ALU.is_equal)

            def break_ties(ch, n, b_):
                low = lower[:, 0:n, 0:n].unsqueeze(1).to_broadcast([P, NT, n, n])
                ch.link(dve.tensor_tensor(b_, b_, low, ALU.mult))

            def count(ch, dst, a_, b_):
                ch.link(dve.tensor_tensor(a_, a_, b_, ALU.add))
                ch.link(dve.tensor_reduce(dst, a_, AX, ALU.add))

            def route(part, st):
                score, biased = rs[:, 1], rs[:, 2]
                by = biased.rearrange("p t (g n) -> p t g n", g=NG)
                if part == 0:
                    dve.wait_ge(score_ready, st.at(1, 1))
                    fr.link(dve.tensor_scalar(score, rs[:, 0], 0.5, 0.5, ALU.mult, ALU.add))
                    fr.link(dve.tensor_tensor(biased, score, rbias[:, :].unsqueeze(1).to_broadcast([P, NT, E]), ALU.add))
                    group_scores(by)
                if part == 1:
                    mask_groups(by)
                if part == 2:
                    compare(rs[:, 6], E, rank_a, rank_b).then_inc(compared, 1)

            def group_scores(by):
                q4 = [rs[:, 3, :, 4 * n:4 * n + 4] for n in range(4)]
                dve.tensor_tensor(q4[0], by[:, :, :, 0], by[:, :, :, 1], ALU.max)
                dve.tensor_tensor(q4[1], by[:, :, :, 0], by[:, :, :, 1], ALU.min)
                dve.tensor_tensor(q4[2], by[:, :, :, 2], by[:, :, :, 3], ALU.max)
                fr.link(dve.tensor_tensor(q4[3], by[:, :, :, 2], by[:, :, :, 3], ALU.min))
                top, mid, rest_, second = [rs[:, 4, :, 4 * n:4 * n + 4] for n in range(4)]
                dve.tensor_tensor(top, q4[0], q4[2], ALU.max)
                dve.tensor_tensor(mid, q4[0], q4[2], ALU.min)
                fr.link(dve.tensor_tensor(rest_, q4[1], q4[3], ALU.max))
                fr.link(dve.tensor_tensor(second, mid, rest_, ALU.max))
                fr.link(dve.tensor_tensor(rs[:, 5, :, 0:4], top, second, ALU.add))

            def mask_groups(by):
                gscore, grank, chosen, off = [rs[:, 5, :, 4 * n:4 * n + 4] for n in range(4)]
                a4, b4 = (work[:, n:n + NT * NG * NG].rearrange("p (t e f) -> p t e f", t=NT, e=NG) for n in (0, 1024))
                fr.link(compare(gscore, NG, a4, b4))
                break_ties(fr, NG, b4)
                count(fr, grank, a4, b4)
                fr.link(dve.tensor_scalar(chosen, grank, float(TOPG), None, ALU.is_lt))
                fr.link(dve.tensor_scalar(off, chosen, 1.0, None, ALU.subtract))
                masked = rs[:, 6].rearrange("p t (g n) -> p t g n", g=NG)
                fr.link(dve.tensor_tensor(masked, by, chosen.unsqueeze(3).to_broadcast([P, NT, NG, EPG]), ALU.mult))
                fr.link(dve.tensor_tensor(masked, masked, off.unsqueeze(3).to_broadcast([P, NT, NG, EPG]), ALU.add))

            def choose(st):
                score = rs[:, 1]
                rc.link(dve.tensor_scalar(rs[:, 8], rs[:, 7], float(TOPK), None, ALU.is_lt))
                rc.link(dve.tensor_tensor(rs[:, 9], rs[:, 8], score, ALU.mult))
                total, scale = rs[:, 10, :, 0], rs[:, 10, :, 1]
                rc.link(dve.tensor_reduce(total, rs[:, 9], AX, ALU.add))
                rc.link(dve.tensor_scalar(total, total, 1e-20, None, ALU.add))
                rc.link(dve.reciprocal(scale, total))
                rc.link(dve.tensor_scalar(scale, scale, 0.5 * SCALE, gains[:, 3:4], ALU.mult, ALU.mult))
                rc.link(dve.tensor_tensor(combine[:, st.half, :, 0:E], rs[:, 9],
                                          scale.unsqueeze(2).to_broadcast([P, NT, E]), ALU.mult))
                rc.end()

            def add_y(ex, e, hf):
                dve.wait_ge(y_ps, ex.at(HID, 2 * e + hf + 1))
                if e:
                    dve.wait_ge(y_used, ex.at(HID, 2 * (e - 1) + hf + 1))
                for t in (2 * hf, 2 * hf + 1):
                    xt = x[:, ex.half, t]
                    last = dve.scalar_tensor_tensor(out=xt, in0=psY[:, t % 2], scalar=combine[:, ex.half, t, e:e + 1],
                                                    in1=xt, op0=ALU.mult, op1=ALU.add)
                last.then_inc(y_used, 1)

            def prelude(j, st):
                if j == NORM1:
                    sn.begin(st.at)
                    dve.wait_ge(xscan_loaded, st.at(16, 16))
                    moments(sn, xscan, scan_norm[:, st.half])
                if j == NORM1 + 1:
                    normalise(sn, xscan, scan_norm[:, st.half], xn_scan)
                    if st.const == 0:
                        setup(0)
                if j == NORM1T:
                    low_half(xT_hi, xT_lo, hi_scan, 2, 0, st, lo_scan, turned=xT_scan, last=2)
                    if st.const == 0:
                        setup(1)
                if j == COPY:
                    if st.const:
                        dve.wait_ge(h_ready, st.at(2 * TXT, 0))
                    dve.wait_ge(feat_ps, st.at(1, 1))
                    dve.tensor_copy(feat[:, :, :], psF[:, 0:KC]).then_inc(feat_ready, 1)
                    dve.tensor_copy(text_now[:, :, :], text_bias[:, :, bass.ds(st.batch() * TXT, TXT)]).then_inc(feat_ready, 1)
                    sn.end()

            def scan(i, st):
                if st.const == 0:
                    if i in (0, 3, 6, 10):
                        setup((0, 3, 6, 10).index(i) + 2)
                    for n in range(len(staged) * i // (SLOTS - 3), min(len(staged) * (i + 1) // (SLOTS - 3), len(staged))):
                        split_expert(n)

            def slot(i, sc, st, ex):
                if ex:
                    e, k = i // 3, i % 3
                    due = halves_at(ex, i)
                    if due:
                        add_y(*due)
                    if k < 2:
                        q = 2 * e + k
                        dve.wait_ge(tanh_done, ex.at(HID, q + 1))
                        dve.scalar_tensor_tensor(out=tile3[:, q % 3], in0=tile3[:, q % 3], scalar=1.0, in1=psG[:, k],
                                                 op0=ALU.add, op1=ALU.mult).then_inc(v_done, 1)
                        dve.wait_ge(v_done, ex.at(HID, q + 1))
                        dve.tensor_tensor(tile3[:, q % 3], tile3[:, q % 3], psU[:, k], ALU.mult).then_inc(g_done, 1)
                if st and i == 0:
                    fr.begin(st.at)
                    dve.wait_ge(rho_part, st.at(SETS, SETS))
                    dve.tensor_copy(rhoT, psF[:, RHO]).then_inc(rhoT_ready, 1)
                if ex and i == CHOOSE:
                    rc.begin(ex.at)
                    dve.wait_ge(ranked, ex.at(1, 1))
                    rc.link(dve.tensor_reduce(rs[:, 7], rank_a, AX, ALU.add))
                    choose(ex)
                if sc:
                    scan(i, sc)
                for phase, nx in preludes(i, sc):
                    prelude(phase, nx)
                kst, k0 = kv_stage(i, sc, st)
                if kst and k0 == -2:
                    kv.begin(kst.batch_at)
                    t0 = kst.batch() * TXT
                    for dst, src in ((ctx8_hi, ctxT_hi), (ctx8_lo, ctxT_lo)):
                        for k2 in range(KC):
                            s = src[:, k2, bass.ds(t0, TXT)].unsqueeze(1).to_broadcast([P, HC, TXT])
                            last = dve.tensor_copy(dst[:, k2], s)
                    last.then_inc(ctx8_ready, 1)
                if kst and 0 <= k0 < KVN:
                    for n in range(2 * k0, min(2 * (k0 + 1), 9)):
                        lo, hi, tmp = kv_parts(n)
                        dve.wait_ge(kv_ps, kst.batch_at(9, n + 1))
                        if n >= 2:
                            dve.wait_ge(kv_lo, kst.batch_at(9, n - 1))
                        if n < 4:
                            c, hf = n // 2, n % 2
                            mask = head_mask[:, HC // 2 * hf:HC // 2 * (hf + 1)].rearrange("p h t -> p (h t)")
                            kv.link(dve.scalar_tensor_tensor(out=tmp, in0=psF[:, n % 2, 0:PH], scalar=bk[:, c:c + 1], in1=mask,
                                                             op0=ALU.add, op1=ALU.mult))
                        else:
                            m, rows = n - 4, ROWS[n - 4]
                            kv.link(dve.tensor_tensor(kv32[0:rows, n % 2, 0:D], psF[0:rows, n % 2, 0:D], bv_row[0:rows, :],
                                                      ALU.add))
                            mask = pair_mask[0:rows, m].rearrange("p h d -> p (h d)").unsqueeze(1).to_broadcast([rows, KC, P])
                            kv.link(dve.tensor_tensor(tmp, tmp, mask, ALU.mult))
                        dve.tensor_copy(hi, tmp).then_inc(kv_hi, 1)
                    if k0 == KVN - 1:
                        kv.end()
                if st is None:
                    return
                xs = x[:, st.half]
                b = st.batch()
                if i == SOFT:
                    dve.wait_ge(rho_ps, st.at(1, 1))
                    rho = psF[:, 0].rearrange("p (t j i) -> p t j i", t=NT, j=4)[:, :, :, 0:GRP]
                    mask = text_mask[:, bass.ds(b, 1), :].rearrange("p b (j i) -> p b j i", j=4).to_broadcast([P, NT, 4, GRP])
                    fr.link(dve.tensor_tensor(sm[:, 0].rearrange("p t (j i) -> p t j i", j=4), rho, mask, ALU.add))
                    fr.link(dve.tensor_reduce(smax[:, :], sm[:, 0], AX, ALU.max))
                    dve.tensor_tensor(sm[:, 1], sm[:, 0], smax[:, :].unsqueeze(2).to_broadcast([P, NT, SL]),
                                      ALU.subtract).then_inc(sm_sub, 1)
                if i == SOFT + 1:
                    dve.wait_ge(sm_exp, st.at(1, 1))
                    dve.tensor_reduce(sden[:, :], sm[:, 2], AX, ALU.add)
                    for n, coef in enumerate((coef_w, coef_b)):
                        cf = coef[:, bass.ds(b, 1), :].to_broadcast([P, NT, SL])
                        fr.link(dve.tensor_tensor(sm[:, n], sm[:, 2], cf, ALU.mult))
                        fr.link(dve.tensor_reduce(snum[:, n], sm[:, n], AX, ALU.add))
                    fr.link(dve.reciprocal(sden[:, :], sden[:, :]))
                    dve.tensor_tensor(film[:, :, :], snum[:, :, :], sden[:, :].unsqueeze(1).to_broadcast([P, 2, NT]),
                                      ALU.mult).then_inc(film_in, 1)
                if i == FILM:
                    dve.wait_ge(film_ready, st.at(1, 1))
                    mean, rstd = scan_norm[:, st.half, 0], scan_norm[:, st.half, 1]
                    fr.link(dve.tensor_scalar(film[:, :, :], film[:, :, :], gains[:, 0:1], None, ALU.mult))
                    fr.link(dve.tensor_tensor(film[:, 0], film[:, 0], rstd, ALU.mult))
                    fr.link(dve.tensor_tensor(nwt[:, :], film[:, 0], mean, ALU.mult))
                    dve.tensor_scalar(film[:, 0], film[:, 0], 1.0, None, ALU.add)
                    fr.link(dve.tensor_tensor(film[:, 1], film[:, 1], nwt[:, :], ALU.subtract))
                if i == X1:
                    dve.wait_ge(x_loaded, st.at(16, 16))
                    if st.const >= 2:
                        dve.wait_ge(stored[st.half], st.batch_at(16, 0))
                    for t in range(NT):
                        last = dve.tensor_scalar(xs[:, t], xin[:, t], film[:, 0, t:t + 1], film[:, 1, t:t + 1],
                                                 ALU.mult, ALU.add)
                    fr.link(last)
                for first in (LN2, LN3, LN4):
                    if i == first:
                        moments(fr, xs, norm)
                    if i == first + 1:
                        normalise(fr, xs, norm, xn_ready)
                if i == LN2T:
                    low_half(xT_hi, xT_lo, hi_ready, 8, 0, st, lo_ready)
                    fr.link(dve.tensor_tensor(xs, xs, b1_row[:, :].unsqueeze(1).to_broadcast([P, NT, D]), ALU.add))
                if i == LIN:
                    for j in range(2):
                        dve.wait_ge(lin_ps, st.at(2, j + 1))
                        xj = xs[:, 2 * j:2 * j + 2].rearrange("p t d -> p (t d)")
                        last = dve.scalar_tensor_tensor(out=xj, in0=psF[:, j], scalar=gains[:, 2:3], in1=xj,
                                                        op0=ALU.mult, op1=ALU.add)
                    fr.link(last)
                if i == LN3T:
                    low_half(xT_hi, xT_lo, hi_ready, 8, 1, st, lo_ready)
                if i == QPROJ:
                    for c in range(KC):
                        dve.wait_ge(q_ps, st.at(2, c + 1))
                        dve.tensor_scalar(xn_t[:, c], psF[:, c], float(DH) ** -0.5, bq[:, c:c + 1], ALU.mult,
                                          ALU.add).then_inc(q32_ready, 1)
                    for c in range(KC):
                        if on_dve(0, st):
                            dve.wait_ge(q32_ready, st.at(2, c + 1))
                            dve.tensor_copy(qT_hi[:, c], xn_t[:, c]).then_inc(q_hi, 1)
                        dve.wait_ge(q_hi, st.at(2, c + 1))
                        dve.tensor_tensor(qT_lo[:, c], xn_t[:, c], qT_hi[:, c], ALU.subtract).then_inc(q_lo, 1)
                for u in range(8):
                    if i == PEAK_SLOTS[u]:
                        dve.wait_ge(peak_ps, st.at(8, u + 1))
                        dve.tensor_reduce(peak[:, u // 2, HC * (u % 2):HC * (u % 2 + 1)].rearrange("p (b h) -> p b h", b=2),
                                          psF[:, 0:2, 0:PH].rearrange("p b (h t) -> p b h t", t=TXT), AX,
                                          ALU.max).then_inc(peak_used, 1)
                if i == PEAKT:
                    fr.link(dve.tensor_tensor(xs, xs, bo_row[:, :].unsqueeze(1).to_broadcast([P, NT, D]), ALU.add))
                for m in range(2 * PCH):
                    if i == SCORE_SLOTS[m]:
                        k, rows = m % PCH, ROWS[m % PCH]
                        dve.wait_ge(p_ready, st.at(2 * PCH, m + 1))
                        dve.tensor_copy(p_hi[0:rows, k], p32[0:rows, m % 2]).then_inc(p_hi_ready, 1)
                if i in PV:
                    c = PV.index(i)
                    dve.wait_ge(pv_ps, st.at(2, c + 1))
                    pv = psF[:, 0:2, 0:2 * (P + HC)].rearrange("p b (t n) -> p b t n", t=2)
                    iv = inv[:, c].rearrange("p (b t) h -> p b t h", b=2)
                    fr.link(dve.reciprocal(iv, pv[:, :, :, P:P + HC]))
                    for t in range(NT):
                        last = dve.tensor_tensor(xn_o[:, c, t], pv[:, t // 2, t % 2, 0:P].rearrange("p (h d) -> p h d", h=HC),
                                                 inv[:, c, t].unsqueeze(2).to_broadcast([P, HC, DH]), ALU.mult)
                    last.then_inc(o_ready, 1)
                if i == OT:
                    low_half(xT_hi, xT_lo, hi_ready, 8, 2, st, lo_ready)
                if i == WO:
                    for j in range(2):
                        dve.wait_ge(wo_ps, st.at(2, j + 1))
                        xj = xs[:, 2 * j:2 * j + 2].rearrange("p t d -> p (t d)")
                        last = dve.scalar_tensor_tensor(out=xj, in0=psF[:, j], scalar=gains[:, 1:2], in1=xj,
                                                        op0=ALU.mult, op1=ALU.add)
                    fr.link(last)
                if i == LN4T:
                    low_half(eT_hi[:, st.half], eT_lo[:, st.half], hi_ready, 8, 3, st, lo_ready)
                if i in ROUTE_SLOTS:
                    route(ROUTE_SLOTS.index(i), st)
                if i == SLOTS - 1:
                    fr.end()

            run(dve, prelude, slot)
            for e, hf in last_halves:
                add_y(Step(STEPS - 1), e, hf)


INPUTS = ["x", "ctx_1024", "mask_BxS2_ik0", "g_xattn", "g_ffn",
          "L0_xattn_Ws", "L0_xattn_W", "L0_xattn_w", "L0_xattn_b", "L0_xattn_Wcw", "L0_xattn_bcw",
          "L0_xattn_Wcb", "L0_xattn_bcb", "L0_ffn_W", "L0_ffn_b", "L0_ffn_lora_down", "L0_ffn_lora_up",
          "L0_ffn_down_aux", "L0_ffn_up_aux", "L1_xattn_Wq", "L1_xattn_bq", "L1_xattn_Wk", "L1_xattn_bk",
          "L1_xattn_Wv", "L1_xattn_bv", "L1_xattn_Wo", "L1_xattn_bo", "L1_ffn_router_w", "L1_ffn_bias",
          "L1_ffn_gate_w", "L1_ffn_up_w", "L1_ffn_down_w", "L1_ffn_sh_gate_w", "L1_ffn_sh_up_w",
          "L1_ffn_sh_down_w"]


def kernel(**inputs):
    import concourse.bacc as bacc
    from concourse.bass_utils import run_bass_kernel_spmd

    nc = bacc.Bacc("TRN2", target_bir_lowering=False, num_devices=1)
    arrays, args = {}, {}
    for name in INPUTS:
        v = np.ascontiguousarray(inputs[name])
        arrays[f"in_{name}"] = v
        args[name] = nc.dram_tensor(f"in_{name}", v.shape, mybir.dt.from_np(v.dtype), kind="ExternalInput").ap()
    out = nc.dram_tensor("out_x", (B, S, D), F32, kind="ExternalOutput").ap()
    build(nc, args, out)
    r = run_bass_kernel_spmd(nc, [arrays], core_ids=[0])
    return r.results[0]["out_x"]
```
